# Optimizing a Trainium2 kernel written in Bass

```python
import numpy as np
import jax
import jax.numpy as jnp

def _softmax(x, axis=-1):
    return jax.nn.softmax(x, axis=axis)

def _gelu(x):
    return jax.nn.gelu(x, approximate=True)

def _silu(x):
    return jax.nn.silu(x)

def _sigmoid(x):
    return jax.nn.sigmoid(x)

def _layernorm(x, axis=-1, eps=1e-05):
    m = jnp.mean(x, axis=axis, keepdims=True)
    v = jnp.var(x, axis=axis, keepdims=True)
    return (x - m) / jnp.sqrt(v + eps)

def _scatter_add(tgt, idx, src, axis=0):
    return tgt.at[idx].add(src)

def _segment_sum(src, seg, n):
    return jax.ops.segment_sum(src, seg, n)
kernel_name = 'mk_hybrid_d2_jaxref_r8_c33284'

def setup_inputs(seed: int=0):
    np.random.seed(seed)
    _w = jnp.asarray

    def _L0_attn_a_setup():
        import jax, jax.numpy as jnp
        import numpy as np
        B, T, D = (4, 512, 128)

        def _rmsnorm(y, w):
            return y * jax.lax.rsqrt(jnp.mean(y * y, axis=-1, keepdims=True) + 1e-06) * w
        key = jax.random.key(seed)
        ks = jax.random.split(key, 6)
        std = np.sqrt(2.0 / D).astype(np.float32)
        return {'x': jax.random.normal(ks[0], (B, T, D), dtype=jnp.float32), 'Wr': jax.random.normal(ks[1], (D, D), dtype=jnp.float32) * std, 'Wk': jax.random.normal(ks[2], (D, D), dtype=jnp.float32) * std, 'Wv': jax.random.normal(ks[3], (D, D), dtype=jnp.float32) * std, 'Wo': jax.random.normal(ks[4], (D, D), dtype=jnp.float32) * std, 'decay': jnp.ones((D,), dtype=jnp.float32) * 0.99, 'ln_w': jnp.ones((D,), dtype=jnp.float32)}
    _L0_attn_a_in = _L0_attn_a_setup()

    def _L0_attn_b_setup():
        import jax, jax.numpy as jnp
        import numpy as np
        EMBED_DIM = 128
        NUM_HEADS = 16
        HEAD_DIM = EMBED_DIM // NUM_HEADS
        key = jax.random.key(seed)
        k1, k2, k3 = jax.random.split(key, 3)
        inputs = jax.random.normal(k1, (4, 256, EMBED_DIM), dtype=jnp.float32)
        rotation_params = jax.random.normal(k2, (NUM_HEADS, HEAD_DIM), dtype=jnp.float32)
        entangle_params = jax.random.normal(k3, (NUM_HEADS, HEAD_DIM), dtype=jnp.float32)
        return {'inputs': inputs, 'rotation_params': rotation_params, 'entangle_params': entangle_params}
    _L0_attn_b_in = _L0_attn_b_setup()

    def _L0_ffn_setup():
        import jax, jax.numpy as jnp
        import numpy as np
        B, T, C = (4, 256, 128)
        E, H, K = (8, 256, 2)
        key = jax.random.key(seed)
        ks = jax.random.split(key, 7)
        s_in = 1.0 / np.sqrt(C)
        s_hid = 1.0 / np.sqrt(H)
        return {'x': jax.random.normal(ks[0], (B, T, C), dtype=jnp.float32), 'gate_w': jax.random.uniform(ks[1], (C, E), jnp.float32, -s_in, s_in), 'gate_b': jnp.zeros((E,), jnp.float32), 'w1': jax.random.uniform(ks[2], (E, C, H), jnp.float32, -s_in, s_in), 'b1': jax.random.uniform(ks[3], (E, H), jnp.float32, -s_in, s_in), 'w2': jax.random.uniform(ks[4], (E, H, C), jnp.float32, -s_hid, s_hid), 'b2': jax.random.uniform(ks[5], (E, C), jnp.float32, -s_hid, s_hid)}
    _L0_ffn_in = _L0_ffn_setup()

    def _L1_attn_a_setup():
        import jax, jax.numpy as jnp
        import numpy as np
        N_EMBD = 128
        N_ATTN = 128
        N_HEAD = 16
        N_LAYER = 12
        LAYER_ID = 5
        CTX = 256
        BATCH = 8
        HEAD_SIZE = N_ATTN // N_HEAD
        K_CLAMP = 60.0
        K_EPS = 1e-16

        def _time_decay_init():
            first = 1
            f1 = 3.0 + (LAYER_ID - first) / (N_LAYER - 1 - first) * (1.2 - 3.0)
            f2 = 0.65 + (LAYER_ID - first) / (N_LAYER - 1 - first) * (0.4 - 0.65)
            if LAYER_ID == first:
                f1 += 0.5
            if LAYER_ID == N_LAYER - 2:
                f2 = 0.4
            if LAYER_ID == N_LAYER - 1:
                f2 = 0.37
            h = np.arange(N_HEAD, dtype=np.float64)
            decay_speed = np.power(f2, h / (N_HEAD - 1) * 7) * f1
            return np.log(decay_speed).astype(np.float32)[:, None]
        key = jax.random.key(seed)
        ks = jax.random.split(key, 5)
        x = jax.random.normal(ks[0], (BATCH, CTX, N_EMBD), dtype=jnp.float32)
        tm = np.ones((1, 1, N_EMBD), dtype=np.float32)
        tm[0, 0, :N_EMBD // 2] = 0.0
        scale = 0.02
        return {'x': x, 'time_decay': jnp.asarray(_time_decay_init()), 'time_first': jnp.full((N_HEAD, 1), np.log(0.3), dtype=jnp.float32), 'time_mix': jnp.asarray(tm), 'Wk': jax.random.normal(ks[1], (N_ATTN, N_EMBD), dtype=jnp.float32) * scale, 'Wv': jax.random.normal(ks[2], (N_ATTN, N_EMBD), dtype=jnp.float32) * scale, 'Wr': jax.random.normal(ks[3], (N_ATTN, N_EMBD), dtype=jnp.float32) * scale, 'Wo': jax.random.normal(ks[4], (N_EMBD, N_ATTN), dtype=jnp.float32) * scale}
    _L1_attn_a_in = _L1_attn_a_setup()

    def _L1_attn_b_setup():
        import jax, jax.numpy as jnp
        import numpy as np
        B_SZ, T, D_MODEL, D_STATE, DT_RANK = (4, 256, 128, 16, 64)
        key = jax.random.key(seed)
        ks = jax.random.split(key, 12)
        s = 0.02
        return {'u': jax.random.normal(ks[0], (B_SZ, T, D_MODEL), dtype=jnp.float32), 'A_log': s * jax.random.normal(ks[1], (D_MODEL, D_STATE), dtype=jnp.float32), 'W_xdt': s * jax.random.normal(ks[2], (DT_RANK, D_MODEL), dtype=jnp.float32), 'b_xdt': s * jax.random.normal(ks[3], (DT_RANK,), dtype=jnp.float32), 'W_dt': s * jax.random.normal(ks[4], (D_MODEL, DT_RANK), dtype=jnp.float32), 'b_dt': jax.random.uniform(ks[5], (D_MODEL,), dtype=jnp.float32, minval=-4.0, maxval=-1.0), 'W_B': s * jax.random.normal(ks[6], (D_STATE, D_MODEL), dtype=jnp.float32), 'b_B': s * jax.random.normal(ks[7], (D_STATE,), dtype=jnp.float32), 'W_C': s * jax.random.normal(ks[8], (D_STATE, D_MODEL), dtype=jnp.float32), 'b_C': s * jax.random.normal(ks[9], (D_STATE,), dtype=jnp.float32), 'D': jnp.ones((D_MODEL,), dtype=jnp.float32)}
    _L1_attn_b_in = _L1_attn_b_setup()

    def _L1_ffn_setup():
        import jax, jax.numpy as jnp
        import numpy as np
        TOPK = 8
        BN_EPS = 1e-05
        key = jax.random.key(seed)
        ks = jax.random.split(key, 5)
        b, n, d = (2, 128, 128)
        h, nk, kd = (8, 32, 128)
        ne = nk * nk
        scale = 0.02
        return {'inputs': jax.random.normal(ks[0], (b, n, d), jnp.float32), 'gamma': jnp.ones((d,), jnp.float32), 'beta': jnp.zeros((d,), jnp.float32), 'w_q': jax.random.normal(ks[1], (2 * h * kd, d), jnp.float32) * scale, 'keys': jax.random.normal(ks[2], (h, nk, 2, kd), jnp.float32) * scale, 'key_in': jax.random.normal(ks[3], (ne, d), jnp.float32) * scale, 'key_out': jax.random.normal(ks[4], (ne, d), jnp.float32) * scale}
    _L1_ffn_in = _L1_ffn_setup()
    _d = {'L0_attn_a_x': _L0_attn_a_in['x'], 'L0_attn_a_Wr': _L0_attn_a_in['Wr'], 'L0_attn_a_Wk': _L0_attn_a_in['Wk'], 'L0_attn_a_Wv': _L0_attn_a_in['Wv'], 'L0_attn_a_Wo': _L0_attn_a_in['Wo'], 'L0_attn_a_decay': _L0_attn_a_in['decay'], 'L0_attn_a_ln_w': _L0_attn_a_in['ln_w'], 'L0_attn_b_rotation_params': _L0_attn_b_in['rotation_params'], 'L0_attn_b_entangle_params': _L0_attn_b_in['entangle_params'], 'L0_ffn_gate_w': _L0_ffn_in['gate_w'], 'L0_ffn_gate_b': _L0_ffn_in['gate_b'], 'L0_ffn_w1': _L0_ffn_in['w1'], 'L0_ffn_b1': _L0_ffn_in['b1'], 'L0_ffn_w2': _L0_ffn_in['w2'], 'L0_ffn_b2': _L0_ffn_in['b2'], 'L1_attn_a_time_decay': _L1_attn_a_in['time_decay'], 'L1_attn_a_time_first': _L1_attn_a_in['time_first'], 'L1_attn_a_time_mix': _L1_attn_a_in['time_mix'], 'L1_attn_a_Wk': _L1_attn_a_in['Wk'], 'L1_attn_a_Wv': _L1_attn_a_in['Wv'], 'L1_attn_a_Wr': _L1_attn_a_in['Wr'], 'L1_attn_a_Wo': _L1_attn_a_in['Wo'], 'L1_attn_b_A_log': _L1_attn_b_in['A_log'], 'L1_attn_b_W_xdt': _L1_attn_b_in['W_xdt'], 'L1_attn_b_b_xdt': _L1_attn_b_in['b_xdt'], 'L1_attn_b_W_dt': _L1_attn_b_in['W_dt'], 'L1_attn_b_b_dt': _L1_attn_b_in['b_dt'], 'L1_attn_b_W_B': _L1_attn_b_in['W_B'], 'L1_attn_b_b_B': _L1_attn_b_in['b_B'], 'L1_attn_b_W_C': _L1_attn_b_in['W_C'], 'L1_attn_b_b_C': _L1_attn_b_in['b_C'], 'L1_attn_b_D': _L1_attn_b_in['D'], 'L1_ffn_gamma': _L1_ffn_in['gamma'], 'L1_ffn_beta': _L1_ffn_in['beta'], 'L1_ffn_w_q': _L1_ffn_in['w_q'], 'L1_ffn_keys': _L1_ffn_in['keys'], 'L1_ffn_key_in': _L1_ffn_in['key_in'], 'L1_ffn_key_out': _L1_ffn_in['key_out']}
    _x0 = _d['L0_attn_a_x']
    _d['L0_attn_a_x'] = jax.random.normal(jax.random.fold_in(jax.random.key(seed), 1), (8, 256, 128), dtype=_x0.dtype)
    del _x0
    return _d

def reference(L0_attn_a_x, L0_attn_a_Wr, L0_attn_a_Wk, L0_attn_a_Wv, L0_attn_a_Wo, L0_attn_a_decay, L0_attn_a_ln_w, L0_attn_b_rotation_params, L0_attn_b_entangle_params, L0_ffn_gate_w, L0_ffn_gate_b, L0_ffn_w1, L0_ffn_b1, L0_ffn_w2, L0_ffn_b2, L1_attn_a_time_decay, L1_attn_a_time_first, L1_attn_a_time_mix, L1_attn_a_Wk, L1_attn_a_Wv, L1_attn_a_Wr, L1_attn_a_Wo, L1_attn_b_A_log, L1_attn_b_W_xdt, L1_attn_b_b_xdt, L1_attn_b_W_dt, L1_attn_b_b_dt, L1_attn_b_W_B, L1_attn_b_b_B, L1_attn_b_W_C, L1_attn_b_b_C, L1_attn_b_D, L1_ffn_gamma, L1_ffn_beta, L1_ffn_w_q, L1_ffn_keys, L1_ffn_key_in, L1_ffn_key_out):

    def _L0_attn_a_ref(x, Wr, Wk, Wv, Wo, decay, ln_w):
        import jax, jax.numpy as jnp
        import numpy as np
        B, T, D = (4, 512, 128)

        def _rmsnorm(y, w):
            return y * jax.lax.rsqrt(jnp.mean(y * y, axis=-1, keepdims=True) + 1e-06) * w
        Bsz, Tlen, Dm = x.shape
        r = jax.nn.sigmoid(jnp.einsum('btd,ed->bte', x, Wr))
        k = jnp.einsum('btd,ed->bte', x, Wk)
        v = jnp.einsum('btd,ed->bte', x, Wv)
        dec = jax.nn.sigmoid(decay)
        log_decay = jnp.log(jnp.clip(dec, 1e-07))
        t = jnp.arange(Tlen, dtype=x.dtype)[:, None]
        scale = jnp.exp(t * log_decay[None, :])
        kv = k * v
        cum = jnp.cumsum(kv / jnp.clip(scale, 1e-10)[None], axis=1)
        state = cum * scale[None]
        y = _rmsnorm(r * state, ln_w)
        return jnp.einsum('btd,ed->bte', y, Wo)

    def _L0_attn_b_ref(inputs, rotation_params, entangle_params):
        import jax, jax.numpy as jnp
        import numpy as np
        EMBED_DIM = 128
        NUM_HEADS = 16
        HEAD_DIM = EMBED_DIM // NUM_HEADS
        B, T, _ = inputs.shape
        x = inputs.reshape(B, T, NUM_HEADS, HEAD_DIM).transpose(0, 2, 1, 3)
        q = x * rotation_params[None, :, None, :]
        k = x * entangle_params[None, :, None, :]
        v = x
        scale = 1.0 / np.sqrt(HEAD_DIM).astype(np.float32)
        attn_scores = jnp.einsum('bhid,bhjd->bhij', q, k) * scale
        attn_weights = jax.nn.softmax(attn_scores, axis=-1)
        out = jnp.einsum('bhij,bhjd->bhid', attn_weights, v)
        out = out.transpose(0, 2, 1, 3).reshape(B, T, EMBED_DIM)
        return out

    def _L0_ffn_ref(x, gate_w, gate_b, w1, b1, w2, b2):
        import jax, jax.numpy as jnp
        import numpy as np
        B, T, C = (4, 256, 128)
        E, H, K = (8, 256, 2)
        b, t, c = x.shape
        xf = x.reshape(b * t, c)
        logits = xf @ gate_w + gate_b
        probs = jax.nn.softmax(logits, axis=-1)
        gates, expert_idx = jax.lax.top_k(probs, K)
        h = jax.nn.relu(jnp.einsum('nc,ech->neh', xf, w1) + b1)
        expert_out = jnp.einsum('neh,ehc->nec', h, w2) + b2
        onehot = jax.nn.one_hot(expert_idx, E, dtype=xf.dtype)
        weights = jnp.einsum('nk,nke->ne', gates, onehot)
        out = jnp.einsum('ne,nec->nc', weights, expert_out)
        return out.reshape(b, t, c)

    def _L1_attn_a_ref(x, time_decay, time_first, time_mix, Wk, Wv, Wr, Wo):
        import jax, jax.numpy as jnp
        import numpy as np
        N_EMBD = 128
        N_ATTN = 128
        N_HEAD = 16
        N_LAYER = 12
        LAYER_ID = 5
        CTX = 256
        BATCH = 8
        HEAD_SIZE = N_ATTN // N_HEAD
        K_CLAMP = 60.0
        K_EPS = 1e-16

        def _time_decay_init():
            first = 1
            f1 = 3.0 + (LAYER_ID - first) / (N_LAYER - 1 - first) * (1.2 - 3.0)
            f2 = 0.65 + (LAYER_ID - first) / (N_LAYER - 1 - first) * (0.4 - 0.65)
            if LAYER_ID == first:
                f1 += 0.5
            if LAYER_ID == N_LAYER - 2:
                f2 = 0.4
            if LAYER_ID == N_LAYER - 1:
                f2 = 0.37
            h = np.arange(N_HEAD, dtype=np.float64)
            decay_speed = np.power(f2, h / (N_HEAD - 1) * 7) * f1
            return np.log(decay_speed).astype(np.float32)[:, None]
        B, T, C = x.shape
        H = time_decay.shape[0]
        D = Wk.shape[0] // H
        xs = jnp.pad(x, ((0, 0), (1, 0), (0, 0)))[:, :T]
        xm = x * time_mix + xs * (1.0 - time_mix)
        k = jnp.exp(jnp.minimum(xm @ Wk.T, K_CLAMP))
        v = xm @ Wv.T
        r = xm @ Wr.T
        kv = k * v
        lag = jnp.arange(T)[:, None] - jnp.arange(T)[None, :]
        dec = jnp.exp(time_decay[:, 0])[:, None, None]
        e = jnp.exp(-dec * jnp.maximum(lag - 1, 0).astype(jnp.float32))
        Wm = jnp.where(lag >= 1, e, 0.0)
        Wm = jnp.where(lag == 0, jnp.exp(time_first[:, 0])[:, None, None], Wm)
        kh = k.reshape(B, T, H, D)
        kvh = kv.reshape(B, T, H, D)
        wkv = jnp.einsum('htu,buhd->bthd', Wm, kvh).reshape(B, T, H * D)
        sum_k = jnp.einsum('htu,buhd->bthd', Wm, kh).reshape(B, T, H * D) + K_EPS
        rwkv = jax.nn.sigmoid(r) * wkv / sum_k
        return rwkv @ Wo.T

    def _L1_attn_b_ref(u, A_log, W_xdt, b_xdt, W_dt, b_dt, W_B, b_B, W_C, b_C, D):
        import jax, jax.numpy as jnp
        import numpy as np
        B_SZ, T, D_MODEL, D_STATE, DT_RANK = (4, 256, 128, 16, 64)
        A = -jnp.exp(A_log)
        x_dt = jnp.einsum('btd,rd->btr', u, W_xdt) + b_xdt
        dt = jax.nn.softplus(jnp.einsum('btr,dr->btd', x_dt, W_dt) + b_dt)
        Bt = jnp.einsum('btd,nd->btn', u, W_B) + b_B
        Ct = jnp.einsum('btd,nd->btn', u, W_C) + b_C

        def step(h, inputs):
            u_t, dt_t, B_t, C_t = inputs
            A_bar = jnp.exp(dt_t[:, :, None] * A[None, :, :])
            B_bar = dt_t[:, :, None] * B_t[:, None, :]
            h = A_bar * h + B_bar * u_t[:, :, None]
            y_t = jnp.sum(h * C_t[:, None, :], axis=-1) + D * u_t
            return (h, y_t)
        h0 = jnp.zeros((u.shape[0], A.shape[0], A.shape[1]), dtype=u.dtype)
        xs = (jnp.swapaxes(u, 0, 1), jnp.swapaxes(dt, 0, 1), jnp.swapaxes(Bt, 0, 1), jnp.swapaxes(Ct, 0, 1))
        _, ys = jax.lax.scan(step, h0, xs)
        return jnp.swapaxes(ys, 0, 1)

    def _L1_ffn_ref(inputs, gamma, beta, w_q, keys, key_in, key_out):
        import jax, jax.numpy as jnp
        import numpy as np
        TOPK = 8
        BN_EPS = 1e-05
        b, n, d = inputs.shape
        h, nk, _, kd = keys.shape
        k = TOPK
        x = inputs.reshape(b * n, d)
        mu = jnp.mean(x, axis=0)
        var = jnp.mean(jnp.square(x - mu), axis=0)
        xn = (x - mu) * jax.lax.rsqrt(var + BN_EPS) * gamma + beta
        q = (xn @ w_q.T).reshape(b, n, 2, h, kd).transpose(2, 0, 1, 3, 4)
        sim = jnp.einsum('pbnhd,hkpd->pbnhk', q, keys)
        s, i = jax.lax.top_k(sim, k)
        sx, sy = (s[0], s[1])
        ix, iy = (i[0], i[1])
        all_scores = (sx[..., :, None] + sy[..., None, :]).reshape(b, n, h, k * k)
        all_idx = (ix[..., :, None] * nk + iy[..., None, :]).reshape(b, n, h, k * k)
        scores, pk = jax.lax.top_k(all_scores, k)
        idx = jnp.take_along_axis(all_idx, pk, axis=-1)
        w_down = key_in[idx]
        w_up = key_out[idx]
        o = jnp.einsum('bnd,bnhkd->bnhk', inputs, w_down)
        o = jax.nn.gelu(o, approximate=False) * jax.nn.softmax(scores, axis=-1)
        return jnp.einsum('bnhk,bnhkd->bnd', o, w_up)
    x = L0_attn_a_x
    x = x + _L0_attn_a_ref(_layernorm(x, axis=-1), L0_attn_a_Wr, L0_attn_a_Wk, L0_attn_a_Wv, L0_attn_a_Wo, L0_attn_a_decay, L0_attn_a_ln_w)
    x = x + _L0_ffn_ref(_layernorm(x, axis=-1), L0_ffn_gate_w, L0_ffn_gate_b, L0_ffn_w1, L0_ffn_b1, L0_ffn_w2, L0_ffn_b2)
    x = x + _L0_attn_b_ref(_layernorm(x, axis=-1), L0_attn_b_rotation_params, L0_attn_b_entangle_params)
    x = x + _L0_ffn_ref(_layernorm(x, axis=-1), L0_ffn_gate_w, L0_ffn_gate_b, L0_ffn_w1, L0_ffn_b1, L0_ffn_w2, L0_ffn_b2)
    x = x + _L1_attn_a_ref(_layernorm(x, axis=-1), L1_attn_a_time_decay, L1_attn_a_time_first, L1_attn_a_time_mix, L1_attn_a_Wk, L1_attn_a_Wv, L1_attn_a_Wr, L1_attn_a_Wo)
    x = x + _L1_ffn_ref(_layernorm(x, axis=-1), L1_ffn_gamma, L1_ffn_beta, L1_ffn_w_q, L1_ffn_keys, L1_ffn_key_in, L1_ffn_key_out)
    x = x + _L1_attn_b_ref(_layernorm(x, axis=-1), L1_attn_b_A_log, L1_attn_b_W_xdt, L1_attn_b_b_xdt, L1_attn_b_W_dt, L1_attn_b_b_dt, L1_attn_b_W_B, L1_attn_b_b_B, L1_attn_b_W_C, L1_attn_b_b_C, L1_attn_b_D)
    x = x + _L1_ffn_ref(_layernorm(x, axis=-1), L1_ffn_gamma, L1_ffn_beta, L1_ffn_w_q, L1_ffn_keys, L1_ffn_key_in, L1_ffn_key_out)
    return x

_drawn_inputs = setup_inputs


def setup_inputs(seed=0):
    import zlib

    import numpy as np

    out = dict(_drawn_inputs(seed))
    spreads = {'L0_attn_a_decay': (0.9900000095367432, 0.2),
     'L0_attn_a_ln_w': (1.0, 0.2),
     'L0_ffn_gate_b': (0.0, 0.1),
     'L1_attn_a_time_first': (-1.2039728164672852, 0.6),
     'L1_attn_b_D': (1.0, 0.6),
     'L1_ffn_gamma': (1.0, 0.6),
     'L1_ffn_beta': (0.0, 0.8)}
    factors = {'L0_ffn_b1': 6.533,
     'L0_ffn_b2': 3.462,
     'L1_attn_a_time_decay': 8.0,
     'L1_attn_a_time_mix': 8.0,
     'L1_attn_a_Wk': 8.0,
     'L1_attn_a_Wv': 5.72,
     'L1_attn_a_Wr': 8.0,
     'L1_attn_a_Wo': 5.809,
     'L1_attn_b_A_log': 64.0,
     'L1_attn_b_W_xdt': 43.056,
     'L1_attn_b_b_xdt': 64.0,
     'L1_attn_b_W_dt': 44.24,
     'L1_attn_b_b_dt': 21.473,
     'L1_attn_b_b_B': 64.0,
     'L1_attn_b_b_C': 64.0,
     'L1_ffn_w_q': 8.0,
     'L1_ffn_keys': 8.0,
     'L1_ffn_key_in': 8.0,
     'L1_ffn_key_out': 8.0,
     'L1_attn_b_W_B': 5.938,
     'L1_attn_b_W_C': 6.401}
    for name, (base, spread) in spreads.items():
        noise = np.random.default_rng([zlib.crc32(name.encode()), seed]).standard_normal(out[name].shape)
        drawn = base * np.exp(spread * noise) if base else spread * noise
        out[name] = jnp.asarray(drawn.astype(out[name].dtype))
    for name, factor in factors.items():
        out[name] = (out[name] * factor).astype(out[name].dtype)
    return out
```

```python
import concourse.bass as bass
from concourse import mybir
from contextlib import ExitStack

F32 = mybir.dt.float32
BF16 = mybir.dt.bfloat16
F16 = mybir.dt.float16
U32 = mybir.dt.uint32
ALU = mybir.AluOpType
ACT = mybir.ActivationFunctionType
AX = mybir.AxisListType

B, T, D = 8, 256, 128
N = B * T
NT = N // 128
CW = 512
NC = N // CW
BPC = CW // T
HEADS, HD = 16, 8
E, HID, TOPE = 8, 256, 2
HT = HID // 128
NS, DTR = 16, 64
PH, NK = 8, 32
TOPK = 8
NE = NK * NK
ET = NE // 128
LN_EPS, RMS_EPS, BN_EPS = 1e-5, 1e-6, 1e-5

(V_DECAY, V_LNW, V_ROT, V_ENT, V_MIX, V_BDT, V_D, V_GAMMA, V_BETA, V_BXDT, V_BBC) = range(11)


def chunk(c, w=CW):
    return slice(c * w, (c + 1) * w)


class Norm:

    def __init__(self, k, sem, name):
        self.k = k
        self.centred_ready = sem(name + "_centred_ready")
        self.square_ready = sem(name + "_square_ready")
        self.var_ready = sem(name + "_var_ready")
        self.log_ready = sem(name + "_log_ready")
        self.rstd_ready = sem(name + "_rstd_ready")
        self.z_ready = sem(name + "_z_ready")

    def pe(self, e):
        k = self.k

        def centre(c):
            if c >= 2:
                e.wait_ge(self.z_ready, c - 1)
            e.matmul(k.bank[c % 2][:, :], k.centre[:, :], k.xT[:, chunk(c)],
                     start=True, stop=True).then_inc(self.centred_ready, 1)

        def var(c):
            e.wait_ge(self.square_ready, c + 1)
            if c >= 2:
                e.wait_ge(self.log_ready, c - 1)
            e.matmul(k.bank[2 + c % 2][:, :], k.mean[:, :], k.sq[:, c % 2, :],
                     start=True, stop=True).then_inc(self.var_ready, 1)

        centre(0)
        for c in range(NC):
            if c + 1 < NC:
                centre(c + 1)
            var(c)

    def act(self, e):
        k = self.k
        e.preload_act_table_set("natural_log_exp_and_others")

        def square(c):
            e.wait_ge(self.centred_ready, c + 1)
            if c >= 2:
                e.wait_ge(self.var_ready, c - 1)
            e.activation(k.sq[:, c % 2, :], k.bank[c % 2][:, :], ACT.Square).then_inc(self.square_ready, 1)

        square(0)
        for c in range(NC):
            if c + 1 < NC:
                square(c + 1)
            e.wait_ge(self.var_ready, c + 1)
            e.activation(k.logv[:, c % 2, :], k.bank[2 + c % 2][:, :], ACT.Ln,
                         bias=k.eps_ln[:, 0:1]).then_inc(self.log_ready, 1)
            e.wait_ge(self.log_ready, c + 1)
            if c >= 2:
                e.wait_ge(self.z_ready, c - 1)
            e.activation(k.rstd[:, c % 2, :], k.logv[:, c % 2, :], ACT.Exp,
                         scale=-0.5).then_inc(self.rstd_ready, 1)

    def dve(self, e):
        k = self.k
        for c in range(NC):
            e.wait_ge(self.rstd_ready, c + 1)
            e.tensor_tensor(k.zT[:, chunk(c)], k.bank[c % 2][:, :], k.rstd[:, c % 2, :],
                            ALU.mult).then_inc(self.z_ready, 1)


class Kit:
    pass


def phase(nc, k):
    ctx = ExitStack()
    made = ctx.enter_context
    sems = []

    def clear():
        nc.clear_and_free_semaphores(sems)
        nc.all_engine_barrier()
    ctx.callback(clear)

    def sb(name, shape, dt=F32):
        return made(nc.sbuf_tensor(f"{name}_{k.stage}", shape, dt))

    def sem(name):
        sems.append(nc.alloc_semaphore(name=f"{name}_{k.stage}"))
        return sems[-1]

    return ctx, sb, sem


def setup(nc, k, t):
    ctx, sb, sem = phase(nc, k)
    with ctx:
        xin = sb("xin", [128, NT, D])
        w_nat = sb("w_nat", [128, 8, 128])
        key_in_nat = sb("key_in_nat", [128, ET, D])
        keys_nat = sb("keys_nat", [128, 2, 2, 128])
        wq_nat = sb("wq_nat", [128, 2 * PH, D])
        keysT = sb("keysT", [128, 2, PH * NK])
        small_nat = sb("small_nat", [128, 4, 128])
        by_head = sb("by_head", [128, HEADS])
        load_x = [sem(f"load_x{c}") for c in range(NC)]
        load_w, const, loads = sem("load_w"), sem("const"), sem("load_small")
        packed, evac, mready, ones_done, fold = sem("packed"), sem("evac"), sem("mready"), sem("ones_done"), sem("fold")
        load_q, loads2, loads_big, evac_act = sem("load_q"), sem("loads2"), sem("loads_big"), sem("evac_act")
        load_heads = sem("load_heads")

        groups = []
        for c in range(NC):
            groups.append((load_x[c], 16, [xin[:, 4 * c + j, :] for j in range(4)], k.xT[:, chunk(c)], 128))
        groups.append((load_w, 128, [w_nat[:, j, :] for j in range(4)], k.w0T[:, :, :], 128))
        groups.append((load_w, 128, [w_nat[:, 4 + j, :] for j in range(4)], k.w1T[:, :, :], 128))
        for g in range(2):
            groups.append((load_q, 64, [key_in_nat[:, 4 * g + j, :] for j in range(4)],
                           k.key_inT[:, chunk(g)], 128))
        groups.append((load_q, 64, [keys_nat[:, h, p, :] for p in range(2) for h in range(2)],
                       keysT[:, :, :], 128))
        groups.append((loads, 16 * 15, [small_nat[:, j, :] for j in range(4)], k.smallT[:, :, :], 128))
        NG = len(groups)

        with nc.Block() as block:
            @block.sync
            def _(e):
                xr = t["L0_attn_a_x"].rearrange("b (s p) d -> p (b s) d", p=128)
                for c in range(NC):
                    e.dma_start(xin[:, 4 * c:4 * c + 4, :], xr[:, 4 * c:4 * c + 4, :]).then_inc(load_x[c], 16)
                names = ["L0_attn_a_Wr", "L0_attn_a_Wk", "L0_attn_a_Wv", "L0_attn_a_Wo",
                         "L1_attn_a_Wk", "L1_attn_a_Wv", "L1_attn_a_Wr", "L1_attn_a_Wo"]
                for j, n in enumerate(names):
                    e.dma_start(w_nat[:, j, :], t[n]).then_inc(load_w, 16)
                e.dma_start(k.w1[:, :, :], t["L0_ffn_w1"].rearrange("e c h -> c e h")).then_inc(loads_big, 16)
                e.dma_start(k.w2[:, :, :, :], t["L0_ffn_w2"].rearrange("e (s p) c -> p e s c", p=128)).then_inc(loads_big, 16)
                e.dma_start(k.key_out[:, :, :], t["L1_ffn_key_out"].rearrange("(s p) d -> p s d", p=128)).then_inc(loads_big, 16)
                e.dma_start(k.gate_w[:, :], t["L0_ffn_gate_w"]).then_inc(loads_big, 16)
                e.dma_start(k.gate_b[:, :], t["L0_ffn_gate_b"].rearrange("(a n) -> a n", a=1)).then_inc(loads_big, 16)
                e.dma_start(k.b2[:, :], t["L0_ffn_b2"]).then_inc(loads_big, 16)
                e.dma_start(k.A[:, :], t["L1_attn_b_A_log"]).then_inc(loads_big, 16)
                e.wait_ge(loads_big, 16 * 7)

            @block.scalar
            def _(e):
                e.wait_ge(const, 1)
                rows = {V_DECAY: "L0_attn_a_decay", V_LNW: "L0_attn_a_ln_w", V_ROT: "L0_attn_b_rotation_params",
                        V_ENT: "L0_attn_b_entangle_params", V_BDT: "L1_attn_b_b_dt", V_D: "L1_attn_b_D",
                        V_GAMMA: "L1_ffn_gamma", V_BETA: "L1_ffn_beta"}

                def row(v, lo, n):
                    return small_nat[v:v + 1, 0, lo:lo + n]
                for v, name in rows.items():
                    a = t[name]
                    a = a.rearrange("(a n) -> a n", a=1) if len(a.shape) == 1 else a.rearrange("(o h) d -> o (h d)", o=1)
                    e.dma_start(row(v, 0, D), a).then_inc(loads, 16)
                e.dma_start(row(V_MIX, 0, D), t["L1_attn_a_time_mix"].rearrange("a b n -> (a b) n")).then_inc(loads, 16)
                e.dma_start(row(V_BXDT, 0, DTR), t["L1_attn_b_b_xdt"].rearrange("(a n) -> a n", a=1)).then_inc(loads, 16)
                e.dma_start(row(V_BBC, 0, NS), t["L1_attn_b_b_B"].rearrange("(a n) -> a n", a=1)).then_inc(loads, 16)
                e.dma_start(row(V_BBC, NS, NS), t["L1_attn_b_b_C"].rearrange("(a n) -> a n", a=1)).then_inc(loads, 16)
                for r, name in ((32, "L1_attn_a_time_first"), (64, "L1_attn_a_time_decay")):
                    e.dma_start(by_head[r:r + 1, :], t[name].rearrange("h a -> a h")).then_inc(load_heads, 16)
                e.dma_start(small_nat[32:32 + E * HT, 0, :], t["L0_ffn_b1"].rearrange("e (s p) -> (e s) p", p=128)).then_inc(loads, 16)
                e.dma_start(small_nat[0:DTR, 1, :], t["L1_attn_b_W_xdt"]).then_inc(loads, 16)
                e.dma_start(small_nat[:, 2, 0:DTR], t["L1_attn_b_W_dt"]).then_inc(loads, 16)
                e.dma_start(small_nat[0:NS, 3, :], t["L1_attn_b_W_B"]).then_inc(loads2, 16)
                e.dma_start(small_nat[NS:2 * NS, 3, :], t["L1_attn_b_W_C"]).then_inc(loads2, 16)
                e.dma_start(key_in_nat[:, :, :], t["L1_ffn_key_in"].rearrange("(s p) d -> p s d", p=128)).then_inc(load_q, 16)
                kr = t["L1_ffn_keys"].rearrange("(g h) n p c -> g (h n) p c", g=2)
                for g in range(2):
                    e.dma_start(keys_nat[:, g, :, :], kr[g]).then_inc(load_q, 16)
                e.dma_start(wq_nat[:, :, :], t["L1_ffn_w_q"].rearrange("(s p) d -> p s d", p=128)).then_inc(load_q, 16)
                for g in range(1, NG, 2):
                    e.wait_ge(packed, g + 1)
                    e.activation(groups[g][3], k.bank[g % 8][:, :].rearrange("p (a n) -> p a n", a=4)
                                 if len(groups[g][3].shape) == 3 and groups[g][3].shape[1] == 4 else
                                 (k.bank[g % 8][:, :].rearrange("p (a n) -> p a n", a=2)
                                  if len(groups[g][3].shape) == 3 else k.bank[g % 8][:, :]),
                                 ACT.Copy).then_inc(evac_act, 1)
                e.wait_ge(mready, 1)
                e.activation(k.M[:, :], k.bank[7][:, :], ACT.Copy).then_inc(evac_act, 1)

            @block.gpsimd
            def _(e):
                e.memset(small_nat[:, :, :], 0.0).then_inc(const, 1)
                e.memset(k.ident[:, :], 0.0).then_inc(ones_done, 1)
                e.memset(k.mean[:, :], 1.0 / D).then_inc(ones_done, 1)
                e.memset(k.eps_ln[:, :], LN_EPS).then_inc(ones_done, 1)
                e.memset(k.eps_rms[:, :], RMS_EPS).then_inc(ones_done, 1)
                e.memset(k.ones_row[:, :], 1.0).then_inc(ones_done, 1)
                e.wait_ge(ones_done, 5)
                e.affine_select(out=k.ident[:, :], in_=k.ident[:, :], compare_op=ALU.not_equal, fill=1.0,
                                base=0, pattern=[[-1, 128]], channel_multiplier=1).then_inc(const, 1)
                e.wait_ge(const, 2)
                e.tensor_tensor(k.centre[:, :], k.ident[:, :], k.mean[:, :], ALU.subtract).then_inc(const, 1)
                e.iota(k.iota_i[:, :], pattern=[[1, 128]], base=0, channel_multiplier=0).then_inc(const, 1)
                e.wait_ge(const, 4)
                e.tensor_copy(k.iota_f[:, :], k.iota_i[:, :]).then_inc(const, 1)
                e.wait_ge(const, 5)
                e.wait_ge(load_heads, 32)
                for r in (32, 64):
                    e.tensor_copy(small_nat[r:r + 1, 3, :].rearrange("o (h d) -> o h d", h=HEADS),
                                  along(by_head[r:r + 1, :], HD)).then_inc(const, 1)
                e.wait_ge(const, 7)

            @block.tensor
            def _(e):
                e.wait_ge(const, 2)
                for g, (s, v, srcs, dst, w) in enumerate(groups):
                    e.wait_ge(s, v)
                    if s is loads:
                        e.wait_ge(loads2, 32)
                        e.wait_ge(const, 7)
                    if g >= 8:
                        if g % 2:
                            e.wait_ge(evac_act, (g - 8) // 2 + 1)
                        else:
                            e.wait_ge(evac, (g - 8) // 2 + 1)
                    for j, src in enumerate(srcs):
                        mm = e.transpose(k.bank[g % 8][:, j * 128:(j + 1) * 128], src, k.ident[:, :])
                    mm.then_inc(packed, 1)
                e.wait_ge(evac, 5)
                e.wait_ge(evac_act, 4)
                for p in range(2):
                    for h in range(PH):
                        s = p * PH + h
                        mm = e.matmul(k.bank[7][:, s * NK:(s + 1) * NK], wq_nat[:, s, :],
                                      keysT[:, p, h * NK:(h + 1) * NK], start=True, stop=True)
                mm.then_inc(mready, 1)

            @block.vector
            def _(e):
                for g in range(0, NG, 2):
                    e.wait_ge(packed, g + 1)
                    dst = groups[g][3]
                    src = k.bank[g % 8][:, :]
                    if len(dst.shape) == 3:
                        src = src.rearrange("p (a n) -> p a n", a=dst.shape[1])
                    e.tensor_copy(dst, src).then_inc(evac, 1)
                e.wait_ge(evac_act, 5)
                e.wait_ge(evac, 5)
                e.tensor_scalar(k.w0T[:, 3, :], k.w0T[:, 3, :], k.vec(V_LNW), None, ALU.mult).then_inc(fold, 1)
                e.tensor_scalar(k.qscale[:, :], k.vec(V_ROT), k.vec(V_ENT), float(1.0 / HD ** 0.5),
                                ALU.mult, ALU.mult).then_inc(fold, 1)
                e.tensor_scalar(k.one_minus_mix[:, :], k.vec(V_MIX), -1.0, 1.0, ALU.mult, ALU.add).then_inc(fold, 1)


def store(nc, k, out):
    ctx, sb, sem = phase(nc, k)
    with ctx:
        xout = sb("xout", [128, NT, D])
        turned, copied, stored = sem("turned"), sem("copied"), sem("stored")
        outr = out.rearrange("b (s p) d -> p (b s) d", p=128)
        with nc.Block() as block:
            @block.tensor
            def _(e):
                for c in range(NC):
                    for j in range(4):
                        mm = e.transpose(k.bank[c][:, j * 128:(j + 1) * 128],
                                         k.xT[:, (4 * c + j) * 128:(4 * c + j + 1) * 128], k.ident[:, :])
                    mm.then_inc(turned, 1)

            @block.vector
            def _(e):
                for c in range(NC):
                    e.wait_ge(turned, c + 1)
                    e.tensor_copy(xout[:, 4 * c:4 * c + 4, :],
                                  k.bank[c][:, :].rearrange("p (a n) -> p a n", a=4)).then_inc(copied, 1)

            @block.sync
            def _(e):
                for c in range(NC):
                    e.wait_ge(copied, c + 1)
                    e.dma_start(outr[:, 4 * c:4 * c + 4, :], xout[:, 4 * c:4 * c + 4, :]).then_inc(stored, 16)
                e.wait_ge(stored, 16 * NC)


def decay_attention(nc, k):
    ctx, sb, sem = phase(nc, k)
    with ctx:
        ln = Norm(k, sem, "a0")
        dec = sb("dec", [128, 1])
        keep = sb("keep", [128, CW])
        scale = sb("scale", [128, T])
        first = sb("first", [128, T])
        clipm = sb("clipm", [128, CW])
        ksb, sr, y, ysq = sb("ksb", [128, N]), sb("sr", [128, N]), sb("y", [128, N]), sb("ysq", [128, N])
        kv = sb("kv", [128, 2, CW])
        kvm = sb("kvm", [128, 2, CW])
        state = sb("state", [128, 2, CW])
        rst2, yn = sb("rst2", [128, 2, CW]), sb("yn", [128, 2, CW])
        dec_ready, prep, proj, k_ready, r_ready = sem("dec_ready"), sem("prep"), sem("proj"), sem("k_ready"), sem("r_ready")
        kv_ready, step, y_ready, ysq_ready, ms_ready = sem("kv_ready"), sem("step"), sem("y_ready"), sem("ysq_ready"), sem("ms_ready")
        lg_ready, rs_ready, yn_ready, o_ready, x_done = sem("lg_ready"), sem("rs_ready"), sem("yn_ready"), sem("o_ready"), sem("x_done")
        with nc.Block() as block:
            @block.tensor
            def _(e):
                ln.pe(e)
                for c in range(NC):
                    e.wait_ge(ln.z_ready, c + 1)
                    if c >= 1:
                        e.wait_ge(r_ready, c)
                        e.wait_ge(kv_ready, c)
                    for j in (1, 2, 0):
                        e.matmul(k.bank[4 + j][:, :], k.w0T[:, j, :], k.zT[:, chunk(c)],
                                 start=True, stop=True).then_inc(proj, 1)
                for c in range(NC):
                    e.wait_ge(ysq_ready, c + 1)
                    if c >= 2:
                        e.wait_ge(lg_ready, c - 1)
                    e.matmul(k.bank[2 + c % 2][:, :], k.mean[:, :], ysq[:, chunk(c)],
                             start=True, stop=True).then_inc(ms_ready, 1)
                for c in range(NC):
                    e.wait_ge(yn_ready, c + 1)
                    if c >= 2:
                        e.wait_ge(x_done, c - 1)
                    e.matmul(k.bank[c % 2][:, :], k.w0T[:, 3, :], yn[:, c % 2, :],
                             start=True, stop=True).then_inc(o_ready, 1)

            @block.scalar
            def _(e):
                ln.act(e)
                e.activation(dec[:, :], k.vec(V_DECAY), ACT.Sigmoid).then_inc(dec_ready, 1)
                for c in range(NC):
                    e.wait_ge(proj, 3 * c + 1)
                    e.activation(ksb[:, chunk(c)], k.bank[5][:, :], ACT.Copy).then_inc(k_ready, 1)
                    e.wait_ge(proj, 3 * c + 3)
                    e.activation(sr[:, chunk(c)], k.bank[4][:, :], ACT.Sigmoid).then_inc(r_ready, 1)
                for c in range(NC):
                    e.wait_ge(y_ready, c + 1)
                    e.activation(ysq[:, chunk(c)], y[:, chunk(c)], ACT.Square).then_inc(ysq_ready, 1)
                e.preload_act_table_set("natural_log_exp_and_others")
                for c in range(NC):
                    e.wait_ge(ms_ready, c + 1)
                    e.activation(k.logv[:, c % 2, :], k.bank[2 + c % 2][:, :], ACT.Ln,
                                 bias=k.eps_rms[:, 0:1]).then_inc(lg_ready, 1)
                    e.wait_ge(lg_ready, c + 1)
                    if c >= 2:
                        e.wait_ge(yn_ready, c - 1)
                    e.activation(rst2[:, c % 2, :], k.logv[:, c % 2, :], ACT.Exp, scale=-0.5).then_inc(rs_ready, 1)

            @block.vector
            def _(e):
                ln.dve(e)
                e.memset(first[:, :], 0.0).then_inc(prep, 1)
                e.wait_ge(prep, 1)
                e.memset(first[:, 0:1], 1.0).then_inc(prep, 1)
                e.wait_ge(dec_ready, 1)
                e.memset(keep[:, :], 1.0).then_inc(prep, 1)
                e.tensor_scalar(dec[:, :], dec[:, :], 1e-7, None, ALU.max).then_inc(prep, 1)
                e.wait_ge(prep, 4)
                e.tensor_scalar(keep[:, :], keep[:, :], dec[:, 0:1], None, ALU.mult).then_inc(prep, 1)
                e.wait_ge(prep, 5)
                e.tensor_tensor_scan(scale[:, :], keep[:, 0:T], first[:, :], 0.0, ALU.mult, ALU.add).then_inc(prep, 1)
                e.wait_ge(prep, 6)
                for b in range(BPC):
                    e.tensor_scalar(clipm[:, b * T:(b + 1) * T], scale[:, :], 1e10, 1.0, ALU.mult, ALU.min).then_inc(prep, 1)
                    e.memset(keep[:, b * T:b * T + 1], 0.0).then_inc(prep, 1)
                e.wait_ge(prep, 6 + 2 * BPC)
                for c in range(NC):
                    e.wait_ge(proj, 3 * c + 2)
                    e.wait_ge(k_ready, c + 1)
                    e.tensor_tensor(kv[:, c % 2, :], k.bank[6][:, :], ksb[:, chunk(c)], ALU.mult).then_inc(kv_ready, 1)
                    e.wait_ge(kv_ready, c + 1)
                    e.tensor_tensor(kvm[:, c % 2, :], kv[:, c % 2, :], clipm[:, :], ALU.mult).then_inc(step, 1)
                    e.wait_ge(step, 2 * c + 1)
                    e.tensor_tensor_scan(state[:, c % 2, :], keep[:, :], kvm[:, c % 2, :], 0.0,
                                         ALU.mult, ALU.add).then_inc(step, 1)
                    e.wait_ge(step, 2 * c + 2)
                    e.wait_ge(r_ready, c + 1)
                    e.tensor_tensor(y[:, chunk(c)], state[:, c % 2, :], sr[:, chunk(c)], ALU.mult).then_inc(y_ready, 1)
                for c in range(NC + 1):
                    if c < NC:
                        e.wait_ge(rs_ready, c + 1)
                        if c >= 2:
                            e.wait_ge(o_ready, c - 1)
                        e.tensor_tensor(yn[:, c % 2, :], y[:, chunk(c)], rst2[:, c % 2, :], ALU.mult).then_inc(yn_ready, 1)
                    if c >= 1:
                        e.wait_ge(o_ready, c)
                        e.tensor_tensor(k.xT[:, chunk(c - 1)], k.bank[(c - 1) % 2][:, :], k.xT[:, chunk(c - 1)],
                                        ALU.add).then_inc(x_done, 1)


def along(a, n):
    return a.unsqueeze(len(a.shape)).broadcast_to([*a.shape, n])


def across(a, n):
    return a.unsqueeze(len(a.shape) - 1).broadcast_to([*a.shape[:-1], n, a.shape[-1]])


def mixture(nc, k):
    ctx, sb, sem = phase(nc, k)
    with ctx:
        ln = Norm(k, sem, "moe")
        top, shifted, ex = sb("top", [128, NT]), sb("shifted", [128, NT, E]), sb("ex", [128, NT, E])
        total, best = sb("total", [128, NT]), sb("best", [128, NT, 8])
        best_i, best_f = sb("best_i", [128, NT, 8], U32), sb("best_f", [128, NT, 8])
        picked, picked2 = sb("picked", [128, NT, E]), sb("picked2", [128, NT, E])
        wts, wT, wch = sb("wts", [128, NT, E]), sb("wT", [E, N]), sb("wch", [128, 4, E])
        base = sb("base", [128, NT, D])
        h = sb("h", [128, 4, HT, CW])
        acc = sb("acc", [128, 4, D])
        logits, g, ex_ready, wts_ready = sem("logits"), sem("gate_step"), sem("ex_ready"), sem("wts_ready")
        wT_turned, wT_ready, base_mm, base_ready = sem("wT_turned"), sem("wT_ready"), sem("base_mm"), sem("base_ready")
        hidden, h_ready, y_ready, gated = sem("hidden"), sem("h_ready"), sem("y_ready"), sem("gated")
        turned, x_done, w_copied = sem("turned"), sem("x_done"), sem("w_copied")
        JT = E * HT

        with nc.Block() as block:
            @block.tensor
            def _(e):
                ln.pe(e)
                e.wait_ge(ln.z_ready, NC)
                for t in range(NT):
                    e.matmul(k.bank[4][:, t * E:(t + 1) * E], k.zT[:, t * 128:(t + 1) * 128], k.gate_w[:, :],
                             start=True, stop=False)
                    mm = e.matmul(k.bank[4][:, t * E:(t + 1) * E], k.ones_row[:, :], k.gate_b[:, :],
                                  start=False, stop=True)
                mm.then_inc(logits, 1)

                def first(c, x, head):
                    for s in range(HT):
                        j = x * HT + s
                        if not (head and j < 4):
                            e.wait_ge(h_ready, c * JT + (j - 3))
                        e.matmul(k.bank[j % 4][:, :], k.w1[:, x, s * 128:(s + 1) * 128],
                                 k.zT[:, bass.ds(c * CW, CW)], start=True, stop=True).then_inc(hidden, 1)

                def second(c, x, head):
                    e.wait_ge(h_ready, c * JT + (x + 1) * HT)
                    if not (head and x < 2):
                        e.wait_ge(gated, c * E + (x - 1))
                    for q in range(4):
                        for s in range(HT):
                            mm = e.matmul(k.bank[4 + x % 2][:, q * 128:(q + 1) * 128],
                                          h[:, x % 4, s, q * 128:(q + 1) * 128], k.w2[:, x, s, :],
                                          start=(s == 0), stop=(s == HT - 1))
                    mm.then_inc(y_ready, 1)

                e.wait_ge(wts_ready, 1)
                for c in range(NC):
                    for q in range(4):
                        mm = e.transpose(k.bank[4 + c][0:E, q * 128:(q + 1) * 128], wts[:, 4 * c + q, :], k.ident[:, :])
                    mm.then_inc(wT_turned, 1)
                for c in range(NC):
                    e.wait_ge(wT_ready, c + 1)
                    for q in range(4):
                        mm = e.matmul(k.bank[4 + c][:, q * 128:(q + 1) * 128],
                                      wT[:, (4 * c + q) * 128:(4 * c + q + 1) * 128], k.b2[:, :], start=True, stop=True)
                    mm.then_inc(base_mm, 1)
                e.wait_ge(base_ready, NC)

                def run(c, head):
                    first(c, 0, head)
                    for x in range(E):
                        if x + 1 < E:
                            first(c, x + 1, head)
                        second(c, x, head)
                    e.wait_ge(gated, c * E + E)
                    if not head:
                        e.wait_ge(x_done, c)
                    for q in range(4):
                        mm = e.transpose(k.bank[6][:, q * 128:(q + 1) * 128], acc[:, q, :], k.ident[:, :])
                    mm.then_inc(turned, 1)
                run(0, True)
                with e.Fori(1, NC) as c:
                    run(c, False)

            @block.scalar
            def _(e):
                ln.act(e)
                e.wait_ge(g, 2)
                e.activation(ex[:, :, :], shifted[:, :, :], ACT.Exp).then_inc(ex_ready, 1)
                for c in range(NC):
                    e.wait_ge(wT_turned, c + 1)
                    e.activation(wT[:, chunk(c)], k.bank[4 + c][0:E, :], ACT.Copy).then_inc(wT_ready, 1)
                for c in range(NC):
                    e.wait_ge(base_mm, c + 1)
                    e.activation(base[:, 4 * c:4 * c + 4, :], k.bank[4 + c][:, :].rearrange("p (a n) -> p a n", a=4),
                                 ACT.Copy).then_inc(base_ready, 1)

                def run(c, head):
                    for j in range(JT):
                        x, s = j // HT, j % HT
                        e.wait_ge(hidden, c * JT + j + 1)
                        if not (head and x < 4):
                            e.wait_ge(y_ready, c * E + (x - 3))
                        e.activation(h[:, x % 4, s, :], k.bank[j % 4][:, :], ACT.Relu,
                                     bias=k.b1[:, j:j + 1]).then_inc(h_ready, 1)
                run(0, True)
                with e.Fori(1, NC) as c:
                    run(c, False)

            @block.vector
            def _(e):
                ln.dve(e)
                e.wait_ge(logits, 1)
                lg = k.bank[4][:, 0:NT * E].rearrange("p (t x) -> p t x", x=E)
                e.tensor_reduce(top[:, :], lg, AX.X, ALU.max).then_inc(g, 1)
                e.wait_ge(g, 1)
                e.tensor_tensor(shifted[:, :, :], lg, along(top[:, :], E), ALU.subtract).then_inc(g, 1)
                e.wait_ge(ex_ready, 1)
                e.tensor_reduce(total[:, :], ex[:, :, :], AX.X, ALU.add).then_inc(g, 1)
                e.wait_ge(g, 3)
                e.reciprocal(total[:, :], total[:, :]).then_inc(g, 1)
                e.wait_ge(g, 4)
                e.tensor_tensor(ex[:, :, :], ex[:, :, :], along(total[:, :], E), ALU.mult).then_inc(g, 1)
                e.wait_ge(g, 5)
                for t in range(NT):
                    e.max(best[:, t, :], ex[:, t, :]).then_inc(g, 1)
                e.wait_ge(g, 5 + NT)
                for t in range(NT):
                    e.max_index(best_i[:, t, :], best[:, t, :], ex[:, t, :]).then_inc(g, 1)
                n = 5 + 2 * NT
                e.wait_ge(g, n)
                e.tensor_copy(best_f[:, :, :], best_i[:, :, :]).then_inc(g, 1)
                e.wait_ge(g, n + 1)
                number = k.iota_f[:, 0:E].unsqueeze(1).broadcast_to([128, NT, E])
                for r, out_r in ((0, picked), (1, picked2)):
                    e.tensor_tensor(out_r[:, :, :], number, along(best_f[:, :, r], E), ALU.is_equal).then_inc(g, 1)
                e.wait_ge(g, n + 3)
                e.tensor_tensor(picked[:, :, :], picked[:, :, :], picked2[:, :, :], ALU.add).then_inc(g, 1)
                e.wait_ge(g, n + 4)
                e.tensor_tensor(wts[:, :, :], picked[:, :, :], ex[:, :, :], ALU.mult).then_inc(wts_ready, 1)
                e.wait_ge(wts_ready, 1)
                e.wait_ge(base_ready, NC)

                def run(c, head):
                    if not head:
                        e.wait_ge(gated, c * E)
                        e.wait_ge(turned, c)
                    e.tensor_copy(wch[:, :, :], wts[:, bass.ds(c * 4, 4), :]).then_inc(w_copied, 1)
                    e.wait_ge(w_copied, c + 1)
                    for x in range(E):
                        e.wait_ge(y_ready, c * E + x + 1)
                        if x:
                            e.wait_ge(gated, c * E + x)
                        for q in range(4):
                            prior = base[:, bass.ds(c * 4 + q, 1), :].rearrange("p a n -> p (a n)") if x == 0 else acc[:, q, :]
                            i = e.scalar_tensor_tensor(out=acc[:, q, :], in0=k.bank[4 + x % 2][:, q * 128:(q + 1) * 128],
                                                       scalar=wch[:, q, x:x + 1], in1=prior, op0=ALU.mult, op1=ALU.add)
                        i.then_inc(gated, 1)
                    e.wait_ge(turned, c + 1)
                    e.tensor_tensor(k.xT[:, bass.ds(c * CW, CW)], k.bank[6][:, :], k.xT[:, bass.ds(c * CW, CW)],
                                    ALU.add).then_inc(x_done, 1)
                run(0, True)
                with e.Fori(1, NC) as c:
                    run(c, False)



Q_PARTS = (0, 0, 0, 1, 1, 2)
K_PARTS = (0, 1, 2, 0, 1, 0)
QK_ROWS = len(Q_PARTS) * HD
HC = HD + 1
HR = 8 * HC
MAX_ROWS = 3


def per_batch(e, step):
    step(0, 0)
    step(1, 1)
    with e.Fori(1, B // 2 - 1) as i:
        step(2 * i, 0)
        step(2 * i + 1, 1)
    step(B - 2, 0)
    step(B - 1, 1)


def head_attention(nc, k):
    ctx, sb, sem = phase(nc, k)
    with ctx:
        ln = Norm(k, sem, "hd")
        q = sb("q", [128, 2, CW])
        rest = sb("rest", [128, 2, CW])
        parts = sb("parts", [128, 2, 2, 3, CW], BF16)
        kept = nc.dram_tensor("attention_parts", (2, 3, 128, N), BF16, kind="Internal").ap()
        slots = sb("slots", [64, 2, 2, HEADS, T], BF16)
        V = sb("V", [128, NT, HEADS, HD + 1])
        m = sb("m", [128, 2, HEADS])
        negm, nrest = sb("negm", [HEADS, T]), sb("nrest", [HEADS, T])
        mparts = sb("mparts", [HEADS, 2, MAX_ROWS, T], BF16)
        P = sb("P", [128, 2, 2, 2, T])
        Vh = sb("Vh", [128, 2, 2, 2, 8 * (HR + HC)])
        both = sb("both", [HR, 2, T])
        recip, o = sb("recip", [128, 2 * HEADS]), sb("o", [128, 2, D])
        q_ready, hi_ready, rest_ready, mid_ready, lo_ready = sem("q_ready"), sem("hi_ready"), sem("rest_ready"), sem("mid_ready"), sem("lo_ready")
        parts_kept = [sem("parts_kept0"), sem("parts_kept1")]
        slot_loaded = [sem("slot_loaded0"), sem("slot_loaded1")]
        max_loaded = [sem("max_loaded0"), sem("max_loaded1")]
        v_turned, v_ready, ones_set = sem("v_turned"), sem("v_ready"), sem("ones_set")
        s1_ready, max_ready, mt_ready, mstep, mparts_ready = sem("s1_ready"), sem("max_ready"), sem("mt_ready"), sem("mstep"), sem("mparts_ready")
        s2_ready, p_ready, pv_group, pv_ready = sem("s2_ready"), sem("p_ready"), sem("pv_group"), sem("pv_ready")
        vh_zero, vh_ready, both_ready, both_turned = sem("vh_zero"), sem("vh_ready"), sem("both_ready"), sem("both_turned")
        recip_ready, o_ready, o_turned, x_done = sem("recip_ready"), sem("o_ready"), sem("o_turned"), sem("x_done")
        G1, G2 = 16, 8
        LOADS = 2 * len(Q_PARTS)

        def wait(e, s, v):
            if not (isinstance(v, int) and v <= 0):
                e.wait_ge(s, v)

        with nc.Block() as block:
            @block.sync
            def _(e):
                for c in range(NC):
                    e.wait_ge(lo_ready, 2 * (c + 1))
                    for w in range(2):
                        e.dma_start(kept[w, :, :, chunk(c)].rearrange("s p n -> p s n"),
                                    parts[:, c % 2, w, :, :]).then_inc(parts_kept[c % 2], 16)

                def load(b, u):
                    for i in range(len(Q_PARTS)):
                        for w, part in ((0, Q_PARTS[i]), (1, K_PARTS[i])):
                            e.dma_start(slots[i * HD:(i + 1) * HD, u, w, :, :],
                                        kept[w, part, :, bass.ds(b * T, T)].rearrange("(h d) t -> d h t", d=HD))\
                                .then_inc(slot_loaded[u], 16)

                def maxima(b, i, u):
                    wait(e, mparts_ready, b + 1)
                    for s in range(MAX_ROWS):
                        e.dma_start(slots[QK_ROWS + s:QK_ROWS + s + 1, u, 0, :, :],
                                    mparts[:, u, s, :]).then_inc(max_loaded[u], 16)

                e.wait_ge(ones_set, 2)
                for u in range(2):
                    e.wait_ge(parts_kept[u], 2 * 16 * (NC // 2))
                load(0, 0)
                load(1, 1)
                maxima(0, 0, 0)

                def step(b, u):
                    if not (isinstance(b, int) and b + 1 >= B):
                        maxima(b + 1, None, 1 - u)
                    if not (isinstance(b, int) and b + 2 >= B):
                        e.wait_ge(s2_ready, (b + 1) * G2)
                        load(b + 2, u)
                per_batch(e, step)

            @block.gpsimd
            def _(e):
                e.memset(slots[32:64, :, :, :, :], 1.0).then_inc(ones_set, 1)
                e.wait_ge(ones_set, 1)
                e.memset(V[:, :, :, :], 1.0).then_inc(ones_set, 1)
                for c in range(NC):
                    for w in range(2):
                        n = 2 * c + w
                        e.wait_ge(mid_ready, n + 1)
                        e.tensor_tensor(parts[:, c % 2, w, 2, :], rest[:, n % 2, :], parts[:, c % 2, w, 1, :],
                                        ALU.subtract).then_inc(lo_ready, 1)
                e.memset(Vh[:, :, :, :, :], 0.0).then_inc(vh_zero, 1)
                e.wait_ge(vh_zero, 1)
                e.wait_ge(v_ready, NC)

                def step(b, u):
                    wait(e, pv_group, (b - 1) * G2)
                    for j in range(2):
                        e.tensor_copy(Vh[:, u, j, :, :].rearrange("p g (h c) -> p (g h) c", c=HR + HC)[:, :, 0:HC],
                                      V[:, bass.ds(2 * b + j, 1), :, :].rearrange("p a h c -> p (a h) c"))\
                            .then_inc(vh_ready, 1)
                per_batch(e, step)

            @block.scalar
            def _(e):
                ln.act(e)
                for c in range(NC):
                    for w in range(2):
                        n = 2 * c + w
                        src = q[:, c % 2, :] if w == 0 else k.zT[:, chunk(c)]
                        e.wait_ge(q_ready, c + 1)
                        if c >= 2:
                            e.wait_ge(parts_kept[c % 2], 32 * (c // 2))
                        e.activation(parts[:, c % 2, w, 0, :], src, ACT.Copy).then_inc(hi_ready, 1)
                        e.wait_ge(rest_ready, n + 1)
                        e.activation(parts[:, c % 2, w, 1, :], rest[:, n % 2, :], ACT.Copy).then_inc(mid_ready, 1)
                    e.wait_ge(v_turned, c + 1)
                    e.wait_ge(ones_set, 2)
                    e.activation(V[:, 4 * c:4 * c + 4, :, 0:HD].rearrange("p t h d -> p (t h) d"),
                                 k.bank[4 + c % 2].rearrange("p (a d) -> p a d", d=HD), ACT.Copy).then_inc(v_ready, 1)

                def both_out(b):
                    e.wait_ge(pv_group, (b + 1) * G2)
                    wait(e, both_turned, b)
                    e.activation(both[:, :, :], k.bank[6][0:HR, :].rearrange("p (g t) -> p g t", g=2),
                                 ACT.Copy).then_inc(both_ready, 1)

                def step(b, u):
                    for g in range(G2):
                        if g == 1 and not (isinstance(b, int) and b == 0):
                            both_out(b - 1)
                        wait(e, s2_ready, b * G2 + g + 1)
                        wait(e, pv_group, b * G2 + g - 1)
                        e.activation(P[:, g % 2, :, :, :].rearrange("p a j t -> p (a j t)"),
                                     k.psum[:, 2 + 2 * (g % 2):4 + 2 * (g % 2), :].rearrange("p a n -> p (a n)"),
                                     ACT.Exp).then_inc(p_ready, 1)
                per_batch(e, step)
                both_out(B - 1)

            @block.tensor
            def _(e):
                ln.pe(e)
                for c in range(NC):
                    e.wait_ge(ln.z_ready, c + 1)
                    if c >= 2:
                        e.wait_ge(v_ready, c - 1)
                    for j in range(4):
                        mm = e.transpose(k.bank[4 + c % 2][:, j * 128:(j + 1) * 128],
                                         k.zT[:, (4 * c + j) * 128:(4 * c + j + 1) * 128], k.ident[:, :])
                    mm.then_inc(v_turned, 1)
                e.wait_ge(v_ready, NC)

                def scores_for_max(b, u, g):
                    wait(e, max_ready, b * G1 + g - 1)
                    for a in range(2):
                        h = 2 * (g % 8) + a
                        mm = e.matmul(k.bank[g % 2][:, a * T:(a + 1) * T],
                                      slots[0:QK_ROWS, u, 0, h, (g // 8) * 128:(g // 8 + 1) * 128],
                                      slots[0:QK_ROWS, u, 1, h, :], start=True, stop=True)
                    mm.then_inc(s1_ready, 1)

                def turn_max(b):
                    wait(e, max_ready, (b + 1) * G1)
                    wait(e, x_done, b - 1)
                    for s in range(2):
                        mm = e.transpose(k.bank[7][0:HEADS, s * 128:(s + 1) * 128], m[:, s, :], k.ident[:, :])
                    mm.then_inc(mt_ready, 1)

                def scores(b, u, g):
                    if g == 0:
                        e.wait_ge(max_loaded[u], 16 * MAX_ROWS * (b // 2 + 1) if isinstance(b, int) else 8 * MAX_ROWS * (b - u) + 16 * MAX_ROWS)
                    wait(e, p_ready, b * G2 + g - 1)
                    for a in range(2):
                        h = 2 * g + a
                        for j in range(2):
                            mm = e.matmul(k.psum[:, 2 + 2 * (g % 2) + a, j * T:(j + 1) * T],
                                          slots[0:QK_ROWS + MAX_ROWS, u, 1, h, j * 128:(j + 1) * 128],
                                          slots[0:QK_ROWS + MAX_ROWS, u, 0, h, :], start=True, stop=True)
                    mm.then_inc(s2_ready, 1)

                def values(b, u, g):
                    wait(e, p_ready, b * G2 + g + 1)
                    if g == 0:
                        wait(e, both_ready, b)
                        wait(e, vh_ready, 2 * b + 2)
                    for a in range(2):
                        h = 2 * g + a
                        for j in range(2):
                            mm = e.matmul(k.bank[6][0:HR, (h // 8) * T:(h // 8 + 1) * T],
                                          Vh[:, u, j, h // 8, (h % 8) * HR:(h % 8 + 1) * HR],
                                          P[:, g % 2, a, j, :], start=(h % 8 == 0 and j == 0),
                                          stop=(h % 8 == 7 and j == 1))
                    mm.then_inc(pv_group, 1)

                def turn_both(b):
                    wait(e, both_ready, b + 1)
                    wait(e, mstep, (b + 1) * 5 + 1 if not (isinstance(b, int) and b + 1 >= B) else B * 5)
                    wait(e, x_done, b)
                    for i in range(2):
                        for g in range(2):
                            mm = e.transpose(k.bank[7][:, (2 * i + g) * HR:(2 * i + g + 1) * HR],
                                             both[:, g, i * 128:(i + 1) * 128], k.ident[0:HR, 0:HR])
                    mm.then_inc(both_turned, 1)

                def turn_out(b):
                    wait(e, o_ready, b + 1)
                    for i in range(2):
                        mm = e.transpose(k.bank[7][:, i * 128:(i + 1) * 128], o[:, i, :], k.ident[:, :])
                    mm.then_inc(o_turned, 1)

                e.wait_ge(slot_loaded[0], 16 * LOADS)
                for g in range(G1):
                    scores_for_max(0, 0, g)
                turn_max(0)

                def step(b, u):
                    ahead = not (isinstance(b, int) and b + 1 >= B)
                    if ahead:
                        n = b + 1 - (1 - u)
                        e.wait_ge(slot_loaded[1 - u], 8 * LOADS * n + 16 * LOADS)
                    for g in range(G2):
                        if ahead:
                            scores_for_max(b + 1, 1 - u, 2 * g)
                            scores_for_max(b + 1, 1 - u, 2 * g + 1)
                        scores(b, u, g)
                        if g:
                            values(b, u, g - 1)
                        if not (isinstance(b, int) and b == 0):
                            if g == 2:
                                turn_both(b - 1)
                            if g == 4:
                                turn_out(b - 1)
                    if ahead:
                        turn_max(b + 1)
                    values(b, u, G2 - 1)
                per_batch(e, step)
                turn_both(B - 1)
                turn_out(B - 1)

            @block.vector
            def _(e):
                ln.dve(e)
                for c in range(NC):
                    if c >= 2:
                        e.wait_ge(rest_ready, 2 * (c - 2) + 1)
                    e.tensor_scalar(q[:, c % 2, :], k.zT[:, chunk(c)], k.qscale[:, 0:1], None, ALU.mult).then_inc(q_ready, 1)
                    for w in range(2):
                        n = 2 * c + w
                        if w == 0:
                            e.wait_ge(q_ready, c + 1)
                        e.wait_ge(hi_ready, n + 1)
                        if n >= 2:
                            e.wait_ge(lo_ready, n - 1)
                        src = q[:, c % 2, :] if w == 0 else k.zT[:, chunk(c)]
                        e.tensor_tensor(rest[:, n % 2, :], src, parts[:, c % 2, w, 0, :], ALU.subtract).then_inc(rest_ready, 1)

                def maxima(b, u, between):
                    for g in range(G1):
                        e.wait_ge(s1_ready, b * G1 + g + 1)
                        if g == 0:
                            wait(e, mt_ready, b)
                        e.tensor_reduce(m[:, g // 8, 2 * (g % 8):2 * (g % 8) + 2],
                                        k.bank[g % 2].rearrange("p (a t) -> p a t", a=2), AX.X, ALU.max)\
                            .then_inc(max_ready, 1)
                        between(g)
                    e.wait_ge(mt_ready, b + 1)
                    i = 5 * b
                    e.tensor_scalar(negm[:, :], k.bank[7][0:HEADS, 0:T], -1.0, None, ALU.mult).then_inc(mstep, 1)
                    e.wait_ge(mstep, i + 1)
                    if not (isinstance(b, int) and b < 2):
                        n = (b - u) if not isinstance(b, int) else b - u
                        e.wait_ge(max_loaded[u], 8 * MAX_ROWS * n)
                    e.tensor_copy(mparts[:, u, 0, :], negm[:, :]).then_inc(mstep, 1)
                    e.wait_ge(mstep, i + 2)
                    e.tensor_tensor(nrest[:, :], negm[:, :], mparts[:, u, 0, :], ALU.subtract).then_inc(mstep, 1)
                    e.wait_ge(mstep, i + 3)
                    e.tensor_copy(mparts[:, u, 1, :], nrest[:, :]).then_inc(mstep, 1)
                    e.wait_ge(mstep, i + 4)
                    e.tensor_tensor(mparts[:, u, 2, :], nrest[:, :], mparts[:, u, 1, :], ALU.subtract).then_inc(mstep, 1)
                    e.wait_ge(mstep, i + 5)
                    e.sem_inc(mparts_ready, 1)

                def normalise(b):
                    e.wait_ge(both_turned, b + 1)
                    out = k.bank[7][:, 0:2 * HEADS * HC].rearrange("p (a d) -> p a d", d=HC)
                    e.reciprocal(recip[:, :], out[:, :, HD]).then_inc(recip_ready, 1)
                    e.wait_ge(recip_ready, b + 1)
                    wait(e, o_turned, b)
                    e.tensor_tensor(o[:, :, :].rearrange("p i (h d) -> p (i h) d", d=HD), out[:, :, 0:HD],
                                    along(recip[:, :], HD), ALU.mult).then_inc(o_ready, 1)

                def add(b):
                    e.wait_ge(o_turned, b + 1)
                    e.tensor_tensor(k.xT[:, bass.ds(b * T, T)], k.bank[7][:, 0:T], k.xT[:, bass.ds(b * T, T)],
                                    ALU.add).then_inc(x_done, 1)

                maxima(0, 0, lambda g: None)

                def step(b, u):
                    if isinstance(b, int) and b == 0:
                        maxima(1, 1, lambda g: None)
                    elif isinstance(b, int) and b == B - 1:
                        normalise(b - 1)
                        add(b - 1)
                    else:
                        maxima(b + 1, 1 - u, lambda g: normalise(b - 1) if g == 7 else add(b - 1) if g == 11 else None)
                per_batch(e, step)
                normalise(B - 1)
                add(B - 1)


def time_mix_attention(nc, k):
    ctx, sb, sem = phase(nc, k)
    with ctx:
        ln = Norm(k, sem, "a1")
        mixed, xm = sb("mixed", [128, 2, CW]), sb("xm", [128, 2, CW])
        w = sb("w", [128, 1])
        now = sb("now", [128, 1])
        keep = sb("keep", [128, CW])
        kc, gate_r = sb("kc", [128, 2, CW]), sb("gate_r", [128, 2, CW])
        ek, kv = sb("ek", [128, 2, CW]), sb("kv", [128, 2, CW])
        past_k, past_kv = sb("past_k", [128, 2, CW]), sb("past_kv", [128, 2, CW])
        num, den = sb("num", [128, 2, CW]), sb("den", [128, 2, CW])
        xm_ready, mix_ready, proj, kc_ready, ek_ready, gate_ready = sem("xm_ready"), sem("mix_ready"), sem("proj"), sem("kc_ready"), sem("ek_ready"), sem("gate_ready")
        w1_ready, w_ready, prep, step, kv_ready, y_ready, o_ready, x_done = sem("w1_ready"), sem("w_ready"), sem("prep"), sem("step"), sem("kv_ready"), sem("y_ready"), sem("o_ready"), sem("x_done")
        PROJ = 3
        DVE_STEPS = 9

        def batches(a):
            return a.rearrange("p (b t) -> p b t", t=T)

        with nc.Block() as block:
            @block.tensor
            def _(e):
                ln.pe(e)

                def out(c):
                    e.wait_ge(y_ready, c + 1)
                    if c >= 1:
                        e.wait_ge(x_done, c)
                    e.matmul(k.bank[7][:, :], k.w1T[:, 3, :], num[:, c % 2, :], start=True, stop=True).then_inc(o_ready, 1)

                for c in range(NC):
                    e.wait_ge(xm_ready, c + 1)
                    for j in range(PROJ):
                        if c >= 1:
                            e.wait_ge((kc_ready, kv_ready, gate_ready)[j], c)
                        e.matmul(k.bank[4 + j][:, :], k.w1T[:, j, :], xm[:, c % 2, :],
                                 start=True, stop=True).then_inc(proj, 1)
                    if c:
                        out(c - 1)
                out(NC - 1)

            @block.scalar
            def _(e):
                ln.act(e)
                e.activation(w[:, :], k.smallT[:, 3, 64:65], ACT.Exp).then_inc(w1_ready, 1)
                e.activation(now[:, :], k.smallT[:, 3, 32:33], ACT.Exp).then_inc(w1_ready, 1)
                e.wait_ge(w1_ready, 2)
                e.activation(w[:, :], w[:, :], ACT.Exp, scale=-1.0).then_inc(w_ready, 1)

                def weights(c):
                    e.wait_ge(kc_ready, c + 1)
                    if c >= 2:
                        e.wait_ge(step, (c - 2) * DVE_STEPS + DVE_STEPS)
                    e.activation(ek[:, c % 2, :], kc[:, c % 2, :], ACT.Exp).then_inc(ek_ready, 1)

                def gate(c):
                    e.wait_ge(proj, PROJ * c + 3)
                    if c >= 2:
                        e.wait_ge(y_ready, c - 1)
                    e.activation(gate_r[:, c % 2, :], k.bank[6][:, :], ACT.Sigmoid).then_inc(gate_ready, 1)

                for c in range(0, NC, 2):
                    weights(c)
                    gate(c)
                    gate(c + 1)
                    weights(c + 1)

            @block.vector
            def _(e):
                ln.dve(e)
                e.wait_ge(w_ready, 1)
                e.memset(keep[:, :], 1.0).then_inc(prep, 1)
                e.wait_ge(prep, 1)
                e.tensor_scalar(keep[:, :], keep[:, :], w[:, 0:1], None, ALU.mult).then_inc(prep, 1)
                e.wait_ge(prep, 2)
                for b in range(BPC):
                    e.memset(keep[:, b * T:b * T + 1], 0.0).then_inc(prep, 1)
                e.wait_ge(prep, 2 + BPC)

                def mix(c):
                    z, a, o = batches(k.zT[:, chunk(c)]), batches(mixed[:, c % 2, :]), batches(xm[:, c % 2, :])
                    e.wait_ge(ln.z_ready, c + 1)
                    if c >= 2:
                        e.wait_ge(proj, PROJ * (c - 1))
                    e.tensor_scalar(mixed[:, c % 2, :], k.zT[:, chunk(c)], k.vec(V_MIX), None, ALU.mult).then_inc(mix_ready, 1)
                    e.wait_ge(mix_ready, 3 * c + 1)
                    e.tensor_copy(o[:, :, 0:1], a[:, :, 0:1]).then_inc(mix_ready, 1)
                    e.scalar_tensor_tensor(out=o[:, :, 1:T], in0=z[:, :, 0:T - 1], scalar=k.one_minus_mix[:, 0:1],
                                           in1=a[:, :, 1:T], op0=ALU.mult, op1=ALU.add).then_inc(mix_ready, 1)
                    e.wait_ge(mix_ready, 3 * c + 3)
                    e.sem_inc(xm_ready, 1)

                mix(0)
                for c in range(NC):
                    u, s = c % 2, c * DVE_STEPS
                    e.wait_ge(proj, PROJ * c + 1)
                    if c >= 2:
                        e.wait_ge(ek_ready, c - 1)
                    e.tensor_scalar(kc[:, u, :], k.bank[4][:, :], 60.0, None, ALU.min).then_inc(kc_ready, 1)
                    if c + 1 < NC:
                        mix(c + 1)
                    e.wait_ge(ek_ready, c + 1)
                    e.wait_ge(proj, PROJ * c + 2)
                    e.tensor_tensor(kv[:, u, :], k.bank[5][:, :], ek[:, u, :], ALU.mult).then_inc(kv_ready, 1)
                    e.tensor_tensor_scan(past_k[:, u, :], keep[:, :], ek[:, u, :], 0.0, ALU.mult, ALU.add).then_inc(step, 1)
                    e.wait_ge(kv_ready, c + 1)
                    e.tensor_tensor_scan(past_kv[:, u, :], keep[:, :], kv[:, u, :], 0.0, ALU.mult, ALU.add).then_inc(step, 1)
                    if c >= 2:
                        e.wait_ge(o_ready, c - 1)
                    e.wait_ge(step, s + 2)
                    for cur, past, dst in ((ek, past_k, den), (kv, past_kv, num)):
                        a, p, o = batches(cur[:, u, :]), batches(past[:, u, :]), batches(dst[:, u, :])
                        e.tensor_scalar(o[:, :, 0:1], a[:, :, 0:1], now[:, 0:1], None, ALU.mult).then_inc(step, 1)
                        e.scalar_tensor_tensor(out=o[:, :, 1:T], in0=a[:, :, 1:T], scalar=now[:, 0:1],
                                               in1=p[:, :, 0:T - 1], op0=ALU.mult, op1=ALU.add).then_inc(step, 1)
                    e.wait_ge(step, s + 6)
                    e.tensor_scalar(den[:, u, :], den[:, u, :], 1e-16, None, ALU.add).then_inc(step, 1)
                    e.wait_ge(step, s + 7)
                    e.reciprocal(den[:, u, :], den[:, u, :]).then_inc(step, 1)
                    e.wait_ge(gate_ready, c + 1)
                    e.tensor_tensor(num[:, u, :], num[:, u, :], gate_r[:, u, :], ALU.mult).then_inc(step, 1)
                    e.wait_ge(step, s + 9)
                    e.tensor_tensor(num[:, u, :], num[:, u, :], den[:, u, :], ALU.mult).then_inc(y_ready, 1)
                    e.wait_ge(o_ready, c + 1)
                    e.tensor_tensor(k.xT[:, chunk(c)], k.bank[7][:, :], k.xT[:, chunk(c)], ALU.add).then_inc(x_done, 1)


def state_space(nc, k):
    ctx, sb, sem = phase(nc, k)
    with ctx:
        ln = Norm(k, sem, "ss")
        one = sb("one", [128, 1])
        xdt = sb("xdt", [DTR, 2, CW])
        v, neg = sb("v", [128, 2, CW]), sb("neg", [128, 2, CW])
        dt, dtu = sb("dt", [128, N]), sb("dtu", [128, N])
        bc, bc_rest, bc_mid = sb("bc", [2 * NS, 2, CW]), sb("bc_rest", [2 * NS, 2, CW]), sb("bc_mid", [2 * NS, 2, CW], BF16)
        parts = sb("parts", [6 * NS, N], BF16)
        pick = sb("pick", [6 * NS, 2 * NS, 128], BF16)
        Bs, Ab, Bu = sb("Bs", [128, 2, CW]), sb("Ab", [128, 2, CW]), sb("Bu", [128, 2, CW])
        h, hc, a_now = sb("h", [128, 2, CW]), sb("hc", [128, NC, CW]), sb("a_now", [128, 2])
        set_up, picked, A_step = sem("set_up"), sem("picked"), sem("A_step")
        xdt_mm, xdt_ready, dt_mm, bc_mm, v_ready, neg_ready = sem("xdt_mm"), sem("xdt_ready"), sem("dt_mm"), sem("bc_mm"), sem("v_ready"), sem("neg_ready")
        ex_ready, log_ready, dt_ready, dtu_ready = sem("ex_ready"), sem("log_ready"), sem("dt_ready"), sem("dtu_ready")
        bc_ready, hi_ready, rest_ready, mid_ready, parts_ready = sem("bc_ready"), sem("hi_ready"), sem("rest_ready"), sem("mid_ready"), sem("parts_ready")
        b_mm, c_mm, bs_ready, ab_ready, bu_ready = sem("b_mm"), sem("c_mm"), sem("bs_ready"), sem("ab_ready"), sem("bu_ready")
        h_ready, hc_ready, y_mm, zd_ready, x_done, a_now_ready = sem("h_ready"), sem("hc_ready"), sem("y_mm"), sem("zd_ready"), sem("x_done"), sem("a_now_ready")

        def wait(e, s, v):
            if not (isinstance(v, int) and v <= 0):
                e.wait_ge(s, v)

        def every_state(e, step):
            step(0, 0)
            step(1, 1)
            with e.Fori(1, NS // 2 - 1) as i:
                step(2 * i, 0)
                step(2 * i + 1, 1)
            step(NS - 2, 0)
            step(NS - 1, 1)

        with nc.Block() as block:
            @block.gpsimd
            def _(e):
                e.memset(one[:, :], 1.0).then_inc(set_up, 1)
                e.wait_ge(set_up, 1)
                e.memset(pick[:, :, :], 0.0).then_inc(picked, 1)
                for s in range(3):
                    e.wait_ge(picked, s + 1)
                    e.affine_select(out=pick[:, :, :], in_=pick[:, :, :], compare_op=ALU.not_equal, fill=1.0,
                                    base=-2 * NS * s, pattern=[[-1, 2 * NS], [0, 128]], channel_multiplier=1)\
                        .then_inc(picked, 1)
                e.wait_ge(picked, 4)
                e.wait_ge(dtu_ready, NC)

                def state(n, s):
                    for c in range(NC):
                        g = n * NC + c
                        e.wait_ge(bs_ready, g + 1)
                        wait(e, h_ready, g - 1)
                        e.tensor_tensor(Bu[:, c % 2, :], Bs[:, c % 2, :], dtu[:, chunk(c)], ALU.mult).then_inc(bu_ready, 1)
                every_state(e, state)

            @block.tensor
            def _(e):
                ln.pe(e)
                for c in range(NC):
                    e.wait_ge(ln.z_ready, NC)
                    if c >= 2:
                        e.wait_ge(xdt_ready, c - 1)
                    e.matmul(k.bank[c % 2][0:DTR, :], k.w_xdtT, k.zT[:, chunk(c)], start=True, stop=True).then_inc(xdt_mm, 1)
                    if c >= 2:
                        e.wait_ge(bc_ready, c - 1)
                    e.matmul(k.bank[4 + c % 2][0:2 * NS, :], k.w_bcT, k.zT[:, chunk(c)], start=True, stop=True).then_inc(bc_mm, 1)
                    e.wait_ge(xdt_ready, c + 1)
                    if c >= 2:
                        e.wait_ge(v_ready, c - 1)
                    e.matmul(k.bank[2 + c % 2][:, :], k.w_dtT, xdt[:, c % 2, :], start=True, stop=True).then_inc(dt_mm, 1)
                e.wait_ge(parts_ready, NC)
                e.wait_ge(v_ready, NC)
                e.wait_ge(picked, 4)

                def row_of(n):
                    return pick[:, bass.ds(n, 1), :].rearrange("p a m -> p (a m)")

                def spread(n, c):
                    g = n * NC + c
                    wait(e, bs_ready, g - 1)
                    e.matmul(k.bank[c % 2][:, :], row_of(n), parts[:, chunk(c)], start=True, stop=True).then_inc(b_mm, 1)
                    wait(e, hc_ready, g - 1)
                    e.matmul(k.bank[2 + c % 2][:, :], row_of(n + NS), parts[:, chunk(c)], start=True, stop=True).then_inc(c_mm, 1)

                def state(n, s):
                    for c in range(NC):
                        if not (isinstance(n, int) and n == NS - 1 and c >= NC - 2):
                            spread(n + (c + 2) // NC, (c + 2) % NC)
                        e.wait_ge(hc_ready, n * NC + c + 1)
                        e.matmul(k.bank[4 + c][:, :], k.ident[:, :], hc[:, c, :], start=isinstance(n, int) and n == 0,
                                 stop=isinstance(n, int) and n == NS - 1).then_inc(y_mm, 1)
                spread(0, 0)
                spread(0, 1)
                every_state(e, state)

            @block.scalar
            def _(e):
                ln.act(e)
                e.activation(k.A[:, :], k.A[:, :], ACT.Exp).then_inc(A_step, 1)
                e.wait_ge(set_up, 1)
                for c in range(NC):
                    u = c % 2
                    e.wait_ge(xdt_mm, c + 1)
                    if c >= 2:
                        e.wait_ge(dt_mm, c - 1)
                    e.activation(xdt[:, u, :], k.bank[u][0:DTR, :], ACT.Identity, bias=k.vec(V_BXDT)[0:DTR, :]).then_inc(xdt_ready, 1)
                    e.wait_ge(bc_mm, c + 1)
                    if c >= 2:
                        e.wait_ge(parts_ready, c - 1)
                    e.activation(bc[:, u, :], k.bank[4 + u][0:2 * NS, :], ACT.Identity, bias=k.vec(V_BBC)[0:2 * NS, :]).then_inc(bc_ready, 1)
                    e.wait_ge(bc_ready, c + 1)
                    e.activation(parts[0:2 * NS, chunk(c)], bc[:, u, :], ACT.Copy).then_inc(hi_ready, 1)
                    e.wait_ge(rest_ready, c + 1)
                    e.activation(bc_mid[:, u, :], bc_rest[:, u, :], ACT.Copy).then_inc(mid_ready, 1)
                    e.activation(parts[2 * NS:4 * NS, chunk(c)], bc_rest[:, u, :], ACT.Copy).then_inc(mid_ready, 1)
                    e.wait_ge(neg_ready, c + 1)
                    e.activation(neg[:, u, :], neg[:, u, :], ACT.Exp).then_inc(ex_ready, 1)
                    e.wait_ge(ex_ready, c + 1)
                    e.activation(neg[:, u, :], neg[:, u, :], ACT.Ln, bias=one[:, 0:1]).then_inc(log_ready, 1)
                e.wait_ge(A_step, 2)
                e.wait_ge(dtu_ready, NC)

                def state(n, s):
                    wait(e, a_now_ready, n + 1)
                    for c in range(NC):
                        g = n * NC + c
                        e.wait_ge(b_mm, g + 1)
                        wait(e, bu_ready, g - 1)
                        e.activation(Bs[:, c % 2, :], k.bank[c % 2][:, :], ACT.Copy).then_inc(bs_ready, 1)
                        wait(e, h_ready, g - 1)
                        e.activation(Ab[:, c % 2, :], dt[:, chunk(c)], ACT.Exp, scale=a_now[:, s:s + 1]).then_inc(ab_ready, 1)
                every_state(e, state)

            @block.vector
            def _(e):
                ln.dve(e)
                e.wait_ge(A_step, 1)
                e.tensor_scalar(k.A[:, :], k.A[:, :], -1.0, None, ALU.mult).then_inc(A_step, 1)
                for c in range(NC):
                    u = c % 2
                    e.wait_ge(hi_ready, c + 1)
                    e.tensor_tensor(bc_rest[:, u, :], bc[:, u, :], parts[0:2 * NS, chunk(c)], ALU.subtract).then_inc(rest_ready, 1)
                    e.wait_ge(dt_mm, c + 1)
                    if c >= 2:
                        e.wait_ge(dt_ready, c - 1)
                    e.tensor_scalar(v[:, u, :], k.bank[2 + u][:, :], k.vec(V_BDT), None, ALU.add).then_inc(v_ready, 1)
                    e.wait_ge(v_ready, c + 1)
                    e.scalar_tensor_tensor(out=neg[:, u, :], in0=v[:, u, :], scalar=-1.0, in1=v[:, u, :],
                                           op0=ALU.mult, op1=ALU.min).then_inc(neg_ready, 1)
                    e.wait_ge(mid_ready, 2 * c + 2)
                    e.tensor_tensor(parts[4 * NS:6 * NS, chunk(c)], bc_rest[:, u, :], bc_mid[:, u, :],
                                    ALU.subtract).then_inc(parts_ready, 1)
                    e.wait_ge(log_ready, c + 1)
                    e.scalar_tensor_tensor(out=dt[:, chunk(c)], in0=v[:, u, :], scalar=0.0, in1=neg[:, u, :],
                                           op0=ALU.max, op1=ALU.add).then_inc(dt_ready, 1)
                    e.wait_ge(dt_ready, c + 1)
                    e.tensor_tensor(dtu[:, chunk(c)], dt[:, chunk(c)], k.zT[:, chunk(c)], ALU.mult).then_inc(dtu_ready, 1)

                def column(n, s):
                    wait(e, ab_ready, (n - 1) * NC)
                    e.tensor_copy(a_now[:, s:s + 1], k.A[:, bass.ds(n, 1)]).then_inc(a_now_ready, 1)

                def state(n, s):
                    if not (isinstance(n, int) and n == NS - 1):
                        column(n + 1, 1 - s)
                    for c in range(NC):
                        g, u = n * NC + c, c % 2
                        e.wait_ge(ab_ready, g + 1)
                        e.wait_ge(bu_ready, g + 1)
                        wait(e, hc_ready, g - 1)
                        for b in range(BPC):
                            r = slice(b * T, (b + 1) * T)
                            i = e.tensor_tensor_scan(h[:, u, r], Ab[:, u, r], Bu[:, u, r], 0.0, ALU.mult, ALU.add)
                        i.then_inc(h_ready, 1)
                        e.wait_ge(h_ready, g + 1)
                        e.wait_ge(c_mm, g + 1)
                        wait(e, y_mm, g - NC + 1)
                        e.tensor_tensor(hc[:, c, :], k.bank[2 + u][:, :], h[:, u, :], ALU.mult).then_inc(hc_ready, 1)
                column(0, 0)
                every_state(e, state)
                for c in range(NC):
                    e.scalar_tensor_tensor(out=k.zT[:, chunk(c)], in0=k.zT[:, chunk(c)], scalar=k.vec(V_D),
                                           in1=k.xT[:, chunk(c)], op0=ALU.mult, op1=ALU.add).then_inc(zd_ready, 1)
                for c in range(NC):
                    e.wait_ge(zd_ready, c + 1)
                    e.wait_ge(y_mm, (NS - 1) * NC + c + 1)
                    e.tensor_tensor(k.xT[:, chunk(c)], k.bank[4 + c][:, :], k.zT[:, chunk(c)], ALU.add).then_inc(x_done, 1)


PAIRS = NT // 2
PW = 256
PK = PH * TOPK
OW = 64
HI = NE // 128


def product_keys(nc, k):
    ctx, sb, sem = phase(nc, k)
    with ctx:
        ln = Norm(k, sem, "pk")
        stats, mv = sb("stats", [128, NC, 6]), sb("mv", [128, 2])
        bn_scale, bn_bias, bn_log, bn_eps = sb("bn_scale", [128, 1]), sb("bn_bias", [128, 1]), sb("bn_log", [128, 1]), sb("bn_eps", [128, 1])
        low_no, high_no = sb("low_no", [128, 128, OW], F16), sb("high_no", [128, HI, 128], F16)
        xn = sb("xn", [128, PW])
        sims = sb("sims", [128, 2, 2 * PH * NK])
        tops, topi, topf = sb("tops", [128, 2, 2, PH, 8]), sb("topi", [128, 2, 2, PH, 8], U32), sb("topf", [128, 2, 2, PH, 8])
        cand = sb("cand", [128, 2 * PH, 8, 8])
        best, pos = sb("best", [128, 2 * PH, 8]), sb("pos", [128, 2 * PH, 8], U32)
        rank, rankf = sb("rank", [128, 2, 2 * PK], U32), sb("rankf", [128, 2, 2 * PK])
        hit = sb("hit", [128, 2, 2 * PH, 8, 8])
        key = sb("key", [128, 2, 2 * PK])
        expert, expert_i = sb("expert", [128, 2 * PK]), sb("expert_i", [128, 2 * PK], U32)
        split_i, split = sb("split_i", [128, 2, 2 * PK], U32), sb("split", [128, 2, 2 * PK])
        shifted, ex = sb("shifted", [128, 2 * PH, 8]), sb("ex", [128, 2 * PH, 8])
        total, share = sb("total", [128, 2 * PH]), sb("share", [128, 2 * PH, 8])
        lowT, highT = sb("lowT", [128, 128], F16), sb("highT", [128, 128], F16)
        shareT = sb("shareT", [128, 2, 128], F16)
        at_high = sb("at_high", [128, HI, 128], F16)
        rows = sb("rows", [128, 2, 2, HI, 128], F16)
        onehot = sb("onehot", [128, 2, 128, OW], F16)
        G, WG = sb("G", [128, ET, PW]), sb("WG", [128, ET, PW])
        A0, TB, O0, XB = 0, 2, 3, 7
        bn, bn_rstd, consts, rows_zero = sem("bn"), sem("bn_rstd"), sem("consts"), sem("rows_zero")
        xn_ready, a_mm, a_used, tops_ready, topi_ready = sem("xn_ready"), sem("a_mm"), sem("a_used"), sem("tops_ready"), sem("topi_ready")
        cand_ready, topf_ready, best_ready, pos_ready = sem("cand_ready"), sem("topf_ready"), sem("best_ready"), sem("pos_ready")
        rank_ready, rankf_ready, hit_ready, picked, key_ready = sem("rank_ready"), sem("rankf_ready"), sem("hit_ready"), sem("picked"), sem("key_ready")
        expert_ready, expert_i_ready, split_i_ready, split_ready = sem("expert_ready"), sem("expert_i_ready"), sem("split_i_ready"), sem("split_ready")
        shifted_ready, ex_ready, total_ready, share_ready = sem("shifted_ready"), sem("ex_ready"), sem("total_ready"), sem("share_ready")
        turned, turned_out, turned_out_part, low_share, at_ready = sem("turned"), sem("turned_out"), sem("turned_out_part"), sem("low_share"), sem("at_ready")
        rows_dve, rows_pool, oh_ready, outer_mm, wg_ready, out_mm, x_done, settled = sem("rows_dve"), sem("rows_pool"), sem("oh_ready"), sem("outer_mm"), sem("wg_ready"), sem("out_mm"), sem("x_done"), sem("settled")

        def wait(e, s, v):
            if not (isinstance(v, int) and v <= 0):
                e.wait_ge(s, v)

        def last(p, n=1):
            return isinstance(p, int) and p + n >= PAIRS

        def sim_use(p):
            return 0 if isinstance(p, int) and p == 0 else 6 * p - 4

        def gelu_use(p):
            return 6 * p + 4 - (2 if last(p) else 0)

        def loop(e, body):
            body(0)
            with e.Fori(1, PAIRS - 2) as p:
                body(p)
            body(PAIRS - 2)
            body(PAIRS - 1)

        with nc.Block() as block:
            @block.tensor
            def _(e):
                ln.pe(e)

                def sim(p):
                    wait(e, xn_ready, p + 1)
                    for t in range(2):
                        n = sim_use(p) + t
                        wait(e, a_used, n - 1)
                        e.matmul(k.bank[A0 + t][:, :], xn[:, t * 128:(t + 1) * 128], k.M[:, :],
                                 start=True, stop=True).then_inc(a_mm, 1)

                def activations(p):
                    for t in range(4):
                        wait(e, a_used, gelu_use(p) + t - 1)
                        for j in range(2):
                            mm = e.matmul(k.bank[A0 + t % 2][:, j * PW:(j + 1) * PW],
                                          k.key_inT[:, (2 * t + j) * 128:(2 * t + j + 1) * 128],
                                          k.zT[:, bass.ds(p * PW, PW)], start=True, stop=True)
                        mm.then_inc(a_mm, 1)

                def turn(p):
                    wait(e, split_ready, p + 1)
                    wait(e, share_ready, p + 1)
                    wait(e, turned_out, p)
                    wait(e, low_share, p)
                    for i, src in enumerate((split[:, 0, :], split[:, 1, :], share[:, :, :].rearrange("p a b -> p (a b)"))):
                        mm = e.transpose(k.bank[TB][:, i * 128:(i + 1) * 128], src, k.ident[:, :])
                    mm.then_inc(turned, 1)

                def outer(p, a):
                    wait(e, oh_ready, 2 * p + a + 1)
                    wait(e, rows_dve, p + 1)
                    wait(e, rows_pool, p + 1)
                    for q in range(2):
                        bank = 2 * a + q
                        wait(e, wg_ready, 4 * (p - 1) + bank + 1)
                        for i in range(32):
                            n = q * 32 + i
                            for s in range(2):
                                mm = e.matmul(k.bank[O0 + bank][:, i * 2 * HI:(i + 1) * 2 * HI], onehot[:, a, :, n],
                                              rows[:, s, :, :, a * OW + n], start=(s == 0), stop=(s == 1))
                        mm.then_inc(outer_mm, 1)

                def out(p):
                    wait(e, wg_ready, 4 * p + 4)
                    wait(e, x_done, p)
                    for j in range(ET):
                        mm = e.matmul(k.bank[XB][:, 0:PW], k.key_out[:, j, :], WG[:, j, :], start=(j == 0), stop=(j == ET - 1))
                    mm.then_inc(out_mm, 1)

                e.wait_ge(ln.z_ready, NC)
                sim(0)
                sim(1)
                turn(0)
                activations(0)

                def body(p):
                    outer(p, 0)
                    outer(p, 1)
                    if not last(p, 2):
                        sim(p + 2)
                    if not last(p):
                        turn(p + 1)
                        activations(p + 1)
                    out(p)
                loop(e, body)

            @block.scalar
            def _(e):
                ln.act(e)
                e.wait_ge(rows_zero, 1)
                e.wait_ge(bn, 2)
                e.activation(bn_log[:, :], mv[:, 1:2], ACT.Ln, bias=bn_eps[:, 0:1]).then_inc(bn_rstd, 1)
                e.wait_ge(bn_rstd, 1)
                e.activation(bn_scale[:, :], bn_log[:, :], ACT.Exp, scale=-0.5).then_inc(bn_rstd, 1)
                e.activation(low_no[:, :, :], along(k.iota_f[:, :], OW), ACT.Copy).then_inc(consts, 1)
                e.activation(high_no[:, :, :], along(k.iota_f[:, 0:HI], 128), ACT.Copy).then_inc(consts, 1)

                def sims_out(p):
                    wait(e, topi_ready, p)
                    for t in range(2):
                        wait(e, a_mm, sim_use(p) + t + 1)
                        e.activation(sims[:, t, :], k.bank[A0 + t][:, :], ACT.Copy).then_inc(a_used, 1)

                def gelus(p):
                    wait(e, wg_ready, 4 * p)
                    for t in range(4):
                        wait(e, a_mm, gelu_use(p) + t + 1)
                        e.activation(G[:, 2 * t:2 * t + 2, :], k.bank[A0 + t % 2].rearrange("p (a n) -> p a n", a=2),
                                     ACT.Gelu).then_inc(a_used, 1)

                def first_half(p):
                    wait(e, topi_ready, p + 1)
                    wait(e, picked, p)
                    e.activation(topf[:, :, :, :, :], topi[:, :, :, :, :], ACT.Copy).then_inc(topf_ready, 1)
                    wait(e, rank_ready, p + 1)
                    wait(e, hit_ready, p)
                    e.activation(rankf[:, :, :], rank[:, :, :], ACT.Copy).then_inc(rankf_ready, 1)

                def second_half(p):
                    wait(e, shifted_ready, p + 1)
                    wait(e, share_ready, p)
                    e.activation(ex[:, :, :], shifted[:, :, :], ACT.Exp).then_inc(ex_ready, 1)
                    wait(e, split_i_ready, p + 1)
                    wait(e, turned, p)
                    e.activation(split[:, :, :], split_i[:, :, :], ACT.Copy).then_inc(split_ready, 1)
                    wait(e, turned, p + 1)
                    wait(e, oh_ready, 2 * p)
                    wait(e, rows_dve, p)
                    e.activation(shareT[:, 0, :], k.bank[TB][:, 256:384], ACT.Copy).then_inc(turned_out_part, 1)
                    e.activation(highT[:, :], k.bank[TB][:, 128:256], ACT.Copy).then_inc(turned_out_part, 1)
                    e.activation(lowT[:, :], k.bank[TB][:, 0:128], ACT.Copy).then_inc(turned_out, 1)

                sims_out(0)
                first_half(0)
                second_half(0)
                sims_out(1)
                gelus(0)

                def body(p):
                    if not last(p):
                        first_half(p + 1)
                        if not last(p, 2):
                            sims_out(p + 2)
                        second_half(p + 1)
                        gelus(p + 1)
                loop(e, body)

            @block.gpsimd
            def _(e):
                e.memset(bn_eps[:, :], BN_EPS).then_inc(rows_zero, 1)
                e.wait_ge(rows_zero, 1)
                e.memset(rows[:, :, :, :, :], 0.0).then_inc(rows_zero, 1)
                e.wait_ge(rows_zero, 2)

                def sums(p):
                    wait(e, tops_ready, p + 1)
                    wait(e, pos_ready, p)
                    for t in range(2):
                        e.tensor_tensor(cand[:, t * PH:(t + 1) * PH, :, :], along(tops[:, t, 0, :, :], 8),
                                        across(tops[:, t, 1, :, :], 8), ALU.add).then_inc(cand_ready, 1)

                def pick(p):
                    wait(e, topf_ready, p + 1)
                    wait(e, hit_ready, p + 1)
                    wait(e, rows_pool, p)
                    for w in range(2):
                        for t in range(2):
                            i = e.tensor_tensor(hit[:, w, t * PH:(t + 1) * PH, :, :], hit[:, w, t * PH:(t + 1) * PH, :, :],
                                                across(topf[:, t, w, :, :], 8), ALU.mult)
                    i.then_inc(picked, 1)

                def low_rows(p):
                    wait(e, cand_ready, 2 * PAIRS if last(p) else 2 * p + 4)
                    wait(e, picked, p + 1)
                    wait(e, at_ready, p + 1)
                    wait(e, low_share, p + 1)
                    wait(e, outer_mm, 4 * p)
                    for t in range(2):
                        s = slice(64 * t, 64 * t + 64)
                        i = e.tensor_tensor(rows[s, 1, t, :, :], at_high[s, :, :], across(shareT[s, 1, :], HI), ALU.mult)
                    i.then_inc(rows_pool, 1)

                sums(0)
                pick(0)

                def body(p):
                    if not last(p):
                        sums(p + 1)
                    low_rows(p)
                    if not last(p):
                        pick(p + 1)
                loop(e, body)

            @block.vector
            def _(e):
                ln.dve(e)
                e.wait_ge(ln.z_ready, NC)
                for c in range(NC):
                    i = e.bn_stats(stats[:, c, :], k.zT[:, chunk(c)])
                i.then_inc(bn, 1)
                e.wait_ge(bn, 1)
                e.bn_aggr(mv[:, :], stats[:, :, :]).then_inc(bn, 1)
                e.wait_ge(bn_rstd, 2)
                e.tensor_scalar(bn_scale[:, :], bn_scale[:, :], k.vec(V_GAMMA), None, ALU.mult).then_inc(bn, 1)
                e.wait_ge(bn, 3)
                e.tensor_scalar(bn_bias[:, :], mv[:, 0:1], bn_scale[:, 0:1], -1.0, ALU.mult, ALU.mult).then_inc(bn, 1)
                e.wait_ge(bn, 4)
                e.tensor_scalar(bn_bias[:, :], bn_bias[:, :], k.vec(V_BETA), None, ALU.add).then_inc(bn, 1)
                e.wait_ge(bn, 5)

                def normalise(p):
                    wait(e, a_mm, sim_use(p - 1) + 2 if not (isinstance(p, int) and p == 0) else 0)
                    e.tensor_scalar(xn[:, :], k.zT[:, bass.ds(p * PW, PW)], bn_scale[:, 0:1], bn_bias[:, 0:1],
                                    ALU.mult, ALU.add).then_inc(xn_ready, 1)

                def top_keys(p):
                    wait(e, a_used, sim_use(p) + 2)
                    wait(e, cand_ready, 2 * p)
                    e.sem_inc(settled, 1)
                    for t in range(2):
                        for w in range(2):
                            for h in range(PH):
                                g = (w * PH + h) * NK
                                i = e.max(tops[:, t, w, h, :], sims[:, t, g:g + NK])
                    i.then_inc(tops_ready, 1)
                    wait(e, tops_ready, p + 1)
                    wait(e, topf_ready, p)
                    e.sem_inc(settled, 1)
                    for t in range(2):
                        for w in range(2):
                            for h in range(PH):
                                g = (w * PH + h) * NK
                                i = e.max_index(topi[:, t, w, h, :], tops[:, t, w, h, :], sims[:, t, g:g + NK])
                    i.then_inc(topi_ready, 1)

                def top_sums(p):
                    wait(e, cand_ready, 2 * p + 2)
                    e.sem_inc(settled, 1)
                    for g in range(2 * PH):
                        i = e.max(best[:, g, :], cand[:, g, :, :].rearrange("p a b -> p (a b)"))
                    i.then_inc(best_ready, 1)
                    wait(e, best_ready, p + 1)
                    e.sem_inc(settled, 1)
                    for g in range(2 * PH):
                        i = e.max_index(pos[:, g, :], best[:, g, :], cand[:, g, :, :].rearrange("p a b -> p (a b)"))
                    i.then_inc(pos_ready, 1)
                    wait(e, pos_ready, p + 1)
                    wait(e, rankf_ready, p)
                    flat = pos[:, :, :].rearrange("p a b -> p (a b)")
                    e.tensor_scalar(rank[:, 0, :], flat, 3, None, ALU.logical_shift_right)
                    e.tensor_scalar(rank[:, 1, :], flat, 7, None, ALU.bitwise_and).then_inc(rank_ready, 1)

                def hits(p):
                    wait(e, rankf_ready, p + 1)
                    wait(e, picked, p)
                    for w in range(2):
                        i = e.tensor_tensor(hit[:, w, :, :, :].rearrange("p a b c -> p (a b) c"), across(k.iota_f[:, 0:8], 2 * PK),
                                            along(rankf[:, w, :], 8), ALU.is_equal)
                    i.then_inc(hit_ready, 1)

                def experts(p):
                    wait(e, ex_ready, p)
                    e.tensor_tensor(shifted[:, :, :], best[:, :, :], best[:, :, 0:1].broadcast_to([128, 2 * PH, 8]),
                                    ALU.subtract).then_inc(shifted_ready, 1)
                    wait(e, picked, p + 1)
                    for w in range(2):
                        i = e.tensor_reduce(key[:, w, :], hit[:, w, :, :, :].rearrange("p a b c -> p (a b) c"), AX.X, ALU.add)
                    i.then_inc(key_ready, 1)
                    wait(e, key_ready, p + 1)
                    e.scalar_tensor_tensor(out=expert_i[:, :], in0=key[:, 0, :], scalar=float(NK), in1=key[:, 1, :],
                                           op0=ALU.mult, op1=ALU.add).then_inc(expert_ready, 1)
                    wait(e, expert_ready, p + 1)
                    wait(e, split_ready, p)
                    e.tensor_scalar(split_i[:, 0, :], expert_i[:, :], 127, None, ALU.bitwise_and)
                    e.tensor_scalar(split_i[:, 1, :], expert_i[:, :], 7, None, ALU.logical_shift_right).then_inc(split_i_ready, 1)
                    wait(e, ex_ready, p + 1)
                    e.tensor_reduce(total[:, :], ex[:, :, :], AX.X, ALU.add).then_inc(total_ready, 1)
                    wait(e, total_ready, 2 * p + 1)
                    e.reciprocal(total[:, :], total[:, :]).then_inc(total_ready, 1)
                    wait(e, total_ready, 2 * p + 2)
                    wait(e, turned, p)
                    e.tensor_tensor(share[:, :, :], ex[:, :, :], along(total[:, :], 8), ALU.mult).then_inc(share_ready, 1)

                def low_part(p):
                    wait(e, turned_out, p + 1)
                    wait(e, rows_pool, p)
                    e.tensor_tensor(shareT[:, 1, :], k.bank[TB][:, 256:384], shareT[:, 0, :], ALU.subtract).then_inc(low_share, 1)

                def high_rows(p):
                    wait(e, turned_out, p + 1)
                    wait(e, rows_pool, p)
                    e.tensor_tensor(at_high[:, :, :], high_no[:, :, :], across(highT[:, :], HI), ALU.is_equal).then_inc(at_ready, 1)
                    wait(e, at_ready, p + 1)
                    wait(e, outer_mm, 4 * p)
                    for t in range(2):
                        s = slice(64 * t, 64 * t + 64)
                        i = e.tensor_tensor(rows[s, 0, t, :, :], at_high[s, :, :], across(shareT[s, 0, :], HI), ALU.mult)
                    i.then_inc(rows_dve, 1)

                def one_hot(p, a):
                    wait(e, outer_mm, 4 * (p - 1) + 2 * a + 2)
                    e.tensor_tensor(onehot[:, a, :, :], low_no[:, :, :], across(lowT[:, a * OW:(a + 1) * OW], 128),
                                    ALU.is_equal).then_inc(oh_ready, 1)

                def weigh(p, a):
                    if a == 0:
                        wait(e, a_used, gelu_use(p) + 4)
                        wait(e, out_mm, p)
                    for q in range(2):
                        bank, n = 2 * a + q, a * OW + 32 * q
                        wait(e, outer_mm, 4 * p + bank + 1)
                        for t in range(2):
                            i = e.tensor_tensor(WG[:, :, t * 128 + n:t * 128 + n + 32],
                                                k.bank[O0 + bank].rearrange("p (n t j) -> p t j n", t=2, j=HI)[:, t, :, :],
                                                G[:, :, t * 128 + n:t * 128 + n + 32], ALU.mult)
                        i.then_inc(wg_ready, 1)

                def add(p):
                    wait(e, out_mm, p + 1)
                    e.tensor_tensor(k.xT[:, bass.ds(p * PW, PW)], k.bank[XB][:, 0:PW], k.xT[:, bass.ds(p * PW, PW)],
                                    ALU.add).then_inc(x_done, 1)

                normalise(0)
                top_keys(0)
                normalise(1)
                top_sums(0)
                hits(0)
                experts(0)
                low_part(0)
                e.wait_ge(consts, 2)
                e.wait_ge(rows_zero, 2)

                def body(p):
                    if not last(p):
                        top_keys(p + 1)
                    high_rows(p)
                    one_hot(p, 0)
                    if not (isinstance(p, int) and p == 0):
                        add(p - 1)
                    if not last(p):
                        top_sums(p + 1)
                    one_hot(p, 1)
                    if not last(p):
                        hits(p + 1)
                    weigh(p, 0)
                    if not last(p, 2):
                        normalise(p + 2)
                    if not last(p):
                        experts(p + 1)
                    weigh(p, 1)
                    if not last(p):
                        low_part(p + 1)
                loop(e, body)
                add(PAIRS - 1)


def build(nc, t, out, stages):
    ctx = ExitStack()
    with ctx:
        def sb(name, shape, dt=F32):
            return ctx.enter_context(nc.sbuf_tensor(name, shape, dt))

        k = Kit()
        k.psum = ctx.enter_context(nc.psum_tensor("psum", [128, 8, CW], F32))
        k.bank = [k.psum[:, i, :] for i in range(8)]
        k.xT, k.zT = sb("xT", [128, N]), sb("zT", [128, N])
        k.ident, k.mean, k.centre = sb("ident", [128, 128]), sb("mean", [128, 128]), sb("centre", [128, 128])
        k.iota_i, k.iota_f = sb("iota_i", [128, 128], mybir.dt.int32), sb("iota_f", [128, 128])
        k.eps_ln, k.eps_rms, k.ones_row = sb("eps_ln", [128, 1]), sb("eps_rms", [128, 1]), sb("ones_row", [1, 128])
        k.w0T, k.w1T = sb("w0T", [128, 4, 128]), sb("w1T", [128, 4, 128])
        k.smallT = sb("smallT", [128, 4, 128])
        k.key_inT, k.key_out, k.M = sb("key_inT", [128, NE]), sb("key_out", [128, ET, D]), sb("M", [128, 2 * PH * NK])
        k.w1, k.w2 = sb("w1", [128, E, HID]), sb("w2", [128, E, HT, D])
        k.gate_w, k.gate_b, k.b2 = sb("gate_w", [128, E]), sb("gate_b", [1, E]), sb("b2", [E, D])
        k.A, k.qscale, k.one_minus_mix = sb("A", [128, NS]), sb("qscale", [128, 1]), sb("one_minus_mix", [128, 1])
        k.sq, k.logv, k.rstd = sb("sq", [128, 2, CW]), sb("logv", [128, 2, CW]), sb("rstd", [128, 2, CW])
        k.vec = lambda v: k.smallT[:, 0, v:v + 1]
        k.b1 = k.smallT[:, 0, 32:32 + E * HT]
        k.w_xdtT, k.w_dtT, k.w_bcT = k.smallT[:, 1, 0:DTR], k.smallT[0:DTR, 2, :], k.smallT[:, 3, 0:2 * NS]
        k.stage = 0
        setup(nc, k, t)
        for s in stages:
            k.stage += 1
            s(nc, k)
        k.stage += 1
        store(nc, k, out)


STAGES = [decay_attention, mixture, head_attention, mixture, time_mix_attention, product_keys, state_space, product_keys]


_INS = ['L0_attn_a_x', 'L0_attn_a_Wr', 'L0_attn_a_Wk', 'L0_attn_a_Wv', 'L0_attn_a_Wo', 'L0_attn_a_decay',
        'L0_attn_a_ln_w', 'L0_attn_b_rotation_params', 'L0_attn_b_entangle_params', 'L0_ffn_gate_w',
        'L0_ffn_gate_b', 'L0_ffn_w1', 'L0_ffn_b1', 'L0_ffn_w2', 'L0_ffn_b2', 'L1_attn_a_time_decay',
        'L1_attn_a_time_first', 'L1_attn_a_time_mix', 'L1_attn_a_Wk', 'L1_attn_a_Wv', 'L1_attn_a_Wr',
        'L1_attn_a_Wo', 'L1_attn_b_A_log', 'L1_attn_b_W_xdt', 'L1_attn_b_b_xdt', 'L1_attn_b_W_dt',
        'L1_attn_b_b_dt', 'L1_attn_b_W_B', 'L1_attn_b_b_B', 'L1_attn_b_W_C', 'L1_attn_b_b_C', 'L1_attn_b_D',
        'L1_ffn_gamma', 'L1_ffn_beta', 'L1_ffn_w_q', 'L1_ffn_keys', 'L1_ffn_key_in', 'L1_ffn_key_out']


def kernel(**inputs):
    import numpy as _np
    import concourse.bacc as _bacc
    from concourse import mybir as _mybir
    from concourse.bass_utils import run_bass_kernel_spmd as _run

    nc = _bacc.Bacc("TRN2", target_bir_lowering=False, num_devices=1)
    arrays, args = {}, {}
    for name in _INS:
        a = _np.ascontiguousarray(inputs[name])
        arrays[f"in_{name}_dram"] = a
        args[name] = nc.dram_tensor(f"in_{name}_dram", a.shape, _mybir.dt.from_np(a.dtype), kind="ExternalInput").ap()
    out = nc.dram_tensor("out_0_dram", (B, T, D), _mybir.dt.float32, kind="ExternalOutput").ap()
    build(nc, args, out, STAGES)
    r = _run(nc, [arrays], core_ids=[0])
    return r.results[0]["out_0_dram"]
```

```python
import concourse.bass as bass
from concourse import mybir
from contextlib import ExitStack

F32 = mybir.dt.float32
F32R = mybir.dt.float32r
BF16 = mybir.dt.bfloat16
F16 = mybir.dt.float16
U32 = mybir.dt.uint32
ALU = mybir.AluOpType
ACT = mybir.ActivationFunctionType
AX = mybir.AxisListType

B, T, D = 8, 256, 128
N = B * T
NT = N // 128
CW = 512
NC = N // CW
BPC = CW // T
HEADS, HD = 16, 8
E, HID, TOPE = 8, 256, 2
HT = HID // 128
NS, DTR = 16, 64
PH, NK = 8, 32
TOPK = 8
NE = NK * NK
ET = NE // 128
LN_EPS, RMS_EPS, BN_EPS = 1e-5, 1e-6, 1e-5

W_STEP, W_ROWS = 32, 96
SPLITS = 7

(V_ROT, V_ENT, V_MIX, V_BDT, V_D, V_GAMMA, V_BETA, V_BXDT, V_BBC) = range(9)


def chunk(c, w=CW):
    return slice(c * w, (c + 1) * w)


def along(a, n):
    return a.unsqueeze(len(a.shape)).broadcast_to([*a.shape, n])


def across(a, n):
    return a.unsqueeze(len(a.shape) - 1).broadcast_to([*a.shape[:-1], n, a.shape[-1]])


class Norm:

    def __init__(self, k, sem, name):
        self.k = k
        self.centred_ready = sem(name + "_centred_ready")
        self.square_ready = sem(name + "_square_ready")
        self.var_ready = sem(name + "_var_ready")
        self.log_ready = sem(name + "_log_ready")
        self.rstd_ready = sem(name + "_rstd_ready")
        self.z_ready = sem(name + "_z_ready")

    def pe(self, e):
        k = self.k

        def centre(c):
            if c >= 2:
                e.wait_ge(self.z_ready, c - 1)
            e.matmul(k.bank[c % 2][:, :], k.centre[:, :], k.xT[:, chunk(c)],
                     start=True, stop=True).then_inc(self.centred_ready, 1)

        def var(c):
            e.wait_ge(self.square_ready, c + 1)
            if c >= 2:
                e.wait_ge(self.log_ready, c - 1)
            e.matmul(k.bank[2 + c % 2][:, :], k.mean[:, :], k.sq[:, c % 2, :],
                     start=True, stop=True).then_inc(self.var_ready, 1)

        centre(0)
        for c in range(NC):
            if c + 1 < NC:
                centre(c + 1)
            var(c)

    def act(self, e):
        k = self.k
        e.preload_act_table_set("natural_log_exp_and_others")

        def square(c):
            e.wait_ge(self.centred_ready, c + 1)
            if c >= 2:
                e.wait_ge(self.var_ready, c - 1)
            e.activation(k.sq[:, c % 2, :], k.bank[c % 2][:, :], ACT.Square).then_inc(self.square_ready, 1)

        square(0)
        for c in range(NC):
            if c + 1 < NC:
                square(c + 1)
            e.wait_ge(self.var_ready, c + 1)
            e.activation(k.logv[:, c % 2, :], k.bank[2 + c % 2][:, :], ACT.Ln,
                         bias=k.eps_ln[:, 0:1]).then_inc(self.log_ready, 1)
            e.wait_ge(self.log_ready, c + 1)
            if c >= 2:
                e.wait_ge(self.z_ready, c - 1)
            e.activation(k.rstd[:, c % 2, :], k.logv[:, c % 2, :], ACT.Exp,
                         scale=-0.5).then_inc(self.rstd_ready, 1)

    def dve_chunk(self, e, c):
        k = self.k
        e.wait_ge(self.rstd_ready, c + 1)
        e.tensor_tensor(k.zT[:, chunk(c)], k.bank[c % 2][:, :], k.rstd[:, c % 2, :],
                        ALU.mult).then_inc(self.z_ready, 1)

    def dve(self, e):
        for c in range(NC):
            self.dve_chunk(e, c)


CUT = 12


def high_part(e, dst, src):
    return e.tensor_scalar(dst.bitcast(U32), src.bitcast(U32), CUT, CUT, ALU.logical_shift_right, ALU.logical_shift_left)


def product(e, out, w, x, start=True, stop=True):
    pairs = ((0, 0), (0, 1), (1, 0))
    for i, (a, b) in enumerate(pairs):
        mm = e.matmul(out, w[a], x[b], start=start and i == 0, stop=stop and i == len(pairs) - 1)
    return mm


class Kit:
    pass


def phase(nc, k):
    ctx = ExitStack()
    made = ctx.enter_context
    sems = []

    def clear():
        nc.clear_and_free_semaphores(sems)
        nc.all_engine_barrier()
    ctx.callback(clear)

    def sb(name, shape, dt=F32):
        return made(nc.sbuf_tensor(f"{name}_{k.stage}", shape, dt))

    def sem(name):
        sems.append(nc.alloc_semaphore(name=f"{name}_{k.stage}"))
        return sems[-1]

    return ctx, sb, sem


class Raw:

    def __init__(self, sb, sem):
        self.w = sb("w_nat", [128, 4, 128])
        self.key_in = sb("key_in_nat", [128, ET, D])
        self.keys = sb("keys_nat", [128, 2, 2, 128])
        self.wq = sb("wq_nat", [128, 2 * PH, D])
        self.small = sb("small_nat", [128, 4, 128])
        self.w1, self.w1cut = sb("w1", [128, E, HID]), sb("w1cut", [128, E, HID])
        self.w2, self.w2cut = sb("w2", [128, E * HT, D]), sb("w2cut", [128, E * HT, D])
        self.by_head = sb("by_head", [128, HEADS])
        self.w_loaded, self.keys_loaded, self.small_loaded = sem("w_loaded"), sem("keys_loaded"), sem("small_loaded")
        self.experts_loaded, self.rest_loaded = sem("experts_loaded"), sem("rest_loaded")


def copy_groups(e, engine, k, groups, which, packed, done):
    for g in which:
        e.wait_ge(packed, g + 1)
        dst = groups[g]
        src = k.bank[g][:, :]
        if len(dst.shape) == 3:
            src = src.rearrange("p (a n) -> p a n", a=dst.shape[1])
        if engine == "scalar":
            e.activation(dst, src, ACT.Copy).then_inc(done, 1)
        else:
            e.tensor_copy(dst, src).then_inc(done, 1)


def setup(nc, k, t, raw):
    ctx, sb, sem = phase(nc, k)
    with ctx:
        xin, w_nat, vec_nat = sb("xin", [128, NT, D]), sb("w0_nat", [128, 4, 128]), sb("vec_nat", [2, 128])
        load_x = [sem(f"load_x{c}") for c in range(NC)]
        load_w, const, small_zero, ones_done = sem("load_w"), sem("const"), sem("small_zero"), sem("ones_done")
        packed, copied, copied_act, fold = sem("packed"), sem("copied"), sem("copied_act"), sem("fold")
        groups = [k.xT[:, chunk(c)] for c in range(NC)] + [k.w0T[:, :, :]]

        with nc.Block() as block:
            @block.sync
            def _(e):
                xr = t["L0_attn_a_x"].rearrange("b (s p) d -> p (b s) d", p=128)
                for c in range(NC):
                    e.dma_start(xin[:, 4 * c:4 * c + 4, :], xr[:, 4 * c:4 * c + 4, :]).then_inc(load_x[c], 16)
                e.dma_start(raw.w1[:, :, :], t["L0_ffn_w1"].rearrange("e c h -> c e h")).then_inc(raw.experts_loaded, 16)
                e.dma_start(raw.w2[:, :, :], t["L0_ffn_w2"].rearrange("e (s p) c -> p (e s) c", p=128)).then_inc(raw.experts_loaded, 16)
                for j, name in enumerate(("L1_attn_a_Wk", "L1_attn_a_Wv", "L1_attn_a_Wr", "L1_attn_a_Wo")):
                    e.dma_start(raw.w[:, j, :], t[name]).then_inc(raw.w_loaded, 16)
                e.dma_start(raw.key_in[:, :, :], t["L1_ffn_key_in"].rearrange("(s p) d -> p s d", p=128)).then_inc(raw.keys_loaded, 16)
                kr = t["L1_ffn_keys"].rearrange("(g h) n p c -> g (h n) p c", g=2)
                for g in range(2):
                    e.dma_start(raw.keys[:, g, :, :], kr[g]).then_inc(raw.keys_loaded, 16)
                e.dma_start(raw.wq[:, :, :], t["L1_ffn_w_q"].rearrange("(s p) d -> p s d", p=128)).then_inc(raw.keys_loaded, 16)
                e.dma_start(k.key_out[:, :, :], t["L1_ffn_key_out"].rearrange("(s p) d -> p s d", p=128)).then_inc(raw.rest_loaded, 16)
                e.dma_start(k.gate_w[:, :], t["L0_ffn_gate_w"]).then_inc(raw.rest_loaded, 16)
                e.dma_start(k.gate_b[:, :], t["L0_ffn_gate_b"].rearrange("(a n) -> a n", a=1)).then_inc(raw.rest_loaded, 16)
                e.dma_start(k.A[:, :], t["L1_attn_b_A_log"]).then_inc(raw.rest_loaded, 16)
                e.wait_ge(small_zero, 1)

                def row(v, lo, n):
                    return raw.small[v:v + 1, 0, lo:lo + n]
                for v, name in ((V_BDT, "L1_attn_b_b_dt"), (V_D, "L1_attn_b_D"), (V_GAMMA, "L1_ffn_gamma"), (V_BETA, "L1_ffn_beta")):
                    e.dma_start(row(v, 0, D), t[name].rearrange("(a n) -> a n", a=1)).then_inc(raw.small_loaded, 16)
                for v, name in ((V_ROT, "L0_attn_b_rotation_params"), (V_ENT, "L0_attn_b_entangle_params")):
                    e.dma_start(row(v, 0, D), t[name].rearrange("(o h) d -> o (h d)", o=1)).then_inc(raw.small_loaded, 16)
                e.dma_start(row(V_MIX, 0, D), t["L1_attn_a_time_mix"].rearrange("a b n -> (a b) n")).then_inc(raw.small_loaded, 16)
                e.dma_start(row(V_BXDT, 0, DTR), t["L1_attn_b_b_xdt"].rearrange("(a n) -> a n", a=1)).then_inc(raw.small_loaded, 16)
                e.dma_start(row(V_BBC, 0, NS), t["L1_attn_b_b_B"].rearrange("(a n) -> a n", a=1)).then_inc(raw.small_loaded, 16)
                e.dma_start(row(V_BBC, NS, NS), t["L1_attn_b_b_C"].rearrange("(a n) -> a n", a=1)).then_inc(raw.small_loaded, 16)
                e.dma_start(raw.small[32:32 + E * HT, 0, :], t["L0_ffn_b1"].rearrange("e (s p) -> (e s) p", p=128)).then_inc(raw.small_loaded, 16)
                e.dma_start(raw.small[0:DTR, 1, :], t["L1_attn_b_W_xdt"]).then_inc(raw.small_loaded, 16)
                e.dma_start(raw.small[:, 2, 0:DTR], t["L1_attn_b_W_dt"]).then_inc(raw.small_loaded, 16)
                e.dma_start(raw.small[0:NS, 3, :], t["L1_attn_b_W_B"]).then_inc(raw.small_loaded, 16)
                e.dma_start(raw.small[NS:2 * NS, 3, :], t["L1_attn_b_W_C"]).then_inc(raw.small_loaded, 16)
                for r, name in ((32, "L1_attn_a_time_first"), (64, "L1_attn_a_time_decay")):
                    e.dma_start(raw.by_head[r:r + 1, :], t[name].rearrange("h a -> a h")).then_inc(raw.small_loaded, 16)
                e.wait_ge(small_zero, 2)
                for s in range(0, W_ROWS, W_STEP):
                    e.dma_start(k.b2[s:s + E, :], t["L0_ffn_b2"]).then_inc(raw.rest_loaded, 16)

            @block.scalar
            def _(e):
                for j, name in enumerate(("L0_attn_a_Wr", "L0_attn_a_Wk", "L0_attn_a_Wv", "L0_attn_a_Wo")):
                    e.dma_start(w_nat[:, j, :], t[name]).then_inc(load_w, 16)
                for r, name in enumerate(("L0_attn_a_decay", "L0_attn_a_ln_w")):
                    e.dma_start(vec_nat[r:r + 1, :], t[name].rearrange("(a n) -> a n", a=1)).then_inc(load_w, 16)
                copy_groups(e, "scalar", k, groups, range(1, len(groups), 2), packed, copied_act)

            @block.gpsimd
            def _(e):
                e.memset(k.ident[:, :], 0.0).then_inc(ones_done, 1)
                e.memset(k.mean[:, :], 1.0 / D).then_inc(ones_done, 1)
                e.wait_ge(ones_done, 2)
                e.affine_select(out=k.ident[:, :], in_=k.ident[:, :], compare_op=ALU.not_equal, fill=1.0,
                                base=0, pattern=[[-1, 128]], channel_multiplier=1).then_inc(const, 1)
                e.memset(raw.small[:, :, :], 0.0).then_inc(small_zero, 1)
                e.memset(k.b2[:, :], 0.0).then_inc(small_zero, 1)
                e.memset(k.eps_ln[:, :], LN_EPS).then_inc(ones_done, 1)
                e.memset(k.eps_rms[:, :], RMS_EPS).then_inc(ones_done, 1)
                e.memset(k.ones_row[:, :], 1.0).then_inc(ones_done, 1)
                e.wait_ge(const, 1)
                e.wait_ge(ones_done, 5)
                e.wait_ge(small_zero, 2)
                e.tensor_tensor(k.centre[:, :], k.ident[:, :], k.mean[:, :], ALU.subtract).then_inc(const, 1)
                e.iota(k.iota_i[:, :], pattern=[[1, 128]], base=0, channel_multiplier=0).then_inc(const, 1)
                e.wait_ge(const, 3)
                e.tensor_copy(k.iota_f[:, :], k.iota_i[:, :]).then_inc(const, 1)
                e.wait_ge(const, 4)

            @block.tensor
            def _(e):
                e.wait_ge(const, 1)
                for c in range(NC):
                    e.wait_ge(load_x[c], 16)
                    for j in range(4):
                        mm = e.transpose(k.bank[c][:, j * 128:(j + 1) * 128], xin[:, 4 * c + j, :], k.ident[:, :])
                    mm.then_inc(packed, 1)
                e.wait_ge(load_w, 16 * 6)
                for j in range(4):
                    mm = e.transpose(k.bank[NC][:, j * 128:(j + 1) * 128], w_nat[:, j, :], k.ident[:, :])
                mm.then_inc(packed, 1)
                e.transpose(k.bank[NC + 1][:, 0:2], vec_nat[:, :], k.ident[0:2, 0:2]).then_inc(packed, 1)

            @block.vector
            def _(e):
                copy_groups(e, "vector", k, groups, range(0, len(groups), 2), packed, copied)
                e.wait_ge(packed, len(groups) + 1)
                e.tensor_copy(k.vec0[:, :], k.bank[NC + 1][:, 0:2]).then_inc(copied, 1)
                e.wait_ge(copied, len(groups[::2]) + 1)
                e.tensor_scalar(k.w0T[:, 3, :], k.w0T[:, 3, :], k.vec0[:, 1:2], None, ALU.mult).then_inc(fold, 1)


def prepare(nc, k, raw):
    ctx, sb, sem = phase(nc, k)
    with ctx:
        keysT = sb("keysT", [128, 2, PH * NK])
        packed, copied, copied_act, fold, spread, multiplied = sem("packed"), sem("copied"), sem("copied_act"), sem("fold"), sem("spread"), sem("multiplied")
        sources = [[raw.keys[:, h, p, :] for p in range(2) for h in range(2)],
                   [raw.w[:, j, :] for j in range(4)],
                   [raw.key_in[:, j, :] for j in range(4)],
                   [raw.key_in[:, 4 + j, :] for j in range(4)],
                   [raw.small[:, j, :] for j in range(4)]]
        groups = [keysT[:, :, :], k.w1T[:, :, :], k.key_inT[:, chunk(0)], k.key_inT[:, chunk(1)], k.smallT[:, :, :]]

        with nc.Block() as block:
            @block.gpsimd
            def _(e):
                e.wait_ge(raw.small_loaded, 16 * 17)
                for r in (32, 64):
                    e.tensor_copy(raw.small[r:r + 1, 3, :].rearrange("o (h d) -> o h d", h=HEADS),
                                  along(raw.by_head[r:r + 1, :], HD)).then_inc(spread, 1)

            @block.tensor
            def _(e):
                e.wait_ge(raw.keys_loaded, 16 * 4)
                e.wait_ge(raw.w_loaded, 16 * 4)
                for g in range(len(groups)):
                    if g == len(groups) - 1:
                        e.wait_ge(spread, 2)
                        e.wait_ge(raw.small_loaded, 16 * 17)
                    for j in range(4):
                        mm = e.transpose(k.bank[g][:, j * 128:(j + 1) * 128], sources[g][j], k.ident[:, :])
                    mm.then_inc(packed, 1)
                e.wait_ge(copied, 1)
                for p in range(2):
                    for h in range(PH):
                        s = p * PH + h
                        mm = e.matmul(k.bank[7][:, s * NK:(s + 1) * NK], raw.wq[:, s, :],
                                      keysT[:, p, h * NK:(h + 1) * NK], start=True, stop=True)
                mm.then_inc(multiplied, 1)

            @block.scalar
            def _(e):
                copy_groups(e, "scalar", k, groups, range(1, len(groups), 2), packed, copied_act)
                e.wait_ge(multiplied, 1)
                e.activation(k.M[:, :], k.bank[7][:, :], ACT.Copy).then_inc(copied_act, 1)

            @block.vector
            def _(e):
                copy_groups(e, "vector", k, groups, range(0, len(groups), 2), packed, copied)
                e.wait_ge(copied, 3)
                e.tensor_scalar(k.qscale[:, :], k.vec(V_ROT), k.vec(V_ENT), float(1.0 / HD ** 0.5),
                                ALU.mult, ALU.mult).then_inc(fold, 1)
                e.tensor_scalar(k.one_minus_mix[:, :], k.vec(V_MIX), -1.0, 1.0, ALU.mult, ALU.add).then_inc(fold, 1)

            @block.sync
            def _(e):
                e.wait_ge(raw.rest_loaded, 16 * 7)


def store(nc, k, out):
    ctx, sb, sem = phase(nc, k)
    with ctx:
        xout = sb("xout", [128, NT, D])
        turned, copied, stored = sem("turned"), sem("copied"), sem("stored")
        outr = out.rearrange("b (s p) d -> p (b s) d", p=128)
        with nc.Block() as block:
            @block.tensor
            def _(e):
                for c in range(NC):
                    for j in range(4):
                        mm = e.transpose(k.bank[c][:, j * 128:(j + 1) * 128],
                                         k.xT[:, (4 * c + j) * 128:(4 * c + j + 1) * 128], k.ident[:, :])
                    mm.then_inc(turned, 1)

            @block.vector
            def _(e):
                for c in range(NC):
                    e.wait_ge(turned, c + 1)
                    e.tensor_copy(xout[:, 4 * c:4 * c + 4, :],
                                  k.bank[c][:, :].rearrange("p (a n) -> p a n", a=4)).then_inc(copied, 1)

            @block.sync
            def _(e):
                for c in range(NC):
                    e.wait_ge(copied, c + 1)
                    e.dma_start(outr[:, 4 * c:4 * c + 4, :], xout[:, 4 * c:4 * c + 4, :]).then_inc(stored, 16)
                e.wait_ge(stored, 16 * NC)


def decay_attention(nc, k, raw):
    ctx, sb, sem = phase(nc, k)
    with ctx:
        ln = Norm(k, sem, "a0")
        dec = sb("dec", [128, 1])
        keep = sb("keep", [128, CW])
        scale = sb("scale", [128, T])
        first = sb("first", [128, T])
        clipm = sb("clipm", [128, CW])
        ksb, sr, y, ysq = sb("ksb", [128, N]), sb("sr", [128, N]), sb("y", [128, N]), sb("ysq", [128, N])
        kv = sb("kv", [128, 2, CW])
        kvm = sb("kvm", [128, 2, CW])
        state = sb("state", [128, 2, CW])
        rst2, yn = sb("rst2", [128, 2, CW]), sb("yn", [128, 2, CW])
        dec_ready, prep, proj, k_ready, r_ready = sem("dec_ready"), sem("prep"), sem("proj"), sem("k_ready"), sem("r_ready")
        kv_ready, step, y_ready, ysq_ready, ms_ready = sem("kv_ready"), sem("step"), sem("y_ready"), sem("ysq_ready"), sem("ms_ready")
        lg_ready, rs_ready, yn_ready, o_ready, x_done = sem("lg_ready"), sem("rs_ready"), sem("yn_ready"), sem("o_ready"), sem("x_done")
        w_cut, w_split = sem("w_cut"), sem("w_split")
        with nc.Block() as block:
            @block.gpsimd
            def _(e):
                e.wait_ge(w_cut, 2)
                for n, (raw_w, cut, high, low) in enumerate(((raw.w1, raw.w1cut, k.w1h, k.w1l), (raw.w2, raw.w2cut, k.w2h, k.w2l))):
                    high, low = (a.rearrange("p e s c -> p (e s) c") if len(a.shape) == 4 else a for a in (high[:], low[:]))
                    e.tensor_copy(high, cut[:, :, :]).then_inc(w_split, 1)
                    e.wait_ge(w_split, 2 * n + 1)
                    e.tensor_tensor(low, raw_w[:, :, :], cut[:, :, :], ALU.subtract).then_inc(w_split, 1)
                    e.wait_ge(w_split, 2 * n + 2)

            @block.tensor
            def _(e):
                ln.pe(e)
                for c in range(NC):
                    e.wait_ge(ln.z_ready, c + 1)
                    if c >= 1:
                        e.wait_ge(r_ready, c)
                        e.wait_ge(kv_ready, c)
                    for j in (1, 2, 0):
                        e.matmul(k.bank[4 + j][:, :], k.w0T[:, j, :], k.zT[:, chunk(c)],
                                 start=True, stop=True).then_inc(proj, 1)
                for c in range(NC):
                    e.wait_ge(ysq_ready, c + 1)
                    if c >= 2:
                        e.wait_ge(lg_ready, c - 1)
                    e.matmul(k.bank[2 + c % 2][:, :], k.mean[:, :], ysq[:, chunk(c)],
                             start=True, stop=True).then_inc(ms_ready, 1)
                for c in range(NC):
                    e.wait_ge(yn_ready, c + 1)
                    if c >= 2:
                        e.wait_ge(x_done, c - 1)
                    e.matmul(k.bank[c % 2][:, :], k.w0T[:, 3, :], yn[:, c % 2, :],
                             start=True, stop=True).then_inc(o_ready, 1)

            @block.scalar
            def _(e):
                ln.act(e)
                e.activation(dec[:, :], k.vec0[:, 0:1], ACT.Sigmoid).then_inc(dec_ready, 1)
                for c in range(NC):
                    e.wait_ge(proj, 3 * c + 1)
                    e.activation(ksb[:, chunk(c)], k.bank[5][:, :], ACT.Copy).then_inc(k_ready, 1)
                    e.wait_ge(proj, 3 * c + 3)
                    e.activation(sr[:, chunk(c)], k.bank[4][:, :], ACT.Sigmoid).then_inc(r_ready, 1)
                for c in range(NC):
                    e.wait_ge(y_ready, c + 1)
                    e.activation(ysq[:, chunk(c)], y[:, chunk(c)], ACT.Square).then_inc(ysq_ready, 1)
                e.preload_act_table_set("natural_log_exp_and_others")
                for c in range(NC):
                    e.wait_ge(ms_ready, c + 1)
                    e.activation(k.logv[:, c % 2, :], k.bank[2 + c % 2][:, :], ACT.Ln,
                                 bias=k.eps_rms[:, 0:1]).then_inc(lg_ready, 1)
                    e.wait_ge(lg_ready, c + 1)
                    if c >= 2:
                        e.wait_ge(yn_ready, c - 1)
                    e.activation(rst2[:, c % 2, :], k.logv[:, c % 2, :], ACT.Exp, scale=-0.5).then_inc(rs_ready, 1)

            @block.vector
            def _(e):
                ln.dve(e)
                e.wait_ge(raw.experts_loaded, 16 * 2)
                high_part(e, raw.w1cut[:, :, :], raw.w1[:, :, :]).then_inc(w_cut, 1)
                high_part(e, raw.w2cut[:, :, :], raw.w2[:, :, :]).then_inc(w_cut, 1)
                e.memset(first[:, :], 0.0).then_inc(prep, 1)
                e.wait_ge(prep, 1)
                e.memset(first[:, 0:1], 1.0).then_inc(prep, 1)
                e.wait_ge(dec_ready, 1)
                e.memset(keep[:, :], 1.0).then_inc(prep, 1)
                e.tensor_scalar(dec[:, :], dec[:, :], 1e-7, None, ALU.max).then_inc(prep, 1)
                e.wait_ge(prep, 4)
                e.tensor_scalar(keep[:, :], keep[:, :], dec[:, 0:1], None, ALU.mult).then_inc(prep, 1)
                e.wait_ge(prep, 5)
                e.tensor_tensor_scan(scale[:, :], keep[:, 0:T], first[:, :], 0.0, ALU.mult, ALU.add).then_inc(prep, 1)
                e.wait_ge(prep, 6)
                for b in range(BPC):
                    e.tensor_scalar(clipm[:, b * T:(b + 1) * T], scale[:, :], 1e10, 1.0, ALU.mult, ALU.min).then_inc(prep, 1)
                    e.memset(keep[:, b * T:b * T + 1], 0.0).then_inc(prep, 1)
                e.wait_ge(prep, 6 + 2 * BPC)
                for c in range(NC):
                    e.wait_ge(proj, 3 * c + 2)
                    e.wait_ge(k_ready, c + 1)
                    e.tensor_tensor(kv[:, c % 2, :], k.bank[6][:, :], ksb[:, chunk(c)], ALU.mult).then_inc(kv_ready, 1)
                    e.wait_ge(kv_ready, c + 1)
                    e.tensor_tensor(kvm[:, c % 2, :], kv[:, c % 2, :], clipm[:, :], ALU.mult).then_inc(step, 1)
                    e.wait_ge(step, 2 * c + 1)
                    e.tensor_tensor_scan(state[:, c % 2, :], keep[:, :], kvm[:, c % 2, :], 0.0,
                                         ALU.mult, ALU.add).then_inc(step, 1)
                    e.wait_ge(step, 2 * c + 2)
                    e.wait_ge(r_ready, c + 1)
                    e.tensor_tensor(y[:, chunk(c)], state[:, c % 2, :], sr[:, chunk(c)], ALU.mult).then_inc(y_ready, 1)
                for c in range(NC + 1):
                    if c < NC:
                        e.wait_ge(rs_ready, c + 1)
                        if c >= 2:
                            e.wait_ge(o_ready, c - 1)
                        e.tensor_tensor(yn[:, c % 2, :], y[:, chunk(c)], rst2[:, c % 2, :], ALU.mult).then_inc(yn_ready, 1)
                    if c >= 1:
                        e.wait_ge(o_ready, c)
                        e.tensor_tensor(k.xT[:, chunk(c - 1)], k.bank[(c - 1) % 2][:, :], k.xT[:, chunk(c - 1)],
                                        ALU.add).then_inc(x_done, 1)




def mixture(nc, k):
    ctx, sb, sem = phase(nc, k)
    with ctx:
        ln = Norm(k, sem, "moe")
        top, shifted, ex = sb("top", [128, NT]), sb("shifted", [128, NT, E]), sb("ex", [128, NT, E])
        total, best = sb("total", [128, NT]), sb("best", [128, NT, 8])
        best_i, best_f = sb("best_i", [128, NT, 8], U32), sb("best_f", [128, NT, 8])
        picked, picked2 = sb("picked", [128, NT, E]), sb("picked2", [128, NT, E])
        wts = sb("wts", [128, NT, E])
        part16 = sb("part16", [128, 2, NT, E], BF16)
        part = sb("part", [128, NT, W_ROWS])
        partT, partT16 = sb("partT", [W_ROWS, N]), sb("partT16", [W_ROWS, N], BF16)
        pick = sb("pick", [W_ROWS, E, 128], BF16)
        zcut, zh, zl = sb("zcut", [128, 2, CW]), sb("zh", [128, N], F32R), sb("zl", [128, N], F32R)
        h, hcut = sb("h", [128, 4, HT, CW]), sb("hcut", [128, 4, HT, CW])
        hh, hl = sb("hh", [128, 4, HT, CW], F32R), sb("hl", [128, 4, HT, CW], F32R)
        zeroed, logits, g, ex_ready, split = sem("zeroed"), sem("logits"), sem("gate_step"), sem("ex_ready"), sem("split")
        turned, turned_act, turned_dve = sem("turned"), sem("turned_act"), sem("turned_dve")
        hidden, h_ready, w_mm, hw_ready = sem("hidden"), sem("h_ready"), sem("w_mm"), sem("hw_ready")
        expert_done, x_done = sem("expert_done"), sem("x_done")
        zcut_ready, hh_ready = sem("zcut_ready"), sem("hh_ready")
        zh_ready, zl_ready, high_ready, low_ready = sem("zh_ready"), sem("zl_ready"), sem("high_ready"), sem("low_ready")
        JT = E * HT
        AHEAD = 3
        W0, SUM = 4, 6

        def wait(e, s, v):
            if not (isinstance(v, int) and v <= 0):
                e.wait_ge(s, v)

        def every_chunk(e, body):
            body(0)
            with e.Fori(1, NC - 1) as c:
                body(c)
            body(NC - 1)

        with nc.Block() as block:
            @block.gpsimd
            def _(e):
                e.memset(part[:, :, :], 0.0).then_inc(zeroed, 1)
                e.wait_ge(zeroed, 1)
                e.memset(pick[:, :, :], 0.0).then_inc(zeroed, 1)
                for s in range(3):
                    e.wait_ge(zeroed, s + 2)
                    e.affine_select(out=pick[:, :, :], in_=pick[:, :, :], compare_op=ALU.not_equal, fill=1.0,
                                    base=-W_STEP * s, pattern=[[-1, E], [0, 128]], channel_multiplier=1)\
                        .then_inc(zeroed, 1)
                e.wait_ge(zeroed, 5)
                for c in range(NC):
                    e.wait_ge(zcut_ready, c + 1)
                    e.tensor_tensor(zl[:, chunk(c)], k.zT[:, chunk(c)], zcut[:, c % 2, :], ALU.subtract).then_inc(zl_ready, 1)

                def body(c):
                    for x in range(E):
                        for s in range(HT):
                            wait(e, high_ready, c * JT + x * HT + s + 1)
                            wait(e, expert_done, c * E + (x - 3))
                            e.tensor_tensor(hl[:, x % 4, s, :], h[:, x % 4, s, :], hcut[:, x % 4, s, :],
                                            ALU.subtract).then_inc(low_ready, 1)
                every_chunk(e, body)

            @block.tensor
            def _(e):
                ln.pe(e)
                for t in range(NT):
                    e.wait_ge(ln.z_ready, t // 4 + 1)
                    e.matmul(k.bank[W0][:, t * E:(t + 1) * E], k.zT[:, t * 128:(t + 1) * 128], k.gate_w[:, :],
                             start=True, stop=False)
                    mm = e.matmul(k.bank[W0][:, t * E:(t + 1) * E], k.ones_row[:, :], k.gate_b[:, :],
                                  start=False, stop=True)
                mm.then_inc(logits, 1)

                def first(c, x):
                    for s in range(HT):
                        j = x * HT + s
                        wait(e, h_ready, c * JT + (j - 3))
                        if isinstance(c, int) and s == 0:
                            e.wait_ge(zh_ready, c + 1)
                            e.wait_ge(zl_ready, c + 1)
                        w = [a[:, x, s * 128:(s + 1) * 128] for a in (k.w1h, k.w1l)]
                        product(e, k.bank[j % 4][:, :], w, [a[:, bass.ds(c * CW, CW)] for a in (zh, zl)]).then_inc(hidden, 1)

                def spread(c, x):
                    wait(e, hw_ready, (c * E + x - 1) * HT)
                    e.matmul(k.bank[W0 + x % 2][:, :], pick[:, x, :], partT16[:, bass.ds(c * CW, CW)],
                             start=True, stop=True).then_inc(w_mm, 1)

                def second(c, x):
                    if x == 0:
                        wait(e, x_done, c)
                        e.matmul(k.bank[SUM][:, :], k.b2[:, :], partT[:, bass.ds(c * CW, CW)], start=True, stop=False)
                    for s in range(HT):
                        wait(e, hh_ready, c * JT + x * HT + s + 1)
                        wait(e, low_ready, c * JT + x * HT + s + 1)
                        mm = product(e, k.bank[SUM][:, :], [a[:, x, s, :] for a in (k.w2h, k.w2l)],
                                     [a[:, x % 4, s, :] for a in (hh, hl)], start=False, stop=(x == E - 1 and s == HT - 1))
                    mm.then_inc(expert_done, 1)

                for x in range(AHEAD):
                    first(0, x)
                e.wait_ge(split, SPLITS)
                for c in range(NC):
                    for q in range(4):
                        mm = e.transpose(k.bank[W0 + c][0:W_ROWS, q * 128:(q + 1) * 128], part[:, 4 * c + q, :], k.ident[:, :])
                    mm.then_inc(turned, 1)
                e.wait_ge(turned_act, NC)
                e.wait_ge(turned_dve, NC)
                e.wait_ge(zeroed, 5)
                spread(0, 0)
                spread(0, 1)

                def body(c):
                    end = isinstance(c, int) and c == NC - 1
                    for x in range(E):
                        if not (end and x + AHEAD >= E):
                            first(c + (x + AHEAD) // E, (x + AHEAD) % E)
                        if not (end and x + 2 >= E):
                            spread(c + (x + 2) // E, (x + 2) % E)
                        second(c, x)
                every_chunk(e, body)

            @block.scalar
            def _(e):
                ln.act(e)

                def relu(c, x):
                    for s in range(HT):
                        j = x * HT + s
                        wait(e, hidden, c * JT + j + 1)
                        wait(e, low_ready, (c * E + x - 3) * HT)
                        e.activation(h[:, x % 4, s, :], k.bank[j % 4][:, :], ACT.Relu,
                                     bias=k.b1[:, j:j + 1]).then_inc(h_ready, 1)

                def round_high(c, x):
                    for s in range(HT):
                        wait(e, high_ready, c * JT + x * HT + s + 1)
                        wait(e, expert_done, c * E + (x - 3))
                        e.activation(hh[:, x % 4, s, :], hcut[:, x % 4, s, :], ACT.Copy).then_inc(hh_ready, 1)

                relu(0, 0)
                e.wait_ge(g, 2)
                e.activation(ex[:, :, :], shifted[:, :, :], ACT.Exp).then_inc(ex_ready, 1)
                relu(0, 1)
                relu(0, 2)
                for c in range(NC):
                    e.wait_ge(turned, c + 1)
                    e.activation(partT16[:, chunk(c)], k.bank[W0 + c][0:W_ROWS, :], ACT.Copy).then_inc(turned_act, 1)

                def body(c):
                    end = isinstance(c, int) and c == NC - 1
                    for x in range(E):
                        round_high(c, x)
                        if not (end and x + AHEAD >= E):
                            relu(c + (x + AHEAD) // E, (x + AHEAD) % E)
                every_chunk(e, body)

            @block.vector
            def _(e):
                for c in range(NC):
                    ln.dve_chunk(e, c)
                    e.wait_ge(ln.z_ready, c + 1)
                    if c >= 2:
                        e.wait_ge(zl_ready, c - 1)
                    high_part(e, zcut[:, c % 2, :], k.zT[:, chunk(c)]).then_inc(zcut_ready, 1)
                    e.wait_ge(zcut_ready, c + 1)
                    e.tensor_copy(zh[:, chunk(c)], zcut[:, c % 2, :]).then_inc(zh_ready, 1)
                e.wait_ge(logits, 1)
                lg = k.bank[W0][:, 0:NT * E].rearrange("p (t x) -> p t x", x=E)
                e.tensor_reduce(top[:, :], lg, AX.X, ALU.max).then_inc(g, 1)
                e.wait_ge(g, 1)
                e.tensor_tensor(shifted[:, :, :], lg, along(top[:, :], E), ALU.subtract).then_inc(g, 1)
                e.wait_ge(ex_ready, 1)
                e.tensor_reduce(total[:, :], ex[:, :, :], AX.X, ALU.add).then_inc(g, 1)
                e.wait_ge(g, 3)
                e.reciprocal(total[:, :], total[:, :]).then_inc(g, 1)
                e.wait_ge(g, 4)
                e.tensor_tensor(ex[:, :, :], ex[:, :, :], along(total[:, :], E), ALU.mult).then_inc(g, 1)
                e.wait_ge(g, 5)
                for t in range(NT):
                    e.max(best[:, t, :], ex[:, t, :]).then_inc(g, 1)
                e.wait_ge(g, 5 + NT)
                for t in range(NT):
                    e.max_index(best_i[:, t, :], best[:, t, :], ex[:, t, :]).then_inc(g, 1)
                n = 5 + 2 * NT
                e.wait_ge(g, n)
                e.tensor_copy(best_f[:, :, :], best_i[:, :, :]).then_inc(g, 1)
                e.wait_ge(g, n + 1)
                number = k.iota_f[:, 0:E].unsqueeze(1).broadcast_to([128, NT, E])
                for r, out_r in ((0, picked), (1, picked2)):
                    e.tensor_tensor(out_r[:, :, :], number, along(best_f[:, :, r], E), ALU.is_equal).then_inc(g, 1)
                e.wait_ge(g, n + 3)
                e.tensor_tensor(picked[:, :, :], picked[:, :, :], picked2[:, :, :], ALU.add).then_inc(g, 1)
                e.wait_ge(g, n + 4)
                e.tensor_tensor(wts[:, :, :], picked[:, :, :], ex[:, :, :], ALU.mult).then_inc(g, 1)
                e.wait_ge(g, n + 5)
                e.wait_ge(zeroed, 1)
                for s in range(3):
                    dst = part[:, :, s * W_STEP:s * W_STEP + E]
                    if s < 2:
                        e.tensor_copy(part16[:, s, :, :], wts[:, :, :]).then_inc(split, 1)
                        e.wait_ge(split, 3 * s + 1)
                        e.tensor_copy(dst, part16[:, s, :, :]).then_inc(split, 1)
                        e.tensor_tensor(wts[:, :, :], wts[:, :, :], part16[:, s, :, :], ALU.subtract).then_inc(split, 1)
                        e.wait_ge(split, 3 * s + 3)
                    else:
                        e.tensor_copy(dst, wts[:, :, :]).then_inc(split, 1)
                for c in range(NC):
                    e.wait_ge(turned_act, c + 1)
                    e.tensor_copy(partT[:, chunk(c)], k.bank[W0 + c][0:W_ROWS, :]).then_inc(turned_dve, 1)

                def add(c):
                    e.wait_ge(expert_done, (c + 1) * E)
                    e.tensor_tensor(k.xT[:, bass.ds(c * CW, CW)], k.bank[SUM][:, :], k.xT[:, bass.ds(c * CW, CW)],
                                    ALU.add).then_inc(x_done, 1)

                def body(c):
                    for x in range(E):
                        wait(e, w_mm, c * E + x + 1)
                        for s in range(HT):
                            wait(e, h_ready, c * JT + x * HT + s + 1)
                            e.tensor_tensor(h[:, x % 4, s, :], k.bank[W0 + x % 2][:, :], h[:, x % 4, s, :],
                                            ALU.mult).then_inc(hw_ready, 1)
                        for s in range(HT):
                            wait(e, hh_ready, (c * E + x - 3) * HT)
                            wait(e, low_ready, (c * E + x - 3) * HT)
                            wait(e, hw_ready, c * JT + x * HT + s + 1)
                            high_part(e, hcut[:, x % 4, s, :], h[:, x % 4, s, :]).then_inc(high_ready, 1)
                        if x == 0 and not (isinstance(c, int) and c == 0):
                            add(c - 1)
                every_chunk(e, body)
                add(NC - 1)


Q_PARTS = (0, 0, 0, 1, 1, 2)
K_PARTS = (0, 1, 2, 0, 1, 0)
QK_ROWS = len(Q_PARTS) * HD
HC = HD + 1
HR = 8 * HC
MAX_ROWS = 3


def per_batch(e, step):
    step(0, 0)
    step(1, 1)
    with e.Fori(1, B // 2 - 1) as i:
        step(2 * i, 0)
        step(2 * i + 1, 1)
    step(B - 2, 0)
    step(B - 1, 1)


def head_attention(nc, k):
    ctx, sb, sem = phase(nc, k)
    with ctx:
        ln = Norm(k, sem, "hd")
        q = sb("q", [128, 2, CW])
        rest = sb("rest", [128, 2, CW])
        parts = sb("parts", [128, 2, 2, 3, CW], BF16)
        kept = nc.dram_tensor("attention_parts", (2, 3, 128, N), BF16, kind="Internal").ap()
        slots = sb("slots", [64, 2, 2, HEADS, T], BF16)
        V = sb("V", [128, NT, HEADS, HD + 1])
        m = sb("m", [128, 2, HEADS])
        negm, nrest = sb("negm", [HEADS, T]), sb("nrest", [HEADS, T])
        mparts = sb("mparts", [HEADS, 2, MAX_ROWS, T], BF16)
        P = sb("P", [128, 2, 2, 2, T])
        Vh = sb("Vh", [128, 2, 2, 2, 8 * (HR + HC)])
        both = sb("both", [HR, 2, T])
        recip, o = sb("recip", [128, 2 * HEADS]), sb("o", [128, 2, D])
        q_ready, hi_ready, rest_ready, mid_ready, lo_ready = sem("q_ready"), sem("hi_ready"), sem("rest_ready"), sem("mid_ready"), sem("lo_ready")
        parts_kept = [sem("parts_kept0"), sem("parts_kept1")]
        slot_loaded = [sem("slot_loaded0"), sem("slot_loaded1")]
        max_loaded = [sem("max_loaded0"), sem("max_loaded1")]
        v_turned, v_ready, ones_set = sem("v_turned"), sem("v_ready"), sem("ones_set")
        s1_ready, max_ready, mt_ready, mstep, mparts_ready = sem("s1_ready"), sem("max_ready"), sem("mt_ready"), sem("mstep"), sem("mparts_ready")
        s2_ready, p_ready, pv_group, pv_ready = sem("s2_ready"), sem("p_ready"), sem("pv_group"), sem("pv_ready")
        vh_zero, vh_ready, both_ready, both_turned = sem("vh_zero"), sem("vh_ready"), sem("both_ready"), sem("both_turned")
        recip_ready, o_ready, o_turned, x_done = sem("recip_ready"), sem("o_ready"), sem("o_turned"), sem("x_done")
        G1, G2 = 16, 8
        LOADS = 2 * len(Q_PARTS)

        def wait(e, s, v):
            if not (isinstance(v, int) and v <= 0):
                e.wait_ge(s, v)

        with nc.Block() as block:
            @block.sync
            def _(e):
                for c in range(NC):
                    e.wait_ge(lo_ready, 2 * (c + 1))
                    for w in range(2):
                        e.dma_start(kept[w, :, :, chunk(c)].rearrange("s p n -> p s n"),
                                    parts[:, c % 2, w, :, :]).then_inc(parts_kept[c % 2], 16)

                def load(b, u):
                    for i in range(len(Q_PARTS)):
                        for w, part in ((0, Q_PARTS[i]), (1, K_PARTS[i])):
                            e.dma_start(slots[i * HD:(i + 1) * HD, u, w, :, :],
                                        kept[w, part, :, bass.ds(b * T, T)].rearrange("(h d) t -> d h t", d=HD))\
                                .then_inc(slot_loaded[u], 16)

                def maxima(b, i, u):
                    wait(e, mparts_ready, b + 1)
                    for s in range(MAX_ROWS):
                        e.dma_start(slots[QK_ROWS + s:QK_ROWS + s + 1, u, 0, :, :],
                                    mparts[:, u, s, :]).then_inc(max_loaded[u], 16)

                e.wait_ge(ones_set, 2)
                for u in range(2):
                    e.wait_ge(parts_kept[u], 2 * 16 * (NC // 2))
                load(0, 0)
                load(1, 1)
                maxima(0, 0, 0)

                def step(b, u):
                    if not (isinstance(b, int) and b + 1 >= B):
                        maxima(b + 1, None, 1 - u)
                    if not (isinstance(b, int) and b + 2 >= B):
                        e.wait_ge(s2_ready, (b + 1) * G2)
                        load(b + 2, u)
                per_batch(e, step)

            @block.gpsimd
            def _(e):
                e.memset(slots[32:64, :, :, :, :], 1.0).then_inc(ones_set, 1)
                e.wait_ge(ones_set, 1)
                e.memset(V[:, :, :, :], 1.0).then_inc(ones_set, 1)
                for c in range(NC):
                    for w in range(2):
                        n = 2 * c + w
                        e.wait_ge(mid_ready, n + 1)
                        e.tensor_tensor(parts[:, c % 2, w, 2, :], rest[:, n % 2, :], parts[:, c % 2, w, 1, :],
                                        ALU.subtract).then_inc(lo_ready, 1)
                e.memset(Vh[:, :, :, :, :], 0.0).then_inc(vh_zero, 1)
                e.wait_ge(vh_zero, 1)
                e.wait_ge(v_ready, NC)

                def step(b, u):
                    wait(e, pv_group, (b - 1) * G2)
                    for j in range(2):
                        e.tensor_copy(Vh[:, u, j, :, :].rearrange("p g (h c) -> p (g h) c", c=HR + HC)[:, :, 0:HC],
                                      V[:, bass.ds(2 * b + j, 1), :, :].rearrange("p a h c -> p (a h) c"))\
                            .then_inc(vh_ready, 1)
                per_batch(e, step)

            @block.scalar
            def _(e):
                ln.act(e)
                for c in range(NC):
                    for w in range(2):
                        n = 2 * c + w
                        src = q[:, c % 2, :] if w == 0 else k.zT[:, chunk(c)]
                        e.wait_ge(q_ready, c + 1)
                        if c >= 2:
                            e.wait_ge(parts_kept[c % 2], 32 * (c // 2))
                        e.activation(parts[:, c % 2, w, 0, :], src, ACT.Copy).then_inc(hi_ready, 1)
                        e.wait_ge(rest_ready, n + 1)
                        e.activation(parts[:, c % 2, w, 1, :], rest[:, n % 2, :], ACT.Copy).then_inc(mid_ready, 1)
                    e.wait_ge(v_turned, c + 1)
                    e.wait_ge(ones_set, 2)
                    e.activation(V[:, 4 * c:4 * c + 4, :, 0:HD].rearrange("p t h d -> p (t h) d"),
                                 k.bank[4 + c % 2].rearrange("p (a d) -> p a d", d=HD), ACT.Copy).then_inc(v_ready, 1)

                def both_out(b):
                    e.wait_ge(pv_group, (b + 1) * G2)
                    wait(e, both_turned, b)
                    e.activation(both[:, :, :], k.bank[6][0:HR, :].rearrange("p (g t) -> p g t", g=2),
                                 ACT.Copy).then_inc(both_ready, 1)

                def step(b, u):
                    for g in range(G2):
                        if g == 1 and not (isinstance(b, int) and b == 0):
                            both_out(b - 1)
                        wait(e, s2_ready, b * G2 + g + 1)
                        wait(e, pv_group, b * G2 + g - 1)
                        e.activation(P[:, g % 2, :, :, :].rearrange("p a j t -> p (a j t)"),
                                     k.psum[:, 2 + 2 * (g % 2):4 + 2 * (g % 2), :].rearrange("p a n -> p (a n)"),
                                     ACT.Exp).then_inc(p_ready, 1)
                per_batch(e, step)
                both_out(B - 1)

            @block.tensor
            def _(e):
                ln.pe(e)
                for c in range(NC):
                    e.wait_ge(ln.z_ready, c + 1)
                    if c >= 2:
                        e.wait_ge(v_ready, c - 1)
                    for j in range(4):
                        mm = e.transpose(k.bank[4 + c % 2][:, j * 128:(j + 1) * 128],
                                         k.zT[:, (4 * c + j) * 128:(4 * c + j + 1) * 128], k.ident[:, :])
                    mm.then_inc(v_turned, 1)
                e.wait_ge(v_ready, NC)

                def scores_for_max(b, u, g):
                    wait(e, max_ready, b * G1 + g - 1)
                    for a in range(2):
                        h = 2 * (g % 8) + a
                        mm = e.matmul(k.bank[g % 2][:, a * T:(a + 1) * T],
                                      slots[0:QK_ROWS, u, 0, h, (g // 8) * 128:(g // 8 + 1) * 128],
                                      slots[0:QK_ROWS, u, 1, h, :], start=True, stop=True)
                    mm.then_inc(s1_ready, 1)

                def turn_max(b):
                    wait(e, max_ready, (b + 1) * G1)
                    wait(e, x_done, b - 1)
                    for s in range(2):
                        mm = e.transpose(k.bank[7][0:HEADS, s * 128:(s + 1) * 128], m[:, s, :], k.ident[:, :])
                    mm.then_inc(mt_ready, 1)

                def scores(b, u, g):
                    if g == 0:
                        e.wait_ge(max_loaded[u], 16 * MAX_ROWS * (b // 2 + 1) if isinstance(b, int) else 8 * MAX_ROWS * (b - u) + 16 * MAX_ROWS)
                    wait(e, p_ready, b * G2 + g - 1)
                    for a in range(2):
                        h = 2 * g + a
                        for j in range(2):
                            mm = e.matmul(k.psum[:, 2 + 2 * (g % 2) + a, j * T:(j + 1) * T],
                                          slots[0:QK_ROWS + MAX_ROWS, u, 1, h, j * 128:(j + 1) * 128],
                                          slots[0:QK_ROWS + MAX_ROWS, u, 0, h, :], start=True, stop=True)
                    mm.then_inc(s2_ready, 1)

                def values(b, u, g):
                    wait(e, p_ready, b * G2 + g + 1)
                    if g == 0:
                        wait(e, both_ready, b)
                        wait(e, vh_ready, 2 * b + 2)
                    for a in range(2):
                        h = 2 * g + a
                        for j in range(2):
                            mm = e.matmul(k.bank[6][0:HR, (h // 8) * T:(h // 8 + 1) * T],
                                          Vh[:, u, j, h // 8, (h % 8) * HR:(h % 8 + 1) * HR],
                                          P[:, g % 2, a, j, :], start=(h % 8 == 0 and j == 0),
                                          stop=(h % 8 == 7 and j == 1))
                    mm.then_inc(pv_group, 1)

                def turn_both(b):
                    wait(e, both_ready, b + 1)
                    wait(e, mstep, (b + 1) * 5 + 1 if not (isinstance(b, int) and b + 1 >= B) else B * 5)
                    wait(e, x_done, b)
                    for i in range(2):
                        for g in range(2):
                            mm = e.transpose(k.bank[7][:, (2 * i + g) * HR:(2 * i + g + 1) * HR],
                                             both[:, g, i * 128:(i + 1) * 128], k.ident[0:HR, 0:HR])
                    mm.then_inc(both_turned, 1)

                def turn_out(b):
                    wait(e, o_ready, b + 1)
                    for i in range(2):
                        mm = e.transpose(k.bank[7][:, i * 128:(i + 1) * 128], o[:, i, :], k.ident[:, :])
                    mm.then_inc(o_turned, 1)

                e.wait_ge(slot_loaded[0], 16 * LOADS)
                for g in range(G1):
                    scores_for_max(0, 0, g)
                turn_max(0)

                def step(b, u):
                    ahead = not (isinstance(b, int) and b + 1 >= B)
                    if ahead:
                        n = b + 1 - (1 - u)
                        e.wait_ge(slot_loaded[1 - u], 8 * LOADS * n + 16 * LOADS)
                    for g in range(G2):
                        if ahead:
                            scores_for_max(b + 1, 1 - u, 2 * g)
                            scores_for_max(b + 1, 1 - u, 2 * g + 1)
                        scores(b, u, g)
                        if g:
                            values(b, u, g - 1)
                        if not (isinstance(b, int) and b == 0):
                            if g == 2:
                                turn_both(b - 1)
                            if g == 4:
                                turn_out(b - 1)
                    if ahead:
                        turn_max(b + 1)
                    values(b, u, G2 - 1)
                per_batch(e, step)
                turn_both(B - 1)
                turn_out(B - 1)

            @block.vector
            def _(e):
                ln.dve(e)
                for c in range(NC):
                    if c >= 2:
                        e.wait_ge(rest_ready, 2 * (c - 2) + 1)
                    e.tensor_scalar(q[:, c % 2, :], k.zT[:, chunk(c)], k.qscale[:, 0:1], None, ALU.mult).then_inc(q_ready, 1)
                    for w in range(2):
                        n = 2 * c + w
                        if w == 0:
                            e.wait_ge(q_ready, c + 1)
                        e.wait_ge(hi_ready, n + 1)
                        if n >= 2:
                            e.wait_ge(lo_ready, n - 1)
                        src = q[:, c % 2, :] if w == 0 else k.zT[:, chunk(c)]
                        e.tensor_tensor(rest[:, n % 2, :], src, parts[:, c % 2, w, 0, :], ALU.subtract).then_inc(rest_ready, 1)

                def maxima(b, u, between):
                    for g in range(G1):
                        e.wait_ge(s1_ready, b * G1 + g + 1)
                        if g == 0:
                            wait(e, mt_ready, b)
                        e.tensor_reduce(m[:, g // 8, 2 * (g % 8):2 * (g % 8) + 2],
                                        k.bank[g % 2].rearrange("p (a t) -> p a t", a=2), AX.X, ALU.max)\
                            .then_inc(max_ready, 1)
                        between(g)
                    e.wait_ge(mt_ready, b + 1)
                    i = 5 * b
                    e.tensor_scalar(negm[:, :], k.bank[7][0:HEADS, 0:T], -1.0, None, ALU.mult).then_inc(mstep, 1)
                    e.wait_ge(mstep, i + 1)
                    if not (isinstance(b, int) and b < 2):
                        n = (b - u) if not isinstance(b, int) else b - u
                        e.wait_ge(max_loaded[u], 8 * MAX_ROWS * n)
                    e.tensor_copy(mparts[:, u, 0, :], negm[:, :]).then_inc(mstep, 1)
                    e.wait_ge(mstep, i + 2)
                    e.tensor_tensor(nrest[:, :], negm[:, :], mparts[:, u, 0, :], ALU.subtract).then_inc(mstep, 1)
                    e.wait_ge(mstep, i + 3)
                    e.tensor_copy(mparts[:, u, 1, :], nrest[:, :]).then_inc(mstep, 1)
                    e.wait_ge(mstep, i + 4)
                    e.tensor_tensor(mparts[:, u, 2, :], nrest[:, :], mparts[:, u, 1, :], ALU.subtract).then_inc(mstep, 1)
                    e.wait_ge(mstep, i + 5)
                    e.sem_inc(mparts_ready, 1)

                def normalise(b):
                    e.wait_ge(both_turned, b + 1)
                    out = k.bank[7][:, 0:2 * HEADS * HC].rearrange("p (a d) -> p a d", d=HC)
                    e.reciprocal(recip[:, :], out[:, :, HD]).then_inc(recip_ready, 1)
                    e.wait_ge(recip_ready, b + 1)
                    wait(e, o_turned, b)
                    e.tensor_tensor(o[:, :, :].rearrange("p i (h d) -> p (i h) d", d=HD), out[:, :, 0:HD],
                                    along(recip[:, :], HD), ALU.mult).then_inc(o_ready, 1)

                def add(b):
                    e.wait_ge(o_turned, b + 1)
                    e.tensor_tensor(k.xT[:, bass.ds(b * T, T)], k.bank[7][:, 0:T], k.xT[:, bass.ds(b * T, T)],
                                    ALU.add).then_inc(x_done, 1)

                maxima(0, 0, lambda g: None)

                def step(b, u):
                    if isinstance(b, int) and b == 0:
                        maxima(1, 1, lambda g: None)
                    elif isinstance(b, int) and b == B - 1:
                        normalise(b - 1)
                        add(b - 1)
                    else:
                        maxima(b + 1, 1 - u, lambda g: normalise(b - 1) if g == 7 else add(b - 1) if g == 11 else None)
                per_batch(e, step)
                normalise(B - 1)
                add(B - 1)


def time_mix_attention(nc, k):
    ctx, sb, sem = phase(nc, k)
    with ctx:
        ln = Norm(k, sem, "a1")
        mixed, xm = sb("mixed", [128, 2, CW]), sb("xm", [128, 2, CW])
        w = sb("w", [128, 1])
        now = sb("now", [128, 1])
        keep = sb("keep", [128, CW])
        kc, gate_r = sb("kc", [128, 2, CW]), sb("gate_r", [128, 2, CW])
        ek, kv = sb("ek", [128, 2, CW]), sb("kv", [128, 2, CW])
        past_k, past_kv = sb("past_k", [128, 2, CW]), sb("past_kv", [128, 2, CW])
        num, den = sb("num", [128, 2, CW]), sb("den", [128, 2, CW])
        xm_ready, mix_ready, proj, kc_ready, ek_ready, gate_ready = sem("xm_ready"), sem("mix_ready"), sem("proj"), sem("kc_ready"), sem("ek_ready"), sem("gate_ready")
        w1_ready, w_ready, prep, step, kv_ready, y_ready, o_ready, x_done = sem("w1_ready"), sem("w_ready"), sem("prep"), sem("step"), sem("kv_ready"), sem("y_ready"), sem("o_ready"), sem("x_done")
        PROJ = 3
        DVE_STEPS = 9

        def batches(a):
            return a.rearrange("p (b t) -> p b t", t=T)

        with nc.Block() as block:
            @block.tensor
            def _(e):
                ln.pe(e)

                def out(c):
                    e.wait_ge(y_ready, c + 1)
                    if c >= 1:
                        e.wait_ge(x_done, c)
                    e.matmul(k.bank[7][:, :], k.w1T[:, 3, :], num[:, c % 2, :], start=True, stop=True).then_inc(o_ready, 1)

                for c in range(NC):
                    e.wait_ge(xm_ready, c + 1)
                    for j in range(PROJ):
                        if c >= 1:
                            e.wait_ge((kc_ready, kv_ready, gate_ready)[j], c)
                        e.matmul(k.bank[4 + j][:, :], k.w1T[:, j, :], xm[:, c % 2, :],
                                 start=True, stop=True).then_inc(proj, 1)
                    if c:
                        out(c - 1)
                out(NC - 1)

            @block.scalar
            def _(e):
                ln.act(e)
                e.activation(w[:, :], k.smallT[:, 3, 64:65], ACT.Exp).then_inc(w1_ready, 1)
                e.activation(now[:, :], k.smallT[:, 3, 32:33], ACT.Exp).then_inc(w1_ready, 1)
                e.wait_ge(w1_ready, 2)
                e.activation(w[:, :], w[:, :], ACT.Exp, scale=-1.0).then_inc(w_ready, 1)

                def weights(c):
                    e.wait_ge(kc_ready, c + 1)
                    if c >= 2:
                        e.wait_ge(step, (c - 2) * DVE_STEPS + DVE_STEPS)
                    e.activation(ek[:, c % 2, :], kc[:, c % 2, :], ACT.Exp).then_inc(ek_ready, 1)

                def gate(c):
                    e.wait_ge(proj, PROJ * c + 3)
                    if c >= 2:
                        e.wait_ge(y_ready, c - 1)
                    e.activation(gate_r[:, c % 2, :], k.bank[6][:, :], ACT.Sigmoid).then_inc(gate_ready, 1)

                for c in range(0, NC, 2):
                    weights(c)
                    gate(c)
                    gate(c + 1)
                    weights(c + 1)

            @block.vector
            def _(e):
                ln.dve(e)
                e.wait_ge(w_ready, 1)
                e.memset(keep[:, :], 1.0).then_inc(prep, 1)
                e.wait_ge(prep, 1)
                e.tensor_scalar(keep[:, :], keep[:, :], w[:, 0:1], None, ALU.mult).then_inc(prep, 1)
                e.wait_ge(prep, 2)
                for b in range(BPC):
                    e.memset(keep[:, b * T:b * T + 1], 0.0).then_inc(prep, 1)
                e.wait_ge(prep, 2 + BPC)

                def mix(c):
                    z, a, o = batches(k.zT[:, chunk(c)]), batches(mixed[:, c % 2, :]), batches(xm[:, c % 2, :])
                    e.wait_ge(ln.z_ready, c + 1)
                    if c >= 2:
                        e.wait_ge(proj, PROJ * (c - 1))
                    e.tensor_scalar(mixed[:, c % 2, :], k.zT[:, chunk(c)], k.vec(V_MIX), None, ALU.mult).then_inc(mix_ready, 1)
                    e.wait_ge(mix_ready, 3 * c + 1)
                    e.tensor_copy(o[:, :, 0:1], a[:, :, 0:1]).then_inc(mix_ready, 1)
                    e.scalar_tensor_tensor(out=o[:, :, 1:T], in0=z[:, :, 0:T - 1], scalar=k.one_minus_mix[:, 0:1],
                                           in1=a[:, :, 1:T], op0=ALU.mult, op1=ALU.add).then_inc(mix_ready, 1)
                    e.wait_ge(mix_ready, 3 * c + 3)
                    e.sem_inc(xm_ready, 1)

                mix(0)
                for c in range(NC):
                    u, s = c % 2, c * DVE_STEPS
                    e.wait_ge(proj, PROJ * c + 1)
                    if c >= 2:
                        e.wait_ge(ek_ready, c - 1)
                    e.tensor_scalar(kc[:, u, :], k.bank[4][:, :], 60.0, None, ALU.min).then_inc(kc_ready, 1)
                    if c + 1 < NC:
                        mix(c + 1)
                    e.wait_ge(ek_ready, c + 1)
                    e.wait_ge(proj, PROJ * c + 2)
                    e.tensor_tensor(kv[:, u, :], k.bank[5][:, :], ek[:, u, :], ALU.mult).then_inc(kv_ready, 1)
                    e.tensor_tensor_scan(past_k[:, u, :], keep[:, :], ek[:, u, :], 0.0, ALU.mult, ALU.add).then_inc(step, 1)
                    e.wait_ge(kv_ready, c + 1)
                    e.tensor_tensor_scan(past_kv[:, u, :], keep[:, :], kv[:, u, :], 0.0, ALU.mult, ALU.add).then_inc(step, 1)
                    if c >= 2:
                        e.wait_ge(o_ready, c - 1)
                    e.wait_ge(step, s + 2)
                    for cur, past, dst in ((ek, past_k, den), (kv, past_kv, num)):
                        a, p, o = batches(cur[:, u, :]), batches(past[:, u, :]), batches(dst[:, u, :])
                        e.tensor_scalar(o[:, :, 0:1], a[:, :, 0:1], now[:, 0:1], None, ALU.mult).then_inc(step, 1)
                        e.scalar_tensor_tensor(out=o[:, :, 1:T], in0=a[:, :, 1:T], scalar=now[:, 0:1],
                                               in1=p[:, :, 0:T - 1], op0=ALU.mult, op1=ALU.add).then_inc(step, 1)
                    e.wait_ge(step, s + 6)
                    e.tensor_scalar(den[:, u, :], den[:, u, :], 1e-16, None, ALU.add).then_inc(step, 1)
                    e.wait_ge(step, s + 7)
                    e.reciprocal(den[:, u, :], den[:, u, :]).then_inc(step, 1)
                    e.wait_ge(gate_ready, c + 1)
                    e.tensor_tensor(num[:, u, :], num[:, u, :], gate_r[:, u, :], ALU.mult).then_inc(step, 1)
                    e.wait_ge(step, s + 9)
                    e.tensor_tensor(num[:, u, :], num[:, u, :], den[:, u, :], ALU.mult).then_inc(y_ready, 1)
                    e.wait_ge(o_ready, c + 1)
                    e.tensor_tensor(k.xT[:, chunk(c)], k.bank[7][:, :], k.xT[:, chunk(c)], ALU.add).then_inc(x_done, 1)


def state_space(nc, k):
    ctx, sb, sem = phase(nc, k)
    with ctx:
        ln = Norm(k, sem, "ss")
        one = sb("one", [128, 1])
        xdt = sb("xdt", [DTR, 2, CW])
        v, neg = sb("v", [128, 2, CW]), sb("neg", [128, 2, CW])
        dt, dtu = sb("dt", [128, N]), sb("dtu", [128, N])
        bc, bc_rest, bc_mid = sb("bc", [2 * NS, 2, CW]), sb("bc_rest", [2 * NS, 2, CW]), sb("bc_mid", [2 * NS, 2, CW], BF16)
        parts = sb("parts", [6 * NS, N], BF16)
        pick = sb("pick", [6 * NS, 2 * NS, 128], BF16)
        Bs, Ab, Bu = sb("Bs", [128, 2, CW]), sb("Ab", [128, 2, CW]), sb("Bu", [128, 2, CW])
        h, hc, a_now = sb("h", [128, 2, CW]), sb("hc", [128, NC, CW]), sb("a_now", [128, 2])
        set_up, picked, A_step = sem("set_up"), sem("picked"), sem("A_step")
        xdt_mm, xdt_ready, dt_mm, bc_mm, v_ready, neg_ready = sem("xdt_mm"), sem("xdt_ready"), sem("dt_mm"), sem("bc_mm"), sem("v_ready"), sem("neg_ready")
        ex_ready, log_ready, dt_ready, dtu_ready = sem("ex_ready"), sem("log_ready"), sem("dt_ready"), sem("dtu_ready")
        bc_ready, hi_ready, rest_ready, mid_ready, parts_ready = sem("bc_ready"), sem("hi_ready"), sem("rest_ready"), sem("mid_ready"), sem("parts_ready")
        b_mm, c_mm, bs_ready, ab_ready, bu_ready = sem("b_mm"), sem("c_mm"), sem("bs_ready"), sem("ab_ready"), sem("bu_ready")
        h_ready, hc_ready, y_mm, zd_ready, x_done, a_now_ready = sem("h_ready"), sem("hc_ready"), sem("y_mm"), sem("zd_ready"), sem("x_done"), sem("a_now_ready")

        def wait(e, s, v):
            if not (isinstance(v, int) and v <= 0):
                e.wait_ge(s, v)

        def every_state(e, step):
            step(0, 0)
            step(1, 1)
            with e.Fori(1, NS // 2 - 1) as i:
                step(2 * i, 0)
                step(2 * i + 1, 1)
            step(NS - 2, 0)
            step(NS - 1, 1)

        with nc.Block() as block:
            @block.gpsimd
            def _(e):
                e.memset(one[:, :], 1.0).then_inc(set_up, 1)
                e.wait_ge(set_up, 1)
                e.memset(pick[:, :, :], 0.0).then_inc(picked, 1)
                for s in range(3):
                    e.wait_ge(picked, s + 1)
                    e.affine_select(out=pick[:, :, :], in_=pick[:, :, :], compare_op=ALU.not_equal, fill=1.0,
                                    base=-2 * NS * s, pattern=[[-1, 2 * NS], [0, 128]], channel_multiplier=1)\
                        .then_inc(picked, 1)
                e.wait_ge(picked, 4)
                e.wait_ge(dtu_ready, NC)

                def state(n, s):
                    for c in range(NC):
                        g = n * NC + c
                        e.wait_ge(bs_ready, g + 1)
                        wait(e, h_ready, g - 1)
                        e.tensor_tensor(Bu[:, c % 2, :], Bs[:, c % 2, :], dtu[:, chunk(c)], ALU.mult).then_inc(bu_ready, 1)
                every_state(e, state)

            @block.tensor
            def _(e):
                ln.pe(e)
                for c in range(NC):
                    e.wait_ge(ln.z_ready, NC)
                    if c >= 2:
                        e.wait_ge(xdt_ready, c - 1)
                    e.matmul(k.bank[c % 2][0:DTR, :], k.w_xdtT, k.zT[:, chunk(c)], start=True, stop=True).then_inc(xdt_mm, 1)
                    if c >= 2:
                        e.wait_ge(bc_ready, c - 1)
                    e.matmul(k.bank[4 + c % 2][0:2 * NS, :], k.w_bcT, k.zT[:, chunk(c)], start=True, stop=True).then_inc(bc_mm, 1)
                    e.wait_ge(xdt_ready, c + 1)
                    if c >= 2:
                        e.wait_ge(v_ready, c - 1)
                    e.matmul(k.bank[2 + c % 2][:, :], k.w_dtT, xdt[:, c % 2, :], start=True, stop=True).then_inc(dt_mm, 1)
                e.wait_ge(parts_ready, NC)
                e.wait_ge(v_ready, NC)
                e.wait_ge(picked, 4)

                def row_of(n):
                    return pick[:, bass.ds(n, 1), :].rearrange("p a m -> p (a m)")

                def spread(n, c):
                    g = n * NC + c
                    wait(e, bs_ready, g - 1)
                    e.matmul(k.bank[c % 2][:, :], row_of(n), parts[:, chunk(c)], start=True, stop=True).then_inc(b_mm, 1)
                    wait(e, hc_ready, g - 1)
                    e.matmul(k.bank[2 + c % 2][:, :], row_of(n + NS), parts[:, chunk(c)], start=True, stop=True).then_inc(c_mm, 1)

                def state(n, s):
                    for c in range(NC):
                        if not (isinstance(n, int) and n == NS - 1 and c >= NC - 2):
                            spread(n + (c + 2) // NC, (c + 2) % NC)
                        e.wait_ge(hc_ready, n * NC + c + 1)
                        e.matmul(k.bank[4 + c][:, :], k.ident[:, :], hc[:, c, :], start=isinstance(n, int) and n == 0,
                                 stop=isinstance(n, int) and n == NS - 1).then_inc(y_mm, 1)
                spread(0, 0)
                spread(0, 1)
                every_state(e, state)

            @block.scalar
            def _(e):
                ln.act(e)
                e.activation(k.A[:, :], k.A[:, :], ACT.Exp).then_inc(A_step, 1)
                e.wait_ge(set_up, 1)
                for c in range(NC):
                    u = c % 2
                    e.wait_ge(xdt_mm, c + 1)
                    if c >= 2:
                        e.wait_ge(dt_mm, c - 1)
                    e.activation(xdt[:, u, :], k.bank[u][0:DTR, :], ACT.Identity, bias=k.vec(V_BXDT)[0:DTR, :]).then_inc(xdt_ready, 1)
                    e.wait_ge(bc_mm, c + 1)
                    if c >= 2:
                        e.wait_ge(parts_ready, c - 1)
                    e.activation(bc[:, u, :], k.bank[4 + u][0:2 * NS, :], ACT.Identity, bias=k.vec(V_BBC)[0:2 * NS, :]).then_inc(bc_ready, 1)
                    e.wait_ge(bc_ready, c + 1)
                    e.activation(parts[0:2 * NS, chunk(c)], bc[:, u, :], ACT.Copy).then_inc(hi_ready, 1)
                    e.wait_ge(rest_ready, c + 1)
                    e.activation(bc_mid[:, u, :], bc_rest[:, u, :], ACT.Copy).then_inc(mid_ready, 1)
                    e.activation(parts[2 * NS:4 * NS, chunk(c)], bc_rest[:, u, :], ACT.Copy).then_inc(mid_ready, 1)
                    e.wait_ge(neg_ready, c + 1)
                    e.activation(neg[:, u, :], neg[:, u, :], ACT.Exp).then_inc(ex_ready, 1)
                    e.wait_ge(ex_ready, c + 1)
                    e.activation(neg[:, u, :], neg[:, u, :], ACT.Ln, bias=one[:, 0:1]).then_inc(log_ready, 1)
                e.wait_ge(A_step, 2)
                e.wait_ge(dtu_ready, NC)

                def state(n, s):
                    wait(e, a_now_ready, n + 1)
                    for c in range(NC):
                        g = n * NC + c
                        e.wait_ge(b_mm, g + 1)
                        wait(e, bu_ready, g - 1)
                        e.activation(Bs[:, c % 2, :], k.bank[c % 2][:, :], ACT.Copy).then_inc(bs_ready, 1)
                        wait(e, h_ready, g - 1)
                        e.activation(Ab[:, c % 2, :], dt[:, chunk(c)], ACT.Exp, scale=a_now[:, s:s + 1]).then_inc(ab_ready, 1)
                every_state(e, state)

            @block.vector
            def _(e):
                ln.dve(e)
                e.wait_ge(A_step, 1)
                e.tensor_scalar(k.A[:, :], k.A[:, :], -1.0, None, ALU.mult).then_inc(A_step, 1)
                for c in range(NC):
                    u = c % 2
                    e.wait_ge(hi_ready, c + 1)
                    e.tensor_tensor(bc_rest[:, u, :], bc[:, u, :], parts[0:2 * NS, chunk(c)], ALU.subtract).then_inc(rest_ready, 1)
                    e.wait_ge(dt_mm, c + 1)
                    if c >= 2:
                        e.wait_ge(dt_ready, c - 1)
                    e.tensor_scalar(v[:, u, :], k.bank[2 + u][:, :], k.vec(V_BDT), None, ALU.add).then_inc(v_ready, 1)
                    e.wait_ge(v_ready, c + 1)
                    e.scalar_tensor_tensor(out=neg[:, u, :], in0=v[:, u, :], scalar=-1.0, in1=v[:, u, :],
                                           op0=ALU.mult, op1=ALU.min).then_inc(neg_ready, 1)
                    e.wait_ge(mid_ready, 2 * c + 2)
                    e.tensor_tensor(parts[4 * NS:6 * NS, chunk(c)], bc_rest[:, u, :], bc_mid[:, u, :],
                                    ALU.subtract).then_inc(parts_ready, 1)
                    e.wait_ge(log_ready, c + 1)
                    e.scalar_tensor_tensor(out=dt[:, chunk(c)], in0=v[:, u, :], scalar=0.0, in1=neg[:, u, :],
                                           op0=ALU.max, op1=ALU.add).then_inc(dt_ready, 1)
                    e.wait_ge(dt_ready, c + 1)
                    e.tensor_tensor(dtu[:, chunk(c)], dt[:, chunk(c)], k.zT[:, chunk(c)], ALU.mult).then_inc(dtu_ready, 1)

                def column(n, s):
                    wait(e, ab_ready, (n - 1) * NC)
                    e.tensor_copy(a_now[:, s:s + 1], k.A[:, bass.ds(n, 1)]).then_inc(a_now_ready, 1)

                def state(n, s):
                    if not (isinstance(n, int) and n == NS - 1):
                        column(n + 1, 1 - s)
                    for c in range(NC):
                        g, u = n * NC + c, c % 2
                        e.wait_ge(ab_ready, g + 1)
                        e.wait_ge(bu_ready, g + 1)
                        wait(e, hc_ready, g - 1)
                        for b in range(BPC):
                            r = slice(b * T, (b + 1) * T)
                            i = e.tensor_tensor_scan(h[:, u, r], Ab[:, u, r], Bu[:, u, r], 0.0, ALU.mult, ALU.add)
                        i.then_inc(h_ready, 1)
                        e.wait_ge(h_ready, g + 1)
                        e.wait_ge(c_mm, g + 1)
                        wait(e, y_mm, g - NC + 1)
                        e.tensor_tensor(hc[:, c, :], k.bank[2 + u][:, :], h[:, u, :], ALU.mult).then_inc(hc_ready, 1)
                column(0, 0)
                every_state(e, state)
                for c in range(NC):
                    e.scalar_tensor_tensor(out=k.zT[:, chunk(c)], in0=k.zT[:, chunk(c)], scalar=k.vec(V_D),
                                           in1=k.xT[:, chunk(c)], op0=ALU.mult, op1=ALU.add).then_inc(zd_ready, 1)
                for c in range(NC):
                    e.wait_ge(zd_ready, c + 1)
                    e.wait_ge(y_mm, (NS - 1) * NC + c + 1)
                    e.tensor_tensor(k.xT[:, chunk(c)], k.bank[4 + c][:, :], k.zT[:, chunk(c)], ALU.add).then_inc(x_done, 1)


PAIRS = NT // 2
PW = 256
PK = PH * TOPK
OW = 64
HI = NE // 128


def product_keys(nc, k):
    ctx, sb, sem = phase(nc, k)
    with ctx:
        ln = Norm(k, sem, "pk")
        stats, mv = sb("stats", [128, NC, 6]), sb("mv", [128, 2])
        bn_scale, bn_bias, bn_log, bn_eps = sb("bn_scale", [128, 1]), sb("bn_bias", [128, 1]), sb("bn_log", [128, 1]), sb("bn_eps", [128, 1])
        low_no, high_no = sb("low_no", [128, 128, OW], F16), sb("high_no", [128, HI, 128], F16)
        xn = sb("xn", [128, PW])
        sims = sb("sims", [128, 2, 2 * PH * NK])
        tops, topi, topf = sb("tops", [128, 2, 2, PH, 8]), sb("topi", [128, 2, 2, PH, 8], U32), sb("topf", [128, 2, 2, PH, 8])
        cand = sb("cand", [128, 2 * PH, 8, 8])
        best, pos = sb("best", [128, 2 * PH, 8]), sb("pos", [128, 2 * PH, 8], U32)
        rank, rankf = sb("rank", [128, 2, 2 * PK], U32), sb("rankf", [128, 2, 2 * PK])
        hit = sb("hit", [128, 2, 2 * PH, 8, 8])
        key = sb("key", [128, 2, 2 * PK])
        expert, expert_i = sb("expert", [128, 2 * PK]), sb("expert_i", [128, 2 * PK], U32)
        split_i, split = sb("split_i", [128, 2, 2 * PK], U32), sb("split", [128, 2, 2 * PK])
        shifted, ex = sb("shifted", [128, 2 * PH, 8]), sb("ex", [128, 2 * PH, 8])
        total, share = sb("total", [128, 2 * PH]), sb("share", [128, 2 * PH, 8])
        lowT, highT = sb("lowT", [128, 128], F16), sb("highT", [128, 128], F16)
        shareT = sb("shareT", [128, 2, 128], F16)
        at_high = sb("at_high", [128, HI, 128], F16)
        rows = sb("rows", [128, 2, 2, HI, 128], F16)
        onehot = sb("onehot", [128, 2, 128, OW], F16)
        G, WG = sb("G", [128, ET, PW]), sb("WG", [128, ET, PW])
        A0, TB, O0, XB = 0, 2, 3, 7
        bn, bn_rstd, consts, rows_zero = sem("bn"), sem("bn_rstd"), sem("consts"), sem("rows_zero")
        xn_ready, a_mm, a_used, tops_ready, topi_ready = sem("xn_ready"), sem("a_mm"), sem("a_used"), sem("tops_ready"), sem("topi_ready")
        cand_ready, topf_ready, best_ready, pos_ready = sem("cand_ready"), sem("topf_ready"), sem("best_ready"), sem("pos_ready")
        rank_ready, rankf_ready, hit_ready, picked, key_ready = sem("rank_ready"), sem("rankf_ready"), sem("hit_ready"), sem("picked"), sem("key_ready")
        expert_ready, expert_i_ready, split_i_ready, split_ready = sem("expert_ready"), sem("expert_i_ready"), sem("split_i_ready"), sem("split_ready")
        shifted_ready, ex_ready, total_ready, share_ready = sem("shifted_ready"), sem("ex_ready"), sem("total_ready"), sem("share_ready")
        turned, turned_out, turned_out_part, low_share, at_ready = sem("turned"), sem("turned_out"), sem("turned_out_part"), sem("low_share"), sem("at_ready")
        rows_dve, rows_pool, oh_ready, outer_mm, wg_ready, out_mm, x_done, settled, folded = sem("rows_dve"), sem("rows_pool"), sem("oh_ready"), sem("outer_mm"), sem("wg_ready"), sem("out_mm"), sem("x_done"), sem("settled"), sem("folded")

        def wait(e, s, v):
            if not (isinstance(v, int) and v <= 0):
                e.wait_ge(s, v)

        def last(p, n=1):
            return isinstance(p, int) and p + n >= PAIRS

        def sim_use(p):
            return 0 if isinstance(p, int) and p == 0 else 6 * p - 4

        def gelu_use(p):
            return 6 * p + 4 - (2 if last(p) else 0)

        def loop(e, body):
            body(0)
            with e.Fori(1, PAIRS - 2) as p:
                body(p)
            body(PAIRS - 2)
            body(PAIRS - 1)

        with nc.Block() as block:
            @block.tensor
            def _(e):
                ln.pe(e)

                def sim(p):
                    wait(e, xn_ready, p + 1)
                    for t in range(2):
                        n = sim_use(p) + t
                        wait(e, a_used, n - 1)
                        e.matmul(k.bank[A0 + t][:, :], xn[:, t * 128:(t + 1) * 128], k.M[:, :],
                                 start=True, stop=True).then_inc(a_mm, 1)

                def activations(p):
                    for t in range(4):
                        wait(e, a_used, gelu_use(p) + t - 1)
                        for j in range(2):
                            mm = e.matmul(k.bank[A0 + t % 2][:, j * PW:(j + 1) * PW],
                                          k.key_inT[:, (2 * t + j) * 128:(2 * t + j + 1) * 128],
                                          k.zT[:, bass.ds(p * PW, PW)], start=True, stop=True)
                        mm.then_inc(a_mm, 1)

                def turn(p):
                    wait(e, split_ready, p + 1)
                    wait(e, share_ready, p + 1)
                    wait(e, turned_out, p)
                    wait(e, low_share, p)
                    for i, src in enumerate((split[:, 0, :], split[:, 1, :], share[:, :, :].rearrange("p a b -> p (a b)"))):
                        mm = e.transpose(k.bank[TB][:, i * 128:(i + 1) * 128], src, k.ident[:, :])
                    mm.then_inc(turned, 1)

                def outer(p, a):
                    wait(e, oh_ready, 2 * p + a + 1)
                    wait(e, rows_dve, p + 1)
                    wait(e, rows_pool, p + 1)
                    for q in range(2):
                        bank = 2 * a + q
                        wait(e, wg_ready, 4 * (p - 1) + bank + 1)
                        for i in range(32):
                            n = q * 32 + i
                            for s in range(2):
                                mm = e.matmul(k.bank[O0 + bank][:, i * 2 * HI:(i + 1) * 2 * HI], onehot[:, a, :, n],
                                              rows[:, s, :, :, a * OW + n], start=(s == 0), stop=(s == 1))
                        mm.then_inc(outer_mm, 1)

                def out(p):
                    wait(e, wg_ready, 4 * p + 4)
                    wait(e, x_done, p)
                    for j in range(ET):
                        mm = e.matmul(k.bank[XB][:, 0:PW], k.key_out[:, j, :], WG[:, j, :], start=(j == 0), stop=(j == ET - 1))
                    mm.then_inc(out_mm, 1)

                e.wait_ge(ln.z_ready, NC)
                sim(0)
                sim(1)
                turn(0)
                activations(0)

                def body(p):
                    if not last(p, 2):
                        sim(p + 2)
                    outer(p, 0)
                    outer(p, 1)
                    if not last(p):
                        turn(p + 1)
                        activations(p + 1)
                    out(p)
                loop(e, body)

            @block.scalar
            def _(e):
                ln.act(e)
                e.wait_ge(rows_zero, 1)
                e.wait_ge(bn, 2)
                e.activation(bn_log[:, :], mv[:, 1:2], ACT.Ln, bias=bn_eps[:, 0:1]).then_inc(bn_rstd, 1)
                e.wait_ge(bn_rstd, 1)
                e.activation(bn_scale[:, :], bn_log[:, :], ACT.Exp, scale=-0.5).then_inc(bn_rstd, 1)

                def sims_out(p):
                    wait(e, topi_ready, p)
                    for t in range(2):
                        wait(e, a_mm, sim_use(p) + t + 1)
                        e.activation(sims[:, t, :], k.bank[A0 + t][:, :], ACT.Copy).then_inc(a_used, 1)

                def gelus(p):
                    wait(e, wg_ready, 4 * p)
                    for t in range(4):
                        wait(e, a_mm, gelu_use(p) + t + 1)
                        e.activation(G[:, 2 * t:2 * t + 2, :], k.bank[A0 + t % 2].rearrange("p (a n) -> p a n", a=2),
                                     ACT.Gelu).then_inc(a_used, 1)

                def first_half(p):
                    wait(e, topi_ready, p + 1)
                    wait(e, picked, p)
                    e.activation(topf[:, :, :, :, :], topi[:, :, :, :, :], ACT.Copy).then_inc(topf_ready, 1)
                    wait(e, rank_ready, p + 1)
                    wait(e, hit_ready, p)
                    e.activation(rankf[:, :, :], rank[:, :, :], ACT.Copy).then_inc(rankf_ready, 1)
                    wait(e, shifted_ready, p + 1)
                    wait(e, share_ready, p)
                    e.activation(ex[:, :, :], shifted[:, :, :], ACT.Exp).then_inc(ex_ready, 1)

                def second_half(p):
                    wait(e, split_i_ready, p + 1)
                    wait(e, turned, p)
                    e.activation(split[:, :, :], split_i[:, :, :], ACT.Copy).then_inc(split_ready, 1)
                    wait(e, turned, p + 1)
                    wait(e, oh_ready, 2 * p)
                    wait(e, rows_dve, p)
                    e.activation(shareT[:, 0, :], k.bank[TB][:, 256:384], ACT.Copy).then_inc(turned_out_part, 1)
                    e.activation(highT[:, :], k.bank[TB][:, 128:256], ACT.Copy).then_inc(turned_out_part, 1)
                    e.activation(lowT[:, :], k.bank[TB][:, 0:128], ACT.Copy).then_inc(turned_out, 1)

                sims_out(0)
                first_half(0)
                second_half(0)
                sims_out(1)
                gelus(0)

                def body(p):
                    if not last(p):
                        first_half(p + 1)
                        if not last(p, 2):
                            sims_out(p + 2)
                        second_half(p + 1)
                        gelus(p + 1)
                loop(e, body)

            @block.gpsimd
            def _(e):
                e.memset(bn_eps[:, :], BN_EPS).then_inc(rows_zero, 1)
                e.wait_ge(rows_zero, 1)
                e.memset(rows[:, :, :, :, :], 0.0).then_inc(rows_zero, 1)
                e.wait_ge(rows_zero, 2)
                e.tensor_copy(low_no[:, :, :], along(k.iota_f[:, :], OW)).then_inc(consts, 1)
                e.wait_ge(consts, 1)
                e.tensor_copy(high_no[:, :, :], along(k.iota_f[:, 0:HI], 128)).then_inc(consts, 1)
                e.wait_ge(consts, 2)

                def sums(p):
                    wait(e, tops_ready, p + 1)
                    wait(e, pos_ready, p)
                    for t in range(2):
                        e.tensor_tensor(cand[:, t * PH:(t + 1) * PH, :, :], along(tops[:, t, 0, :, :], 8),
                                        across(tops[:, t, 1, :, :], 8), ALU.add).then_inc(cand_ready, 1)

                def pick(p):
                    wait(e, topf_ready, p + 1)
                    wait(e, hit_ready, p + 1)
                    wait(e, rows_pool, p)
                    for w in range(2):
                        for t in range(2):
                            i = e.tensor_tensor(hit[:, w, t * PH:(t + 1) * PH, :, :], hit[:, w, t * PH:(t + 1) * PH, :, :],
                                                across(topf[:, t, w, :, :], 8), ALU.mult)
                    i.then_inc(picked, 1)
                    for step, width in enumerate((4, 2, 1)):
                        wait(e, picked if step == 0 else folded, p + 1 if step == 0 else 2 * p + step)
                        if width == 1:
                            wait(e, expert_ready, p)
                        flat = hit[:, :, :, :, :].rearrange("p w a b c -> p (w a b) c")
                        dst = flat[:, :, 0:width] if width > 1 else key[:, :, :].rearrange("p w n -> p (w n)").unsqueeze(2)
                        e.tensor_tensor(dst, flat[:, :, 0:width], flat[:, :, width:2 * width], ALU.add)\
                            .then_inc(folded if width > 1 else key_ready, 1)

                def low_rows(p):
                    wait(e, cand_ready, 2 * PAIRS if last(p) else 2 * p + 4)
                    wait(e, key_ready, p + 1)
                    wait(e, at_ready, p + 1)
                    wait(e, low_share, p + 1)
                    wait(e, outer_mm, 4 * p)
                    for t in range(2):
                        s = slice(64 * t, 64 * t + 64)
                        i = e.tensor_tensor(rows[s, 1, t, :, :], at_high[s, :, :], across(shareT[s, 1, :], HI), ALU.mult)
                    i.then_inc(rows_pool, 1)

                sums(0)
                pick(0)

                def body(p):
                    if not last(p):
                        sums(p + 1)
                    low_rows(p)
                    if not last(p):
                        pick(p + 1)
                loop(e, body)

            @block.vector
            def _(e):
                ln.dve(e)
                e.wait_ge(ln.z_ready, NC)
                for c in range(NC):
                    i = e.bn_stats(stats[:, c, :], k.zT[:, chunk(c)])
                i.then_inc(bn, 1)
                e.wait_ge(bn, 1)
                e.bn_aggr(mv[:, :], stats[:, :, :]).then_inc(bn, 1)
                e.wait_ge(bn_rstd, 2)
                e.tensor_scalar(bn_scale[:, :], bn_scale[:, :], k.vec(V_GAMMA), None, ALU.mult).then_inc(bn, 1)
                e.wait_ge(bn, 3)
                e.tensor_scalar(bn_bias[:, :], mv[:, 0:1], bn_scale[:, 0:1], -1.0, ALU.mult, ALU.mult).then_inc(bn, 1)
                e.wait_ge(bn, 4)
                e.tensor_scalar(bn_bias[:, :], bn_bias[:, :], k.vec(V_BETA), None, ALU.add).then_inc(bn, 1)
                e.wait_ge(bn, 5)

                def normalise(p):
                    wait(e, a_mm, sim_use(p - 1) + 2 if not (isinstance(p, int) and p == 0) else 0)
                    e.tensor_scalar(xn[:, :], k.zT[:, bass.ds(p * PW, PW)], bn_scale[:, 0:1], bn_bias[:, 0:1],
                                    ALU.mult, ALU.add).then_inc(xn_ready, 1)

                def top_keys(p):
                    wait(e, a_used, sim_use(p) + 2)
                    wait(e, cand_ready, 2 * p)
                    e.sem_inc(settled, 1)
                    for t in range(2):
                        for w in range(2):
                            for h in range(PH):
                                g = (w * PH + h) * NK
                                i = e.max(tops[:, t, w, h, :], sims[:, t, g:g + NK])
                    i.then_inc(tops_ready, 1)
                    wait(e, tops_ready, p + 1)
                    wait(e, topf_ready, p)
                    e.sem_inc(settled, 1)
                    for t in range(2):
                        for w in range(2):
                            for h in range(PH):
                                g = (w * PH + h) * NK
                                i = e.max_index(topi[:, t, w, h, :], tops[:, t, w, h, :], sims[:, t, g:g + NK])
                    i.then_inc(topi_ready, 1)

                def top_sums(p):
                    wait(e, cand_ready, 2 * p + 2)
                    e.sem_inc(settled, 1)
                    for g in range(2 * PH):
                        i = e.max(best[:, g, :], cand[:, g, :, :].rearrange("p a b -> p (a b)"))
                    i.then_inc(best_ready, 1)
                    wait(e, best_ready, p + 1)
                    e.sem_inc(settled, 1)
                    for g in range(2 * PH):
                        i = e.max_index(pos[:, g, :], best[:, g, :], cand[:, g, :, :].rearrange("p a b -> p (a b)"))
                    i.then_inc(pos_ready, 1)
                    wait(e, pos_ready, p + 1)
                    wait(e, rankf_ready, p)
                    flat = pos[:, :, :].rearrange("p a b -> p (a b)")
                    e.tensor_scalar(rank[:, 0, :], flat, 3, None, ALU.logical_shift_right)
                    e.tensor_scalar(rank[:, 1, :], flat, 7, None, ALU.bitwise_and).then_inc(rank_ready, 1)
                    wait(e, ex_ready, p)
                    e.tensor_tensor(shifted[:, :, :], best[:, :, :], best[:, :, 0:1].broadcast_to([128, 2 * PH, 8]),
                                    ALU.subtract).then_inc(shifted_ready, 1)

                def hits(p):
                    wait(e, rankf_ready, p + 1)
                    wait(e, key_ready, p)
                    for w in range(2):
                        i = e.tensor_tensor(hit[:, w, :, :, :].rearrange("p a b c -> p (a b) c"), across(k.iota_f[:, 0:8], 2 * PK),
                                            along(rankf[:, w, :], 8), ALU.is_equal)
                    i.then_inc(hit_ready, 1)

                def experts(p):
                    wait(e, key_ready, p + 1)
                    e.scalar_tensor_tensor(out=expert_i[:, :], in0=key[:, 0, :], scalar=float(NK), in1=key[:, 1, :],
                                           op0=ALU.mult, op1=ALU.add).then_inc(expert_ready, 1)
                    wait(e, expert_ready, p + 1)
                    wait(e, split_ready, p)
                    e.tensor_scalar(split_i[:, 0, :], expert_i[:, :], 127, None, ALU.bitwise_and)
                    e.tensor_scalar(split_i[:, 1, :], expert_i[:, :], 7, None, ALU.logical_shift_right).then_inc(split_i_ready, 1)
                    wait(e, ex_ready, p + 1)
                    e.tensor_reduce(total[:, :], ex[:, :, :], AX.X, ALU.add).then_inc(total_ready, 1)
                    wait(e, total_ready, 2 * p + 1)
                    e.reciprocal(total[:, :], total[:, :]).then_inc(total_ready, 1)
                    wait(e, total_ready, 2 * p + 2)
                    wait(e, turned, p)
                    e.tensor_tensor(share[:, :, :], ex[:, :, :], along(total[:, :], 8), ALU.mult).then_inc(share_ready, 1)

                def low_part(p):
                    wait(e, turned_out, p + 1)
                    wait(e, rows_pool, p)
                    e.tensor_tensor(shareT[:, 1, :], k.bank[TB][:, 256:384], shareT[:, 0, :], ALU.subtract).then_inc(low_share, 1)

                def high_rows(p):
                    wait(e, turned_out, p + 1)
                    wait(e, rows_pool, p)
                    e.tensor_tensor(at_high[:, :, :], high_no[:, :, :], across(highT[:, :], HI), ALU.is_equal).then_inc(at_ready, 1)
                    wait(e, at_ready, p + 1)
                    wait(e, outer_mm, 4 * p)
                    for t in range(2):
                        s = slice(64 * t, 64 * t + 64)
                        i = e.tensor_tensor(rows[s, 0, t, :, :], at_high[s, :, :], across(shareT[s, 0, :], HI), ALU.mult)
                    i.then_inc(rows_dve, 1)

                def one_hot(p, a):
                    wait(e, outer_mm, 4 * (p - 1) + 2 * a + 2)
                    e.tensor_tensor(onehot[:, a, :, :], low_no[:, :, :], across(lowT[:, a * OW:(a + 1) * OW], 128),
                                    ALU.is_equal).then_inc(oh_ready, 1)

                def weigh(p, a):
                    if a == 0:
                        wait(e, a_used, gelu_use(p) + 4)
                        wait(e, out_mm, p)
                    for q in range(2):
                        bank, n = 2 * a + q, a * OW + 32 * q
                        wait(e, outer_mm, 4 * p + bank + 1)
                        for t in range(2):
                            i = e.tensor_tensor(WG[:, :, t * 128 + n:t * 128 + n + 32],
                                                k.bank[O0 + bank].rearrange("p (n t j) -> p t j n", t=2, j=HI)[:, t, :, :],
                                                G[:, :, t * 128 + n:t * 128 + n + 32], ALU.mult)
                        i.then_inc(wg_ready, 1)

                def add(p):
                    wait(e, out_mm, p + 1)
                    e.tensor_tensor(k.xT[:, bass.ds(p * PW, PW)], k.bank[XB][:, 0:PW], k.xT[:, bass.ds(p * PW, PW)],
                                    ALU.add).then_inc(x_done, 1)

                normalise(0)
                top_keys(0)
                normalise(1)
                top_sums(0)
                hits(0)
                experts(0)
                e.wait_ge(consts, 2)
                e.wait_ge(rows_zero, 2)

                def body(p):
                    if not last(p):
                        top_keys(p + 1)
                    if not last(p, 2):
                        normalise(p + 2)
                    low_part(p)
                    high_rows(p)
                    if not last(p):
                        top_sums(p + 1)
                    if not (isinstance(p, int) and p == 0):
                        add(p - 1)
                    if not last(p):
                        hits(p + 1)
                    one_hot(p, 0)
                    one_hot(p, 1)
                    weigh(p, 0)
                    if not last(p):
                        experts(p + 1)
                    weigh(p, 1)
                loop(e, body)
                add(PAIRS - 1)


def build(nc, t, out, stages):
    ctx = ExitStack()
    with ctx:
        def sb(name, shape, dt=F32):
            return ctx.enter_context(nc.sbuf_tensor(name, shape, dt))

        k = Kit()
        k.psum = ctx.enter_context(nc.psum_tensor("psum", [128, 8, CW], F32))
        k.bank = [k.psum[:, i, :] for i in range(8)]
        k.xT, k.zT = sb("xT", [128, N]), sb("zT", [128, N])
        k.ident, k.mean, k.centre = sb("ident", [128, 128]), sb("mean", [128, 128]), sb("centre", [128, 128])
        k.iota_i, k.iota_f = sb("iota_i", [128, 128], mybir.dt.int32), sb("iota_f", [128, 128])
        k.eps_ln, k.eps_rms, k.ones_row = sb("eps_ln", [128, 1]), sb("eps_rms", [128, 1]), sb("ones_row", [1, 128])
        k.w0T, k.w1T = sb("w0T", [128, 4, 128]), sb("w1T", [128, 4, 128])
        k.vec0 = sb("vec0", [128, 2])
        k.smallT = sb("smallT", [128, 4, 128])
        k.key_inT, k.key_out, k.M = sb("key_inT", [128, NE]), sb("key_out", [128, ET, D]), sb("M", [128, 2 * PH * NK])
        k.w1h, k.w1l = sb("w1h", [128, E, HID], F32R), sb("w1l", [128, E, HID], F32R)
        k.w2h, k.w2l = sb("w2h", [128, E, HT, D], F32R), sb("w2l", [128, E, HT, D], F32R)
        k.gate_w, k.gate_b, k.b2 = sb("gate_w", [128, E]), sb("gate_b", [1, E]), sb("b2", [W_ROWS, D])
        k.A, k.qscale, k.one_minus_mix = sb("A", [128, NS]), sb("qscale", [128, 1]), sb("one_minus_mix", [128, 1])
        k.sq, k.logv, k.rstd = sb("sq", [128, 2, CW]), sb("logv", [128, 2, CW]), sb("rstd", [128, 2, CW])
        k.vec = lambda v: k.smallT[:, 0, v:v + 1]
        k.b1 = k.smallT[:, 0, 32:32 + E * HT]
        k.w_xdtT, k.w_dtT, k.w_bcT = k.smallT[:, 1, 0:DTR], k.smallT[0:DTR, 2, :], k.smallT[:, 3, 0:2 * NS]
        k.stage = 0
        raw_ctx, raw_sb, raw_sem = phase(nc, k)
        with raw_ctx:
            raw = Raw(raw_sb, raw_sem)
            setup(nc, k, t, raw)
            k.stage = 1
            decay_attention(nc, k, raw)
            k.stage = 2
            prepare(nc, k, raw)
        for s in stages:
            k.stage += 1
            s(nc, k)
        k.stage += 1
        store(nc, k, out)


STAGES = [mixture, head_attention, mixture, time_mix_attention, product_keys, state_space, product_keys]


_INS = ['L0_attn_a_x', 'L0_attn_a_Wr', 'L0_attn_a_Wk', 'L0_attn_a_Wv', 'L0_attn_a_Wo', 'L0_attn_a_decay',
        'L0_attn_a_ln_w', 'L0_attn_b_rotation_params', 'L0_attn_b_entangle_params', 'L0_ffn_gate_w',
        'L0_ffn_gate_b', 'L0_ffn_w1', 'L0_ffn_b1', 'L0_ffn_w2', 'L0_ffn_b2', 'L1_attn_a_time_decay',
        'L1_attn_a_time_first', 'L1_attn_a_time_mix', 'L1_attn_a_Wk', 'L1_attn_a_Wv', 'L1_attn_a_Wr',
        'L1_attn_a_Wo', 'L1_attn_b_A_log', 'L1_attn_b_W_xdt', 'L1_attn_b_b_xdt', 'L1_attn_b_W_dt',
        'L1_attn_b_b_dt', 'L1_attn_b_W_B', 'L1_attn_b_b_B', 'L1_attn_b_W_C', 'L1_attn_b_b_C', 'L1_attn_b_D',
        'L1_ffn_gamma', 'L1_ffn_beta', 'L1_ffn_w_q', 'L1_ffn_keys', 'L1_ffn_key_in', 'L1_ffn_key_out']


def kernel(**inputs):
    import numpy as _np
    import concourse.bacc as _bacc
    from concourse import mybir as _mybir
    from concourse.bass_utils import run_bass_kernel_spmd as _run

    nc = _bacc.Bacc("TRN2", target_bir_lowering=False, num_devices=1)
    arrays, args = {}, {}
    for name in _INS:
        a = _np.ascontiguousarray(inputs[name])
        arrays[f"in_{name}_dram"] = a
        args[name] = nc.dram_tensor(f"in_{name}_dram", a.shape, _mybir.dt.from_np(a.dtype), kind="ExternalInput").ap()
    out = nc.dram_tensor("out_0_dram", (B, T, D), _mybir.dt.float32, kind="ExternalOutput").ap()
    build(nc, args, out, STAGES)
    r = _run(nc, [arrays], core_ids=[0])
    return r.results[0]["out_0_dram"]
```

```python
import concourse.bass as bass
from concourse import mybir
from contextlib import ExitStack

F32 = mybir.dt.float32
F32R = mybir.dt.float32r
BF16 = mybir.dt.bfloat16
F16 = mybir.dt.float16
U32 = mybir.dt.uint32
ALU = mybir.AluOpType
ACT = mybir.ActivationFunctionType
AX = mybir.AxisListType

B, T, D = 8, 256, 128
N = B * T
NT = N // 128
CW = 512
NC = N // CW
BPC = CW // T
HEADS, HD = 16, 8
E, HID, TOPE = 8, 256, 2
HT = HID // 128
NS, DTR = 16, 64
PH, NK = 8, 32
TOPK = 8
NE = NK * NK
ET = NE // 128
LN_EPS, RMS_EPS, BN_EPS = 1e-5, 1e-6, 1e-5

W_STEP, W_ROWS = 32, 96
SPLITS = 7

(V_ROT, V_ENT, V_MIX, V_BDT, V_D, V_GAMMA, V_BETA, V_BXDT, V_BBC) = range(9)


def chunk(c, w=CW):
    return slice(c * w, (c + 1) * w)


def along(a, n):
    return a.unsqueeze(len(a.shape)).broadcast_to([*a.shape, n])


def across(a, n):
    return a.unsqueeze(len(a.shape) - 1).broadcast_to([*a.shape[:-1], n, a.shape[-1]])


class Norm:

    def __init__(self, k, sem, name):
        self.k = k
        self.centred_ready = sem(name + "_centred_ready")
        self.square_ready = sem(name + "_square_ready")
        self.var_ready = sem(name + "_var_ready")
        self.log_ready = sem(name + "_log_ready")
        self.rstd_ready = sem(name + "_rstd_ready")
        self.z_ready = sem(name + "_z_ready")

    def pe(self, e):
        k = self.k

        def centre(c):
            e.matmul(k.bank[c][:, :], k.centre[:, :], k.xT[:, chunk(c)],
                     start=True, stop=True).then_inc(self.centred_ready, 1)

        def var(c):
            e.wait_ge(self.square_ready, c + 1)
            if c >= 2:
                e.wait_ge(self.log_ready, c - 1)
            e.matmul(k.bank[NC + c % 2][:, :], k.mean[:, :], k.sq[:, c % 2, :],
                     start=True, stop=True).then_inc(self.var_ready, 1)

        centre(0)
        centre(1)
        for c in range(NC):
            var(c)
            if c + 2 < NC:
                centre(c + 2)
        e.wait_ge(self.log_ready, NC)

    def act(self, e):
        k = self.k
        e.preload_act_table_set("natural_log_exp_and_others")

        def square(c):
            e.wait_ge(self.centred_ready, c + 1)
            if c >= 2:
                e.wait_ge(self.var_ready, c - 1)
            e.activation(k.sq[:, c % 2, :], k.bank[c][:, :], ACT.Square).then_inc(self.square_ready, 1)

        square(0)
        square(1)
        for c in range(NC):
            e.wait_ge(self.var_ready, c + 1)
            e.activation(k.logv[:, c % 2, :], k.bank[NC + c % 2][:, :], ACT.Ln,
                         bias=k.eps_ln[:, 0:1]).then_inc(self.log_ready, 1)
            if c + 2 < NC:
                square(c + 2)
            e.wait_ge(self.log_ready, c + 1)
            if c >= 2:
                e.wait_ge(self.z_ready, c - 1)
            e.activation(k.rstd[:, c % 2, :], k.logv[:, c % 2, :], ACT.Exp,
                         scale=-0.5).then_inc(self.rstd_ready, 1)

    def dve_chunk(self, e, c):
        k = self.k
        e.wait_ge(self.rstd_ready, c + 1)
        e.tensor_tensor(k.zT[:, chunk(c)], k.bank[c][:, :], k.rstd[:, c % 2, :],
                        ALU.mult).then_inc(self.z_ready, 1)

    def dve(self, e):
        for c in range(NC):
            self.dve_chunk(e, c)


CUT = 12


def high_part(e, dst, src):
    return e.tensor_scalar(dst.bitcast(U32), src.bitcast(U32), CUT, CUT, ALU.logical_shift_right, ALU.logical_shift_left)


def product(e, out, w, x, start=True, stop=True):
    pairs = ((0, 0), (0, 1), (1, 0))
    for i, (a, b) in enumerate(pairs):
        mm = e.matmul(out, w[a], x[b], start=start and i == 0, stop=stop and i == len(pairs) - 1)
    return mm


class Kit:
    pass


def phase(nc, k):
    ctx = ExitStack()
    made = ctx.enter_context
    sems = []

    def clear():
        nc.clear_and_free_semaphores(sems)
        nc.all_engine_barrier()
    ctx.callback(clear)

    def sb(name, shape, dt=F32):
        return made(nc.sbuf_tensor(f"{name}_{k.stage}", shape, dt))

    def sem(name):
        sems.append(nc.alloc_semaphore(name=f"{name}_{k.stage}"))
        return sems[-1]

    return ctx, sb, sem


def load_the_rest(e, t, k, raw):
    e.dma_start(raw.w1[:, :, :], t["L0_ffn_w1"].rearrange("e c h -> c e h")).then_inc(raw.experts_loaded, 16)
    e.dma_start(raw.w2[:, :, :], t["L0_ffn_w2"].rearrange("e (s p) c -> p (e s) c", p=128)).then_inc(raw.experts_loaded, 16)
    for j, name in enumerate(("L1_attn_a_Wk", "L1_attn_a_Wv", "L1_attn_a_Wr", "L1_attn_a_Wo")):
        e.dma_start(raw.w[:, j, :], t[name]).then_inc(raw.w_loaded, 16)
    e.dma_start(raw.key_in[:, :, :], t["L1_ffn_key_in"].rearrange("(s p) d -> p s d", p=128)).then_inc(raw.keys_loaded, 16)
    kr = t["L1_ffn_keys"].rearrange("(g h) n p c -> g (h n) p c", g=2)
    for g in range(2):
        e.dma_start(raw.keys[:, g, :, :], kr[g]).then_inc(raw.keys_loaded, 16)
    e.dma_start(raw.wq[:, :, :], t["L1_ffn_w_q"].rearrange("(s p) d -> p s d", p=128)).then_inc(raw.keys_loaded, 16)
    e.dma_start(k.key_out[:, :, :], t["L1_ffn_key_out"].rearrange("(s p) d -> p s d", p=128)).then_inc(raw.rest_loaded, 16)
    e.dma_start(k.gate_w[:, :], t["L0_ffn_gate_w"]).then_inc(raw.rest_loaded, 16)
    e.dma_start(k.gate_b[:, :], t["L0_ffn_gate_b"].rearrange("(n a) -> n a", a=1)).then_inc(raw.rest_loaded, 16)
    e.dma_start(k.A[:, :], t["L1_attn_b_A_log"]).then_inc(raw.rest_loaded, 16)

    def row(v, lo, n):
        return raw.small[v:v + 1, 0, lo:lo + n]
    for v, name in ((V_BDT, "L1_attn_b_b_dt"), (V_D, "L1_attn_b_D"), (V_GAMMA, "L1_ffn_gamma"), (V_BETA, "L1_ffn_beta")):
        e.dma_start(row(v, 0, D), t[name].rearrange("(a n) -> a n", a=1)).then_inc(raw.small_loaded, 16)
    for v, name in ((V_ROT, "L0_attn_b_rotation_params"), (V_ENT, "L0_attn_b_entangle_params")):
        e.dma_start(row(v, 0, D), t[name].rearrange("(o h) d -> o (h d)", o=1)).then_inc(raw.small_loaded, 16)
    e.dma_start(row(V_MIX, 0, D), t["L1_attn_a_time_mix"].rearrange("a b n -> (a b) n")).then_inc(raw.small_loaded, 16)
    e.dma_start(row(V_BXDT, 0, DTR), t["L1_attn_b_b_xdt"].rearrange("(a n) -> a n", a=1)).then_inc(raw.small_loaded, 16)
    e.dma_start(row(V_BBC, 0, NS), t["L1_attn_b_b_B"].rearrange("(a n) -> a n", a=1)).then_inc(raw.small_loaded, 16)
    e.dma_start(row(V_BBC, NS, NS), t["L1_attn_b_b_C"].rearrange("(a n) -> a n", a=1)).then_inc(raw.small_loaded, 16)
    e.dma_start(raw.small[32:32 + E * HT, 0, :], t["L0_ffn_b1"].rearrange("e (s p) -> (e s) p", p=128)).then_inc(raw.small_loaded, 16)
    e.dma_start(raw.small[0:DTR, 1, :], t["L1_attn_b_W_xdt"]).then_inc(raw.small_loaded, 16)
    e.dma_start(raw.small[:, 2, 0:DTR], t["L1_attn_b_W_dt"]).then_inc(raw.small_loaded, 16)
    e.dma_start(raw.small[0:NS, 3, :], t["L1_attn_b_W_B"]).then_inc(raw.small_loaded, 16)
    e.dma_start(raw.small[NS:2 * NS, 3, :], t["L1_attn_b_W_C"]).then_inc(raw.small_loaded, 16)
    for r, name in ((32, "L1_attn_a_time_first"), (64, "L1_attn_a_time_decay")):
        e.dma_start(raw.by_head[r:r + 1, :], t[name].rearrange("h a -> a h")).then_inc(raw.small_loaded, 16)
    for s in range(0, W_ROWS, W_STEP):
        e.dma_start(k.b2[s:s + E, :], t["L0_ffn_b2"]).then_inc(raw.rest_loaded, 16)


class Raw:

    def __init__(self, sb, sem):
        self.w0, self.vec0 = sb("w0_nat", [128, 4, 128]), sb("vec_nat", [2, 128])
        self.w0_loaded = sem("w0_loaded")
        self.w = sb("w_nat", [128, 4, 128])
        self.key_in = sb("key_in_nat", [128, ET, D])
        self.keys = sb("keys_nat", [128, 2, 2, 128])
        self.wq = sb("wq_nat", [128, 2 * PH, D])
        self.small = sb("small_nat", [128, 4, 128])
        self.w1, self.w1cut = sb("w1", [128, E, HID]), sb("w1cut", [128, E, HID])
        self.w2, self.w2cut = sb("w2", [128, E * HT, D]), sb("w2cut", [128, E * HT, D])
        self.by_head = sb("by_head", [128, HEADS])
        self.w_loaded, self.keys_loaded, self.small_loaded = sem("w_loaded"), sem("keys_loaded"), sem("small_loaded")
        self.experts_loaded, self.rest_loaded = sem("experts_loaded"), sem("rest_loaded")


def copy_groups(e, engine, k, groups, which, packed, done):
    for g in which:
        e.wait_ge(packed, g + 1)
        dst = groups[g]
        src = k.bank[g][:, :]
        if len(dst.shape) == 3:
            src = src.rearrange("p (a n) -> p a n", a=dst.shape[1])
        if engine == "scalar":
            e.activation(dst, src, ACT.Copy).then_inc(done, 1)
        else:
            e.tensor_copy(dst, src).then_inc(done, 1)


def setup(nc, k, t, raw):
    ctx, sb, sem = phase(nc, k)
    with ctx:
        xin = sb("xin", [128, NT, D])
        load_x = [sem(f"load_x{c}") for c in range(NC)]
        const, small_zero, filled = sem("const"), sem("small_zero"), sem("filled")
        packed, copied, copied_act = sem("packed"), sem("copied"), sem("copied_act")
        groups = [k.xT[:, chunk(c)] for c in range(NC)]

        with nc.Block() as block:
            @block.sync
            def _(e):
                xr = t["L0_attn_a_x"].rearrange("b (s p) d -> p (b s) d", p=128)
                for c in range(NC):
                    e.dma_start(xin[:, 4 * c:4 * c + 4, :], xr[:, 4 * c:4 * c + 4, :]).then_inc(load_x[c], 16)

            @block.scalar
            def _(e):
                for j, name in enumerate(("L0_attn_a_Wr", "L0_attn_a_Wk", "L0_attn_a_Wv", "L0_attn_a_Wo")):
                    e.dma_start(raw.w0[:, j, :], t[name]).then_inc(raw.w0_loaded, 16)
                for r, name in enumerate(("L0_attn_a_decay", "L0_attn_a_ln_w")):
                    e.dma_start(raw.vec0[r:r + 1, :], t[name].rearrange("(a n) -> a n", a=1)).then_inc(raw.w0_loaded, 16)
                copy_groups(e, "scalar", k, groups, range(1, len(groups), 2), packed, copied_act)

            @block.gpsimd
            def _(e):
                e.memset(k.ident[:, :], 0.0).then_inc(filled, 1)
                e.memset(k.mean[:, :], 1.0 / D).then_inc(filled, 1)
                e.wait_ge(filled, 2)
                e.affine_select(out=k.ident[:, :], in_=k.ident[:, :], compare_op=ALU.not_equal, fill=1.0,
                                base=0, pattern=[[-1, 128]], channel_multiplier=1).then_inc(const, 1)
                e.memset(raw.small[:, :, :], 0.0).then_inc(small_zero, 1)
                e.memset(k.b2[:, :], 0.0).then_inc(small_zero, 1)
                e.memset(k.eps_ln[:, :], LN_EPS).then_inc(filled, 1)
                e.memset(k.eps_rms[:, :], RMS_EPS).then_inc(filled, 1)
                e.wait_ge(const, 1)
                e.wait_ge(filled, 4)
                e.wait_ge(small_zero, 2)
                e.tensor_tensor(k.centre[:, :], k.ident[:, :], k.mean[:, :], ALU.subtract).then_inc(const, 1)
                e.iota(k.iota_i[:, :], pattern=[[1, 128]], base=0, channel_multiplier=0).then_inc(const, 1)
                e.wait_ge(const, 3)
                e.tensor_copy(k.iota_f[:, :], k.iota_i[:, :]).then_inc(const, 1)
                e.wait_ge(const, 4)

            @block.tensor
            def _(e):
                e.wait_ge(const, 1)
                for c in range(NC):
                    e.wait_ge(load_x[c], 16)
                    for j in range(4):
                        mm = e.transpose(k.bank[c][:, j * 128:(j + 1) * 128], xin[:, 4 * c + j, :], k.ident[:, :])
                    mm.then_inc(packed, 1)

            @block.vector
            def _(e):
                copy_groups(e, "vector", k, groups, range(0, len(groups), 2), packed, copied)


def prepare(nc, k, raw):
    ctx, sb, sem = phase(nc, k)
    with ctx:
        keysT = sb("keysT", [128, 2, PH * NK])
        packed, copied, copied_act, fold, spread, multiplied = sem("packed"), sem("copied"), sem("copied_act"), sem("fold"), sem("spread"), sem("multiplied")
        sources = [[raw.keys[:, h, p, :] for p in range(2) for h in range(2)],
                   [raw.w[:, j, :] for j in range(4)],
                   [raw.key_in[:, j, :] for j in range(4)],
                   [raw.key_in[:, 4 + j, :] for j in range(4)],
                   [raw.small[:, j, :] for j in range(4)]]
        groups = [keysT[:, :, :], k.w1T[:, :, :], k.key_inT[:, chunk(0)], k.key_inT[:, chunk(1)], k.smallT[:, :, :]]

        with nc.Block() as block:
            @block.gpsimd
            def _(e):
                e.wait_ge(raw.small_loaded, 16 * 17)
                for r in (32, 64):
                    e.tensor_copy(raw.small[r:r + 1, 3, :].rearrange("o (h d) -> o h d", h=HEADS),
                                  along(raw.by_head[r:r + 1, :], HD)).then_inc(spread, 1)

            @block.tensor
            def _(e):
                e.wait_ge(raw.keys_loaded, 16 * 4)
                e.wait_ge(raw.w_loaded, 16 * 4)
                for g in range(len(groups)):
                    if g == len(groups) - 1:
                        e.wait_ge(spread, 2)
                        e.wait_ge(raw.small_loaded, 16 * 17)
                    for j in range(4):
                        mm = e.transpose(k.bank[g][:, j * 128:(j + 1) * 128], sources[g][j], k.ident[:, :])
                    mm.then_inc(packed, 1)
                e.wait_ge(copied, 1)
                for p in range(2):
                    for h in range(PH):
                        s = p * PH + h
                        mm = e.matmul(k.bank[7][:, s * NK:(s + 1) * NK], raw.wq[:, s, :],
                                      keysT[:, p, h * NK:(h + 1) * NK], start=True, stop=True)
                mm.then_inc(multiplied, 1)

            @block.scalar
            def _(e):
                copy_groups(e, "scalar", k, groups, range(1, len(groups), 2), packed, copied_act)
                e.wait_ge(multiplied, 1)
                e.activation(k.M[:, :], k.bank[7][:, :], ACT.Copy).then_inc(copied_act, 1)

            @block.vector
            def _(e):
                copy_groups(e, "vector", k, groups, range(0, len(groups), 2), packed, copied)
                e.wait_ge(copied, 3)
                e.tensor_scalar(k.qscale[:, :], k.vec(V_ROT), k.vec(V_ENT), float(1.0 / HD ** 0.5),
                                ALU.mult, ALU.mult).then_inc(fold, 1)
                e.tensor_scalar(k.one_minus_mix[:, :], k.vec(V_MIX), -1.0, 1.0, ALU.mult, ALU.add).then_inc(fold, 1)

            @block.sync
            def _(e):
                e.wait_ge(raw.rest_loaded, 16 * 7)


def store(nc, k, out):
    ctx, sb, sem = phase(nc, k)
    with ctx:
        xout = sb("xout", [128, NT, D])
        turned, copied, stored = sem("turned"), sem("copied"), sem("stored")
        outr = out.rearrange("b (s p) d -> p (b s) d", p=128)
        with nc.Block() as block:
            @block.tensor
            def _(e):
                for c in range(NC):
                    for j in range(4):
                        mm = e.transpose(k.bank[c][:, j * 128:(j + 1) * 128],
                                         k.xT[:, (4 * c + j) * 128:(4 * c + j + 1) * 128], k.ident[:, :])
                    mm.then_inc(turned, 1)

            @block.vector
            def _(e):
                for c in range(NC):
                    e.wait_ge(turned, c + 1)
                    e.tensor_copy(xout[:, 4 * c:4 * c + 4, :],
                                  k.bank[c][:, :].rearrange("p (a n) -> p a n", a=4)).then_inc(copied, 1)

            @block.sync
            def _(e):
                for c in range(NC):
                    e.wait_ge(copied, c + 1)
                    e.dma_start(outr[:, 4 * c:4 * c + 4, :], xout[:, 4 * c:4 * c + 4, :]).then_inc(stored, 16)
                e.wait_ge(stored, 16 * NC)


def decay_attention(nc, k, t, raw):
    ctx, sb, sem = phase(nc, k)
    with ctx:
        ln = Norm(k, sem, "a0")
        dec = sb("dec", [128, 1])
        keep = sb("keep", [128, CW])
        scale = sb("scale", [128, T])
        first = sb("first", [128, T])
        clipm = sb("clipm", [128, CW])
        ksb, sr, y, ysq = sb("ksb", [128, N]), sb("sr", [128, N]), sb("y", [128, N]), sb("ysq", [128, N])
        kv = sb("kv", [128, 2, CW])
        kvm = sb("kvm", [128, 2, CW])
        state = sb("state", [128, 2, CW])
        rst2, yn = sb("rst2", [128, 2, CW]), sb("yn", [128, 2, CW])
        dec_ready, prep, proj, k_ready, r_ready = sem("dec_ready"), sem("prep"), sem("proj"), sem("k_ready"), sem("r_ready")
        kv_ready, step, y_ready, ysq_ready, ms_ready = sem("kv_ready"), sem("step"), sem("y_ready"), sem("ysq_ready"), sem("ms_ready")
        lg_ready, rs_ready, yn_ready, o_ready, x_done = sem("lg_ready"), sem("rs_ready"), sem("yn_ready"), sem("o_ready"), sem("x_done")
        w_cut, w_split, w2_high, w_turned, w_ready = sem("w_cut"), sem("w_split"), sem("w2_high"), sem("w_turned"), sem("w_ready")
        with nc.Block() as block:
            @block.gpsimd
            def _(e):
                e.wait_ge(w_cut, 1)
                e.tensor_copy(k.w1h[:, :, :], raw.w1cut[:, :, :]).then_inc(w_split, 1)
                e.wait_ge(w_split, 1)
                e.tensor_tensor(k.w1l[:, :, :], raw.w1[:, :, :], raw.w1cut[:, :, :], ALU.subtract).then_inc(w_split, 1)
                e.wait_ge(w_cut, 2)
                e.tensor_tensor(k.w2l[:, :, :, :].rearrange("p e s c -> p (e s) c"), raw.w2[:, :, :], raw.w2cut[:, :, :],
                                ALU.subtract).then_inc(w_split, 1)

            @block.sync
            def _(e):
                load_the_rest(e, t, k, raw)

            @block.tensor
            def _(e):
                ln.pe(e)
                e.wait_ge(raw.w0_loaded, 16 * 6)
                for j in range(4):
                    e.transpose(k.bank[7][:, j * 128:(j + 1) * 128], raw.w0[:, j, :], k.ident[:, :])
                e.transpose(k.bank[6][:, 0:2], raw.vec0[:, :], k.ident[0:2, 0:2]).then_inc(w_turned, 1)
                e.wait_ge(w_ready, 3)
                for c in range(NC):
                    e.wait_ge(ln.z_ready, c + 1)
                    if c >= 1:
                        e.wait_ge(r_ready, c)
                        e.wait_ge(kv_ready, c)
                    for j in (1, 2, 0):
                        e.matmul(k.bank[4 + j][:, :], k.w0T[:, j, :], k.zT[:, chunk(c)],
                                 start=True, stop=True).then_inc(proj, 1)
                for c in range(NC):
                    e.wait_ge(ysq_ready, c + 1)
                    if c >= 2:
                        e.wait_ge(lg_ready, c - 1)
                    e.matmul(k.bank[2 + c % 2][:, :], k.mean[:, :], ysq[:, chunk(c)],
                             start=True, stop=True).then_inc(ms_ready, 1)
                for c in range(NC):
                    e.wait_ge(yn_ready, c + 1)
                    if c >= 2:
                        e.wait_ge(x_done, c - 1)
                    e.matmul(k.bank[c % 2][:, :], k.w0T[:, 3, :], yn[:, c % 2, :],
                             start=True, stop=True).then_inc(o_ready, 1)

            @block.scalar
            def _(e):
                ln.act(e)
                e.wait_ge(w_ready, 1)
                e.activation(dec[:, :], k.vec0[:, 0:1], ACT.Sigmoid).then_inc(dec_ready, 1)
                for c in range(NC):
                    e.wait_ge(proj, 3 * c + 1)
                    e.activation(ksb[:, chunk(c)], k.bank[5][:, :], ACT.Copy).then_inc(k_ready, 1)
                    e.wait_ge(proj, 3 * c + 3)
                    e.activation(sr[:, chunk(c)], k.bank[4][:, :], ACT.Sigmoid).then_inc(r_ready, 1)
                for c in range(NC):
                    e.wait_ge(y_ready, c + 1)
                    e.activation(ysq[:, chunk(c)], y[:, chunk(c)], ACT.Square).then_inc(ysq_ready, 1)
                e.preload_act_table_set("natural_log_exp_and_others")
                for c in range(NC):
                    e.wait_ge(ms_ready, c + 1)
                    e.activation(k.logv[:, c % 2, :], k.bank[2 + c % 2][:, :], ACT.Ln,
                                 bias=k.eps_rms[:, 0:1]).then_inc(lg_ready, 1)
                    e.wait_ge(lg_ready, c + 1)
                    if c >= 2:
                        e.wait_ge(yn_ready, c - 1)
                    e.activation(rst2[:, c % 2, :], k.logv[:, c % 2, :], ACT.Exp, scale=-0.5).then_inc(rs_ready, 1)
                e.wait_ge(w_cut, 2)
                e.activation(k.w2h[:, :, :, :].rearrange("p e s c -> p (e s) c"), raw.w2cut[:, :, :], ACT.Copy).then_inc(w2_high, 1)

            @block.vector
            def _(e):
                ln.dve(e)
                e.wait_ge(w_turned, 1)
                e.tensor_copy(k.vec0[:, :], k.bank[6][:, 0:2]).then_inc(w_ready, 1)
                e.tensor_copy(k.w0T[:, :, :], k.bank[7][:, :].rearrange("p (a n) -> p a n", a=4)).then_inc(w_ready, 1)
                e.wait_ge(w_ready, 2)
                e.tensor_scalar(k.w0T[:, 3, :], k.w0T[:, 3, :], k.vec0[:, 1:2], None, ALU.mult).then_inc(w_ready, 1)
                e.memset(first[:, :], 0.0).then_inc(prep, 1)
                e.wait_ge(prep, 1)
                e.memset(first[:, 0:1], 1.0).then_inc(prep, 1)
                e.wait_ge(dec_ready, 1)
                e.memset(keep[:, :], 1.0).then_inc(prep, 1)
                e.tensor_scalar(dec[:, :], dec[:, :], 1e-7, None, ALU.max).then_inc(prep, 1)
                e.wait_ge(prep, 4)
                e.tensor_scalar(keep[:, :], keep[:, :], dec[:, 0:1], None, ALU.mult).then_inc(prep, 1)
                e.wait_ge(prep, 5)
                e.tensor_tensor_scan(scale[:, :], keep[:, 0:T], first[:, :], 0.0, ALU.mult, ALU.add).then_inc(prep, 1)
                e.wait_ge(prep, 6)
                for b in range(BPC):
                    e.tensor_scalar(clipm[:, b * T:(b + 1) * T], scale[:, :], 1e10, 1.0, ALU.mult, ALU.min).then_inc(prep, 1)
                    e.memset(keep[:, b * T:b * T + 1], 0.0).then_inc(prep, 1)
                e.wait_ge(prep, 6 + 2 * BPC)

                def experts_apart():
                    e.wait_ge(raw.experts_loaded, 16 * 2)
                    high_part(e, raw.w1cut[:, :, :], raw.w1[:, :, :]).then_inc(w_cut, 1)
                    high_part(e, raw.w2cut[:, :, :], raw.w2[:, :, :]).then_inc(w_cut, 1)

                for c in range(NC):
                    e.wait_ge(proj, 3 * c + 2)
                    e.wait_ge(k_ready, c + 1)
                    e.tensor_tensor(kv[:, c % 2, :], k.bank[6][:, :], ksb[:, chunk(c)], ALU.mult).then_inc(kv_ready, 1)
                    e.wait_ge(kv_ready, c + 1)
                    e.tensor_tensor(kvm[:, c % 2, :], kv[:, c % 2, :], clipm[:, :], ALU.mult).then_inc(step, 1)
                    e.wait_ge(step, 2 * c + 1)
                    e.tensor_tensor_scan(state[:, c % 2, :], keep[:, :], kvm[:, c % 2, :], 0.0,
                                         ALU.mult, ALU.add).then_inc(step, 1)
                    e.wait_ge(step, 2 * c + 2)
                    e.wait_ge(r_ready, c + 1)
                    e.tensor_tensor(y[:, chunk(c)], state[:, c % 2, :], sr[:, chunk(c)], ALU.mult).then_inc(y_ready, 1)
                    if c == 0:
                        experts_apart()
                for c in range(NC + 1):
                    if c < NC:
                        e.wait_ge(rs_ready, c + 1)
                        if c >= 2:
                            e.wait_ge(o_ready, c - 1)
                        e.tensor_tensor(yn[:, c % 2, :], y[:, chunk(c)], rst2[:, c % 2, :], ALU.mult).then_inc(yn_ready, 1)
                    if c >= 1:
                        e.wait_ge(o_ready, c)
                        e.tensor_tensor(k.xT[:, chunk(c - 1)], k.bank[(c - 1) % 2][:, :], k.xT[:, chunk(c - 1)],
                                        ALU.add).then_inc(x_done, 1)



def mixture(nc, k):
    ctx, sb, sem = phase(nc, k)
    with ctx:
        ln = Norm(k, sem, "moe")
        top, shifted, ex = sb("top", [128, NT]), sb("shifted", [128, NT, E]), sb("ex", [128, NT, E])
        total, best = sb("total", [128, NT]), sb("best", [128, NT, 8])
        best_i, best_f = sb("best_i", [128, NT, 8], U32), sb("best_f", [128, NT, 8])
        picked, picked2 = sb("picked", [128, NT, E]), sb("picked2", [128, NT, E])
        wts = sb("wts", [128, NT, E])
        part16 = sb("part16", [128, 2, NT, E], BF16)
        part = sb("part", [128, NT, W_ROWS])
        partT, partT16 = sb("partT", [W_ROWS, N]), sb("partT16", [W_ROWS, N], BF16)
        pick = sb("pick", [W_ROWS, E, 128], BF16)
        gate = sb("gate", [E, N])
        gate_mm, gate_out = sem("gate_mm"), sem("gate_out")
        zcut, zh, zl = sb("zcut", [128, 2, CW]), sb("zh", [128, N], F32R), sb("zl", [128, N], F32R)
        h, hcut = sb("h", [128, 4, HT, CW]), sb("hcut", [128, 4, HT, CW])
        hh, hl = sb("hh", [128, 4, HT, CW], F32R), sb("hl", [128, 4, HT, CW], F32R)
        zeroed, logits, g, ex_ready, split = sem("zeroed"), sem("logits"), sem("gate_step"), sem("ex_ready"), sem("split")
        turned, turned_act, turned_dve = sem("turned"), sem("turned_act"), sem("turned_dve")
        hidden, h_ready, w_mm, hw_ready = sem("hidden"), sem("h_ready"), sem("w_mm"), sem("hw_ready")
        expert_done, x_done = sem("expert_done"), sem("x_done")
        zcut_ready, hh_ready = sem("zcut_ready"), sem("hh_ready")
        zh_ready, zl_ready, high_ready, low_ready = sem("zh_ready"), sem("zl_ready"), sem("high_ready"), sem("low_ready")
        JT = E * HT
        AHEAD = 3
        W0, GATE, SUM = 4, 6, 6

        def wait(e, s, v):
            if not (isinstance(v, int) and v <= 0):
                e.wait_ge(s, v)

        def every_chunk(e, body):
            body(0)
            with e.Fori(1, NC - 1) as c:
                body(c)
            body(NC - 1)

        with nc.Block() as block:
            @block.gpsimd
            def _(e):
                e.memset(part[:, :, :], 0.0).then_inc(zeroed, 1)
                e.wait_ge(zeroed, 1)
                e.memset(pick[:, :, :], 0.0).then_inc(zeroed, 1)
                for s in range(3):
                    e.wait_ge(zeroed, s + 2)
                    e.affine_select(out=pick[:, :, :], in_=pick[:, :, :], compare_op=ALU.not_equal, fill=1.0,
                                    base=-W_STEP * s, pattern=[[-1, E], [0, 128]], channel_multiplier=1)\
                        .then_inc(zeroed, 1)
                e.wait_ge(zeroed, 5)
                for c in range(NC):
                    e.wait_ge(zcut_ready, c + 1)
                    e.tensor_tensor(zl[:, chunk(c)], k.zT[:, chunk(c)], zcut[:, c % 2, :], ALU.subtract).then_inc(zl_ready, 1)

                def body(c):
                    for x in range(E):
                        for s in range(HT):
                            wait(e, high_ready, c * JT + x * HT + s + 1)
                            wait(e, expert_done, c * E + (x - 3))
                            e.tensor_tensor(hl[:, x % 4, s, :], h[:, x % 4, s, :], hcut[:, x % 4, s, :],
                                            ALU.subtract).then_inc(low_ready, 1)
                every_chunk(e, body)

            @block.tensor
            def _(e):
                ln.pe(e)
                for c in range(NC):
                    e.wait_ge(ln.z_ready, c + 1)
                    if c >= 2:
                        e.wait_ge(gate_out, c - 1)
                    e.matmul(k.bank[GATE + c % 2][0:E, :], k.gate_w[:, :], k.zT[:, chunk(c)],
                             start=True, stop=True).then_inc(gate_mm, 1)

                def first(c, x):
                    for s in range(HT):
                        j = x * HT + s
                        wait(e, h_ready, c * JT + (j - 3))
                        if isinstance(c, int) and s == 0:
                            e.wait_ge(zh_ready, c + 1)
                            e.wait_ge(zl_ready, c + 1)
                        w = [a[:, x, s * 128:(s + 1) * 128] for a in (k.w1h, k.w1l)]
                        product(e, k.bank[j % 4][:, :], w, [a[:, bass.ds(c * CW, CW)] for a in (zh, zl)]).then_inc(hidden, 1)

                def spread(c, x):
                    wait(e, hw_ready, (c * E + x - 1) * HT)
                    e.matmul(k.bank[W0 + x % 2][:, :], pick[:, x, :], partT16[:, bass.ds(c * CW, CW)],
                             start=True, stop=True).then_inc(w_mm, 1)

                def second(c, x):
                    if x == 0:
                        wait(e, x_done, c)
                        e.matmul(k.bank[SUM][:, :], k.b2[:, :], partT[:, bass.ds(c * CW, CW)], start=True, stop=False)
                    for s in range(HT):
                        wait(e, hh_ready, c * JT + x * HT + s + 1)
                        wait(e, low_ready, c * JT + x * HT + s + 1)
                        mm = product(e, k.bank[SUM][:, :], [a[:, x, s, :] for a in (k.w2h, k.w2l)],
                                     [a[:, x % 4, s, :] for a in (hh, hl)], start=False, stop=(x == E - 1 and s == HT - 1))
                    mm.then_inc(expert_done, 1)

                first(0, 0)
                e.wait_ge(gate_out, NC)
                for t in range(NT):
                    mm = e.transpose(k.bank[W0][:, t * E:(t + 1) * E], gate[:, t * 128:(t + 1) * 128], k.ident[0:E, 0:E])
                mm.then_inc(logits, 1)
                for x in range(1, AHEAD):
                    first(0, x)
                e.wait_ge(split, SPLITS)
                for c in range(NC):
                    for q in range(4):
                        mm = e.transpose(k.bank[W0 + c][0:W_ROWS, q * 128:(q + 1) * 128], part[:, 4 * c + q, :], k.ident[:, :])
                    mm.then_inc(turned, 1)
                e.wait_ge(turned_act, NC)
                e.wait_ge(turned_dve, NC)
                e.wait_ge(zeroed, 5)
                spread(0, 0)
                spread(0, 1)

                def body(c):
                    end = isinstance(c, int) and c == NC - 1
                    for x in range(E):
                        if not (end and x + AHEAD >= E):
                            first(c + (x + AHEAD) // E, (x + AHEAD) % E)
                        if not (end and x + 2 >= E):
                            spread(c + (x + 2) // E, (x + 2) % E)
                        second(c, x)
                every_chunk(e, body)

            @block.scalar
            def _(e):
                ln.act(e)

                def relu(c, x):
                    for s in range(HT):
                        j = x * HT + s
                        wait(e, hidden, c * JT + j + 1)
                        wait(e, low_ready, (c * E + x - 3) * HT)
                        e.activation(h[:, x % 4, s, :], k.bank[j % 4][:, :], ACT.Relu,
                                     bias=k.b1[:, j:j + 1]).then_inc(h_ready, 1)

                def round_high(c, x):
                    for s in range(HT):
                        wait(e, high_ready, c * JT + x * HT + s + 1)
                        wait(e, expert_done, c * E + (x - 3))
                        e.activation(hh[:, x % 4, s, :], hcut[:, x % 4, s, :], ACT.Copy).then_inc(hh_ready, 1)

                for c in range(NC):
                    e.wait_ge(gate_mm, c + 1)
                    e.activation(gate[:, chunk(c)], k.bank[GATE + c % 2][0:E, :], ACT.Identity,
                                 bias=k.gate_b[:, 0:1]).then_inc(gate_out, 1)
                relu(0, 0)
                e.wait_ge(g, 2)
                e.activation(ex[:, :, :], shifted[:, :, :], ACT.Exp).then_inc(ex_ready, 1)
                relu(0, 1)
                relu(0, 2)
                for c in range(NC):
                    e.wait_ge(turned, c + 1)
                    e.activation(partT16[:, chunk(c)], k.bank[W0 + c][0:W_ROWS, :], ACT.Copy).then_inc(turned_act, 1)

                def body(c):
                    end = isinstance(c, int) and c == NC - 1
                    for x in range(E):
                        round_high(c, x)
                        if not (end and x + AHEAD >= E):
                            relu(c + (x + AHEAD) // E, (x + AHEAD) % E)
                every_chunk(e, body)

            @block.vector
            def _(e):
                for c in range(NC):
                    ln.dve_chunk(e, c)
                    e.wait_ge(ln.z_ready, c + 1)
                    if c >= 2:
                        e.wait_ge(zl_ready, c - 1)
                    high_part(e, zcut[:, c % 2, :], k.zT[:, chunk(c)]).then_inc(zcut_ready, 1)
                    e.wait_ge(zcut_ready, c + 1)
                    e.tensor_copy(zh[:, chunk(c)], zcut[:, c % 2, :]).then_inc(zh_ready, 1)
                e.wait_ge(logits, 1)
                lg = k.bank[W0][:, 0:NT * E].rearrange("p (t x) -> p t x", x=E)
                e.tensor_reduce(top[:, :], lg, AX.X, ALU.max).then_inc(g, 1)
                e.wait_ge(g, 1)
                e.tensor_tensor(shifted[:, :, :], lg, along(top[:, :], E), ALU.subtract).then_inc(g, 1)
                e.wait_ge(ex_ready, 1)
                e.tensor_reduce(total[:, :], ex[:, :, :], AX.X, ALU.add).then_inc(g, 1)
                e.wait_ge(g, 3)
                e.reciprocal(total[:, :], total[:, :]).then_inc(g, 1)
                e.wait_ge(g, 4)
                e.tensor_tensor(ex[:, :, :], ex[:, :, :], along(total[:, :], E), ALU.mult).then_inc(g, 1)
                e.wait_ge(g, 5)
                for t in range(NT):
                    e.max(best[:, t, :], ex[:, t, :]).then_inc(g, 1)
                e.wait_ge(g, 5 + NT)
                for t in range(NT):
                    e.max_index(best_i[:, t, :], best[:, t, :], ex[:, t, :]).then_inc(g, 1)
                n = 5 + 2 * NT
                e.wait_ge(g, n)
                e.tensor_copy(best_f[:, :, :], best_i[:, :, :]).then_inc(g, 1)
                e.wait_ge(g, n + 1)
                number = k.iota_f[:, 0:E].unsqueeze(1).broadcast_to([128, NT, E])
                for r, out_r in ((0, picked), (1, picked2)):
                    e.tensor_tensor(out_r[:, :, :], number, along(best_f[:, :, r], E), ALU.is_equal).then_inc(g, 1)
                e.wait_ge(g, n + 3)
                e.tensor_tensor(picked[:, :, :], picked[:, :, :], picked2[:, :, :], ALU.add).then_inc(g, 1)
                e.wait_ge(g, n + 4)
                e.tensor_tensor(wts[:, :, :], picked[:, :, :], ex[:, :, :], ALU.mult).then_inc(g, 1)
                e.wait_ge(g, n + 5)
                e.wait_ge(zeroed, 1)
                for s in range(3):
                    dst = part[:, :, s * W_STEP:s * W_STEP + E]
                    if s < 2:
                        e.tensor_copy(part16[:, s, :, :], wts[:, :, :]).then_inc(split, 1)
                        e.wait_ge(split, 3 * s + 1)
                        e.tensor_copy(dst, part16[:, s, :, :]).then_inc(split, 1)
                        e.tensor_tensor(wts[:, :, :], wts[:, :, :], part16[:, s, :, :], ALU.subtract).then_inc(split, 1)
                        e.wait_ge(split, 3 * s + 3)
                    else:
                        e.tensor_copy(dst, wts[:, :, :]).then_inc(split, 1)
                for c in range(NC):
                    e.wait_ge(turned_act, c + 1)
                    e.tensor_copy(partT[:, chunk(c)], k.bank[W0 + c][0:W_ROWS, :]).then_inc(turned_dve, 1)

                def add(c):
                    e.wait_ge(expert_done, (c + 1) * E)
                    e.tensor_tensor(k.xT[:, bass.ds(c * CW, CW)], k.bank[SUM][:, :], k.xT[:, bass.ds(c * CW, CW)],
                                    ALU.add).then_inc(x_done, 1)

                def body(c):
                    for x in range(E):
                        wait(e, w_mm, c * E + x + 1)
                        for s in range(HT):
                            wait(e, h_ready, c * JT + x * HT + s + 1)
                            e.tensor_tensor(h[:, x % 4, s, :], k.bank[W0 + x % 2][:, :], h[:, x % 4, s, :],
                                            ALU.mult).then_inc(hw_ready, 1)
                        for s in range(HT):
                            wait(e, hh_ready, (c * E + x - 3) * HT)
                            wait(e, low_ready, (c * E + x - 3) * HT)
                            wait(e, hw_ready, c * JT + x * HT + s + 1)
                            high_part(e, hcut[:, x % 4, s, :], h[:, x % 4, s, :]).then_inc(high_ready, 1)
                        if x == 0 and not (isinstance(c, int) and c == 0):
                            add(c - 1)
                every_chunk(e, body)
                add(NC - 1)


Q_PARTS = (0, 0, 0, 1, 1, 2)
K_PARTS = (0, 1, 2, 0, 1, 0)
QK_ROWS = len(Q_PARTS) * HD
HC = HD + 1
HR = 8 * HC
MAX_ROWS = 3


def per_batch(e, step):
    step(0, 0)
    step(1, 1)
    with e.Fori(1, B // 2 - 1) as i:
        step(2 * i, 0)
        step(2 * i + 1, 1)
    step(B - 2, 0)
    step(B - 1, 1)


def head_attention(nc, k):
    ctx, sb, sem = phase(nc, k)
    with ctx:
        ln = Norm(k, sem, "hd")
        q = sb("q", [128, 2, CW])
        rest = sb("rest", [128, 2, CW])
        parts = sb("parts", [128, NC, 2, 3, CW], BF16)
        kept = nc.dram_tensor("attention_parts", (2, 3, 128, N), BF16, kind="Internal").ap()
        slots = sb("slots", [64, 2, 2, HEADS, T], BF16)
        V = sb("V", [128, NT, HEADS, HD + 1])
        m = sb("m", [128, 2, HEADS])
        negm, nrest = sb("negm", [HEADS, T]), sb("nrest", [HEADS, T])
        mparts = sb("mparts", [HEADS, 2, MAX_ROWS, T], BF16)
        P = sb("P", [128, 2, 2, 2, T])
        Vh = sb("Vh", [128, 2, 2, 2, 8 * (HR + HC)])
        both = sb("both", [HR, 2, T])
        recip, o = sb("recip", [128, 2 * HEADS]), sb("o", [128, 2, D])
        q_ready, hi_ready, rest_ready, mid_ready, lo_ready = sem("q_ready"), sem("hi_ready"), sem("rest_ready"), sem("mid_ready"), sem("lo_ready")
        parts_kept = [sem(f"parts_kept{c}") for c in range(NC)]
        slot_loaded = [[sem(f"slot_loaded{u}_{half}") for half in range(2)] for u in range(2)]
        max_loaded = [sem("max_loaded0"), sem("max_loaded1")]
        v_turned, v_ready, ones_set = sem("v_turned"), sem("v_ready"), sem("ones_set")
        s1_ready, max_ready, mt_ready, mstep, mparts_ready = sem("s1_ready"), sem("max_ready"), sem("mt_ready"), sem("mstep"), sem("mparts_ready")
        s2_ready, p_ready, pv_group = sem("s2_ready"), sem("p_ready"), sem("pv_group")
        vh_zero, vh_ready, both_ready, both_turned = sem("vh_zero"), sem("vh_ready"), sem("both_ready"), sem("both_turned")
        recip_ready, o_ready, o_turned, x_done = sem("recip_ready"), sem("o_ready"), sem("o_turned"), sem("x_done")
        G1, G2 = 16, 8
        LOADS = 2 * len(Q_PARTS)
        MAX_GROUPS = (3, 3, 3, 3, 2, 2, 0, 0)

        def wait(e, s, v):
            if not (isinstance(v, int) and v <= 0):
                e.wait_ge(s, v)

        with nc.Block() as block:
            @block.sync
            def _(e):
                def keep(c):
                    e.wait_ge(lo_ready, 2 * (c + 1))
                    for w in range(2):
                        e.dma_start(kept[w, :, :, chunk(c)].rearrange("s p n -> p s n"),
                                    parts[:, c, w, :, :]).then_inc(parts_kept[c], 16)

                def load(b, u, half):
                    heads = slice(half * 8, half * 8 + 8)
                    for i in range(len(Q_PARTS)):
                        for w, part in ((0, Q_PARTS[i]), (1, K_PARTS[i])):
                            e.dma_start(slots[i * HD:(i + 1) * HD, u, w, heads, :],
                                        kept[w, part, :, bass.ds(b * T, T)].rearrange("(h d) t -> d h t", d=HD)[:, heads, :])\
                                .then_inc(slot_loaded[u][half], 16)

                def maxima(b, u):
                    wait(e, mparts_ready, b + 1)
                    for s in range(MAX_ROWS):
                        e.dma_start(slots[QK_ROWS + s:QK_ROWS + s + 1, u, 0, :, :],
                                    mparts[:, u, s, :]).then_inc(max_loaded[u], 16)

                keep(0)
                e.wait_ge(ones_set, 1)
                e.wait_ge(parts_kept[0], 32)
                load(0, 0, 0)
                keep(1)
                load(0, 0, 1)
                keep(2)
                load(1, 1, 0)
                keep(3)
                maxima(0, 0)
                load(1, 1, 1)
                for c in range(NC):
                    e.wait_ge(parts_kept[c], 32)

                def step(b, u):
                    ahead = not (isinstance(b, int) and b + 2 >= B)
                    if ahead:
                        e.wait_ge(s2_ready, b * G2 + G2 // 2)
                        load(b + 2, u, 0)
                    if not (isinstance(b, int) and b + 1 >= B):
                        maxima(b + 1, 1 - u)
                    if ahead:
                        e.wait_ge(s2_ready, (b + 1) * G2)
                        load(b + 2, u, 1)
                per_batch(e, step)

            @block.gpsimd
            def _(e):
                e.memset(slots[32:64, :, :, :, :], 1.0).then_inc(ones_set, 1)
                e.wait_ge(ones_set, 1)
                e.memset(V[:, :, :, :], 1.0).then_inc(ones_set, 1)
                for c in range(NC):
                    for w in range(2):
                        n = 2 * c + w
                        e.wait_ge(mid_ready, n + 1)
                        e.tensor_tensor(parts[:, c, w, 2, :], rest[:, n % 2, :], parts[:, c, w, 1, :],
                                        ALU.subtract).then_inc(lo_ready, 1)
                e.memset(Vh[:, :, :, :, :], 0.0).then_inc(vh_zero, 1)
                e.wait_ge(vh_zero, 1)
                e.wait_ge(v_ready, NC)

                def step(b, u):
                    wait(e, pv_group, (b - 1) * G2)
                    for j in range(2):
                        e.tensor_copy(Vh[:, u, j, :, :].rearrange("p g (h c) -> p (g h) c", c=HR + HC)[:, :, 0:HC],
                                      V[:, bass.ds(2 * b + j, 1), :, :].rearrange("p a h c -> p (a h) c"))\
                            .then_inc(vh_ready, 1)
                per_batch(e, step)

            @block.scalar
            def _(e):
                ln.act(e)

                def high(n):
                    c, w = n // 2, n % 2
                    src = q[:, c % 2, :] if w == 0 else k.zT[:, chunk(c)]
                    e.wait_ge(q_ready, c + 1)
                    e.activation(parts[:, c, w, 0, :], src, ACT.Copy).then_inc(hi_ready, 1)

                high(0)
                for c in range(NC):
                    for w in range(2):
                        n = 2 * c + w
                        if n + 1 < 2 * NC:
                            high(n + 1)
                        e.wait_ge(rest_ready, n + 1)
                        e.activation(parts[:, c, w, 1, :], rest[:, n % 2, :], ACT.Copy).then_inc(mid_ready, 1)
                    e.wait_ge(v_turned, c + 1)
                    e.wait_ge(ones_set, 2)
                    e.activation(V[:, 4 * c:4 * c + 4, :, 0:HD].rearrange("p t h d -> p (t h) d"),
                                 k.bank[4 + c % 2].rearrange("p (a d) -> p a d", d=HD), ACT.Copy).then_inc(v_ready, 1)

                def both_out(b):
                    e.wait_ge(pv_group, (b + 1) * G2)
                    wait(e, both_turned, b)
                    e.activation(both[:, :, :], k.bank[6][0:HR, :].rearrange("p (g t) -> p g t", g=2),
                                 ACT.Copy).then_inc(both_ready, 1)

                def step(b, u):
                    for g in range(G2):
                        if g == 1 and not (isinstance(b, int) and b == 0):
                            both_out(b - 1)
                        wait(e, s2_ready, b * G2 + g + 1)
                        wait(e, pv_group, b * G2 + g - 1)
                        e.activation(P[:, g % 2, :, :, :].rearrange("p a j t -> p (a j t)"),
                                     k.psum[:, 2 + 2 * (g % 2):4 + 2 * (g % 2), :].rearrange("p a n -> p (a n)"),
                                     ACT.Exp).then_inc(p_ready, 1)
                per_batch(e, step)
                both_out(B - 1)

            @block.tensor
            def _(e):
                ln.pe(e)
                for c in range(NC):
                    e.wait_ge(ln.z_ready, c + 1)
                    if c >= 2:
                        e.wait_ge(v_ready, c - 1)
                    for j in range(4):
                        mm = e.transpose(k.bank[4 + c % 2][:, j * 128:(j + 1) * 128],
                                         k.zT[:, (4 * c + j) * 128:(4 * c + j + 1) * 128], k.ident[:, :])
                    mm.then_inc(v_turned, 1)
                e.wait_ge(v_ready, NC)

                def scores_for_max(b, u, g):
                    if g % (G1 // 2) == 0:
                        e.wait_ge(slot_loaded[u][g // (G1 // 2)], 16 * LOADS * (b // 2 + 1) if isinstance(b, int) else
                                  8 * LOADS * (b - u) + 16 * LOADS)
                    wait(e, max_ready, b * G1 + g - 1)
                    tile = g % 2
                    for a in range(2):
                        h = 2 * (g // 2) + a
                        mm = e.matmul(k.bank[g % 2][:, a * T:(a + 1) * T],
                                      slots[0:QK_ROWS, u, 0, h, tile * 128:(tile + 1) * 128],
                                      slots[0:QK_ROWS, u, 1, h, :], start=True, stop=True)
                    mm.then_inc(s1_ready, 1)

                def turn_max(b):
                    wait(e, max_ready, (b + 1) * G1)
                    wait(e, x_done, b - 1)
                    for s in range(2):
                        mm = e.transpose(k.bank[7][0:HEADS, s * 128:(s + 1) * 128], m[:, s, :], k.ident[:, :])
                    mm.then_inc(mt_ready, 1)

                def scores(b, u, g):
                    if g == 0:
                        e.wait_ge(max_loaded[u], 16 * MAX_ROWS * (b // 2 + 1) if isinstance(b, int) else 8 * MAX_ROWS * (b - u) + 16 * MAX_ROWS)
                    wait(e, p_ready, b * G2 + g - 1)
                    for a in range(2):
                        h = 2 * g + a
                        for j in range(2):
                            mm = e.matmul(k.psum[:, 2 + 2 * (g % 2) + a, j * T:(j + 1) * T],
                                          slots[0:QK_ROWS + MAX_ROWS, u, 1, h, j * 128:(j + 1) * 128],
                                          slots[0:QK_ROWS + MAX_ROWS, u, 0, h, :], start=True, stop=True)
                    mm.then_inc(s2_ready, 1)

                def values(b, u, g):
                    wait(e, p_ready, b * G2 + g + 1)
                    if g == 0:
                        wait(e, both_ready, b)
                        wait(e, vh_ready, 2 * b + 2)
                    for a in range(2):
                        h = 2 * g + a
                        for j in range(2):
                            mm = e.matmul(k.bank[6][0:HR, (h // 8) * T:(h // 8 + 1) * T],
                                          Vh[:, u, j, h // 8, (h % 8) * HR:(h % 8 + 1) * HR],
                                          P[:, g % 2, a, j, :], start=(h % 8 == 0 and j == 0),
                                          stop=(h % 8 == 7 and j == 1))
                    mm.then_inc(pv_group, 1)

                def turn_both(b):
                    wait(e, both_ready, b + 1)
                    wait(e, mstep, (b + 1) * 5 + 1 if not (isinstance(b, int) and b + 1 >= B) else B * 5)
                    wait(e, x_done, b)
                    for i in range(2):
                        for g in range(2):
                            mm = e.transpose(k.bank[7][:, (2 * i + g) * HR:(2 * i + g + 1) * HR],
                                             both[:, g, i * 128:(i + 1) * 128], k.ident[0:HR, 0:HR])
                    mm.then_inc(both_turned, 1)

                def turn_out(b):
                    wait(e, o_ready, b + 1)
                    for i in range(2):
                        mm = e.transpose(k.bank[7][:, i * 128:(i + 1) * 128], o[:, i, :], k.ident[:, :])
                    mm.then_inc(o_turned, 1)

                for g in range(G1):
                    scores_for_max(0, 0, g)
                turn_max(0)

                def step(b, u):
                    ahead = not (isinstance(b, int) and b + 1 >= B)
                    for g in range(G2):
                        groups = range(sum(MAX_GROUPS[:g]), sum(MAX_GROUPS[:g + 1])) if ahead else ()
                        for n in groups[:1]:
                            scores_for_max(b + 1, 1 - u, n)
                        scores(b, u, g)
                        for n in groups[1:2]:
                            scores_for_max(b + 1, 1 - u, n)
                        if g:
                            values(b, u, g - 1)
                        for n in groups[2:]:
                            scores_for_max(b + 1, 1 - u, n)
                        if not (isinstance(b, int) and b == 0):
                            if g == 2:
                                turn_both(b - 1)
                            if g == 4:
                                turn_out(b - 1)
                        if g == 5 and ahead:
                            turn_max(b + 1)
                    values(b, u, G2 - 1)
                per_batch(e, step)
                turn_both(B - 1)
                turn_out(B - 1)

            @block.vector
            def _(e):
                ln.dve(e)

                def queries(c):
                    if c >= 2:
                        e.wait_ge(rest_ready, 2 * (c - 2) + 1)
                        e.wait_ge(hi_ready, 2 * (c - 2) + 1)
                    e.tensor_scalar(q[:, c % 2, :], k.zT[:, chunk(c)], k.qscale[:, 0:1], None, ALU.mult).then_inc(q_ready, 1)

                queries(0)
                for c in range(NC):
                    if c + 1 < NC:
                        queries(c + 1)
                    for w in range(2):
                        n = 2 * c + w
                        e.wait_ge(q_ready, c + 1)
                        e.wait_ge(hi_ready, n + 1)
                        if n >= 2:
                            e.wait_ge(lo_ready, n - 1)
                        src = q[:, c % 2, :] if w == 0 else k.zT[:, chunk(c)]
                        e.tensor_tensor(rest[:, n % 2, :], src, parts[:, c, w, 0, :], ALU.subtract).then_inc(rest_ready, 1)

                def maxima(b, u, between):
                    for g in range(G1):
                        e.wait_ge(s1_ready, b * G1 + g + 1)
                        if g == 0:
                            wait(e, mt_ready, b)
                        e.tensor_reduce(m[:, g % 2, 2 * (g // 2):2 * (g // 2) + 2],
                                        k.bank[g % 2].rearrange("p (a t) -> p a t", a=2), AX.X, ALU.max)\
                            .then_inc(max_ready, 1)
                        between(g)
                    e.wait_ge(mt_ready, b + 1)
                    i = 5 * b
                    e.tensor_scalar(negm[:, :], k.bank[7][0:HEADS, 0:T], -1.0, None, ALU.mult).then_inc(mstep, 1)
                    e.wait_ge(mstep, i + 1)
                    if not (isinstance(b, int) and b < 2):
                        n = (b - u) if not isinstance(b, int) else b - u
                        e.wait_ge(max_loaded[u], 8 * MAX_ROWS * n)
                    e.tensor_copy(mparts[:, u, 0, :], negm[:, :]).then_inc(mstep, 1)
                    e.wait_ge(mstep, i + 2)
                    e.tensor_tensor(nrest[:, :], negm[:, :], mparts[:, u, 0, :], ALU.subtract).then_inc(mstep, 1)
                    e.wait_ge(mstep, i + 3)
                    e.tensor_copy(mparts[:, u, 1, :], nrest[:, :]).then_inc(mstep, 1)
                    e.wait_ge(mstep, i + 4)
                    e.tensor_tensor(mparts[:, u, 2, :], nrest[:, :], mparts[:, u, 1, :], ALU.subtract).then_inc(mstep, 1)
                    e.wait_ge(mstep, i + 5)
                    e.sem_inc(mparts_ready, 1)

                def normalise(b):
                    e.wait_ge(both_turned, b + 1)
                    out = k.bank[7][:, 0:2 * HEADS * HC].rearrange("p (a d) -> p a d", d=HC)
                    e.reciprocal(recip[:, :], out[:, :, HD]).then_inc(recip_ready, 1)
                    e.wait_ge(recip_ready, b + 1)
                    wait(e, o_turned, b)
                    e.tensor_tensor(o[:, :, :].rearrange("p i (h d) -> p (i h) d", d=HD), out[:, :, 0:HD],
                                    along(recip[:, :], HD), ALU.mult).then_inc(o_ready, 1)

                def add(b):
                    e.wait_ge(o_turned, b + 1)
                    e.tensor_tensor(k.xT[:, bass.ds(b * T, T)], k.bank[7][:, 0:T], k.xT[:, bass.ds(b * T, T)],
                                    ALU.add).then_inc(x_done, 1)

                maxima(0, 0, lambda g: None)

                def step(b, u):
                    if isinstance(b, int) and b == 0:
                        maxima(1, 1, lambda g: None)
                    elif isinstance(b, int) and b == B - 1:
                        normalise(b - 1)
                        add(b - 1)
                    else:
                        maxima(b + 1, 1 - u, lambda g: normalise(b - 1) if g == 8 else add(b - 1) if g == 13 else None)
                per_batch(e, step)
                normalise(B - 1)
                add(B - 1)


def time_mix_attention(nc, k):
    ctx, sb, sem = phase(nc, k)
    with ctx:
        ln = Norm(k, sem, "a1")
        mixed, xm = sb("mixed", [128, 2, CW]), sb("xm", [128, 2, CW])
        w = sb("w", [128, 1])
        now = sb("now", [128, 1])
        keep = sb("keep", [128, CW])
        kc, gate_r = sb("kc", [128, 2, CW]), sb("gate_r", [128, 2, CW])
        ek, kv = sb("ek", [128, 2, CW]), sb("kv", [128, 2, CW])
        en, floor = sb("en", [128, 2, CW]), sb("floor", [128, 1])
        past_k, past_kv = sb("past_k", [128, 2, CW]), sb("past_kv", [128, 2, CW])
        num, den = sb("num", [128, 2, CW]), sb("den", [128, 2, CW])
        xm_ready, mix_ready, proj, kc_ready, ek_ready, gate_ready = sem("xm_ready"), sem("mix_ready"), sem("proj"), sem("kc_ready"), sem("ek_ready"), sem("gate_ready")
        w1_ready, w_ready, prep, step, kv_ready, y_ready, o_ready, x_done = sem("w1_ready"), sem("w_ready"), sem("prep"), sem("step"), sem("kv_ready"), sem("y_ready"), sem("o_ready"), sem("x_done")
        PROJ = 3
        DVE_STEPS = 5

        def batches(a):
            return a.rearrange("p (b t) -> p b t", t=T)

        gated, floor_set, mixed_ready, en_ready, den_ready = sem("gated"), sem("floor_set"), sem("mixed_ready"), sem("en_ready"), sem("den_ready")
        with nc.Block() as block:
            @block.gpsimd
            def _(e):
                e.memset(floor[:, :], 1e-16).then_inc(floor_set, 1)
                for c in range(NC):
                    u = c % 2
                    e.wait_ge(en_ready, c + 1)
                    e.wait_ge(step, c * DVE_STEPS + 1)
                    if c >= 2:
                        e.wait_ge(y_ready, c - 1)
                    a, p, o = batches(en[:, u, :]), batches(past_k[:, u, :]), batches(den[:, u, :])
                    e.tensor_tensor(o[:, :, 1:T], a[:, :, 1:T], p[:, :, 0:T - 1], ALU.add).then_inc(den_ready, 1)
                    e.tensor_copy(o[:, :, 0:1], a[:, :, 0:1]).then_inc(den_ready, 1)
                    e.wait_ge(gate_ready, c + 1)
                    e.wait_ge(step, c * DVE_STEPS + 4)
                    e.tensor_tensor(num[:, u, :], num[:, u, :], gate_r[:, u, :], ALU.mult).then_inc(gated, 1)

            @block.tensor
            def _(e):
                ln.pe(e)

                def out(c):
                    e.wait_ge(y_ready, c + 1)
                    if c >= 1:
                        e.wait_ge(x_done, c)
                    e.matmul(k.bank[7][:, :], k.w1T[:, 3, :], num[:, c % 2, :], start=True, stop=True).then_inc(o_ready, 1)

                for c in range(NC):
                    e.wait_ge(xm_ready, c + 1)
                    for j in range(PROJ):
                        if c >= 1:
                            e.wait_ge((kc_ready, kv_ready, gate_ready)[j], c)
                        e.matmul(k.bank[4 + j][:, :], k.w1T[:, j, :], xm[:, c % 2, :],
                                 start=True, stop=True).then_inc(proj, 1)
                    if c:
                        out(c - 1)
                out(NC - 1)

            @block.scalar
            def _(e):
                ln.act(e)
                e.activation(w[:, :], k.smallT[:, 3, 64:65], ACT.Exp).then_inc(w1_ready, 1)
                e.activation(now[:, :], k.smallT[:, 3, 32:33], ACT.Exp).then_inc(w1_ready, 1)
                e.wait_ge(w1_ready, 2)
                e.activation(w[:, :], w[:, :], ACT.Exp, scale=-1.0).then_inc(w_ready, 1)
                e.wait_ge(floor_set, 1)

                def mixed_in(c):
                    e.wait_ge(ln.z_ready, c + 1)
                    if c >= 2:
                        e.wait_ge(mix_ready, 2 * (c - 1))
                    e.activation(mixed[:, c % 2, :], k.zT[:, chunk(c)], ACT.Copy, scale=k.vec(V_MIX)).then_inc(mixed_ready, 1)

                def weights(c):
                    e.wait_ge(kc_ready, c + 1)
                    if c >= 2:
                        e.wait_ge(step, (c - 2) * DVE_STEPS + DVE_STEPS)
                        e.wait_ge(en_ready, c - 1)
                        e.wait_ge(den_ready, 2 * (c - 1))
                    e.activation(ek[:, c % 2, :], kc[:, c % 2, :], ACT.Exp).then_inc(ek_ready, 1)
                    e.wait_ge(ek_ready, c + 1)
                    e.activation(en[:, c % 2, :], ek[:, c % 2, :], ACT.Identity, scale=now[:, 0:1],
                                 bias=floor[:, 0:1]).then_inc(en_ready, 1)

                def gate(c):
                    e.wait_ge(proj, PROJ * c + 3)
                    if c >= 2:
                        e.wait_ge(gated, c - 1)
                    e.activation(gate_r[:, c % 2, :], k.bank[6][:, :], ACT.Sigmoid).then_inc(gate_ready, 1)

                mixed_in(0)
                mixed_in(1)
                for c in range(0, NC, 2):
                    weights(c)
                    gate(c)
                    if c + 2 < NC:
                        mixed_in(c + 2)
                    gate(c + 1)
                    weights(c + 1)
                    if c + 3 < NC:
                        mixed_in(c + 3)

            @block.vector
            def _(e):
                ln.dve(e)
                e.wait_ge(w_ready, 1)
                e.memset(keep[:, :], 1.0).then_inc(prep, 1)
                e.wait_ge(prep, 1)
                e.tensor_scalar(keep[:, :], keep[:, :], w[:, 0:1], None, ALU.mult).then_inc(prep, 1)
                e.wait_ge(prep, 2)
                for b in range(BPC):
                    e.memset(keep[:, b * T:b * T + 1], 0.0).then_inc(prep, 1)
                e.wait_ge(prep, 2 + BPC)

                def mix(c):
                    z, a, o = batches(k.zT[:, chunk(c)]), batches(mixed[:, c % 2, :]), batches(xm[:, c % 2, :])
                    if c >= 2:
                        e.wait_ge(proj, PROJ * (c - 1))
                    e.wait_ge(mixed_ready, c + 1)
                    e.tensor_copy(o[:, :, 0:1], a[:, :, 0:1]).then_inc(mix_ready, 1)
                    e.scalar_tensor_tensor(out=o[:, :, 1:T], in0=z[:, :, 0:T - 1], scalar=k.one_minus_mix[:, 0:1],
                                           in1=a[:, :, 1:T], op0=ALU.mult, op1=ALU.add).then_inc(mix_ready, 1)
                    e.wait_ge(mix_ready, 2 * c + 2)
                    e.sem_inc(xm_ready, 1)

                def add(c):
                    e.wait_ge(o_ready, c + 1)
                    e.tensor_tensor(k.xT[:, chunk(c)], k.bank[7][:, :], k.xT[:, chunk(c)], ALU.add).then_inc(x_done, 1)

                mix(0)
                for c in range(NC):
                    u, s = c % 2, c * DVE_STEPS
                    e.wait_ge(proj, PROJ * c + 1)
                    if c >= 2:
                        e.wait_ge(ek_ready, c - 1)
                    e.tensor_scalar(kc[:, u, :], k.bank[4][:, :], 60.0, None, ALU.min).then_inc(kc_ready, 1)
                    if c + 1 < NC:
                        mix(c + 1)
                    e.wait_ge(ek_ready, c + 1)
                    e.wait_ge(proj, PROJ * c + 2)
                    e.tensor_tensor(kv[:, u, :], k.bank[5][:, :], ek[:, u, :], ALU.mult).then_inc(kv_ready, 1)
                    e.tensor_tensor_scan(past_k[:, u, :], keep[:, :], ek[:, u, :], 0.0, ALU.mult, ALU.add).then_inc(step, 1)
                    if c:
                        add(c - 1)
                    e.wait_ge(kv_ready, c + 1)
                    e.tensor_tensor_scan(past_kv[:, u, :], keep[:, :], kv[:, u, :], 0.0, ALU.mult, ALU.add).then_inc(step, 1)
                    if c >= 2:
                        e.wait_ge(o_ready, c - 1)
                    e.wait_ge(step, s + 2)
                    a, p, o = batches(kv[:, u, :]), batches(past_kv[:, u, :]), batches(num[:, u, :])
                    e.tensor_scalar(o[:, :, 0:1], a[:, :, 0:1], now[:, 0:1], None, ALU.mult).then_inc(step, 1)
                    e.scalar_tensor_tensor(out=o[:, :, 1:T], in0=a[:, :, 1:T], scalar=now[:, 0:1],
                                           in1=p[:, :, 0:T - 1], op0=ALU.mult, op1=ALU.add).then_inc(step, 1)
                    e.wait_ge(den_ready, 2 * c + 2)
                    e.reciprocal(den[:, u, :], den[:, u, :]).then_inc(step, 1)
                    e.wait_ge(gated, c + 1)
                    e.wait_ge(step, s + 5)
                    e.tensor_tensor(num[:, u, :], num[:, u, :], den[:, u, :], ALU.mult).then_inc(y_ready, 1)
                add(NC - 1)


def state_space(nc, k):
    ctx, sb, sem = phase(nc, k)
    with ctx:
        ln = Norm(k, sem, "ss")
        one = sb("one", [128, 1])
        xdt = sb("xdt", [DTR, 2, CW])
        v, neg = sb("v", [128, 2, CW]), sb("neg", [128, 2, CW])
        dt, dtu = sb("dt", [128, N]), sb("dtu", [128, N])
        bc, bc_rest, bc_mid = sb("bc", [2 * NS, 2, CW]), sb("bc_rest", [2 * NS, 2, CW]), sb("bc_mid", [2 * NS, 2, CW], BF16)
        parts = sb("parts", [6 * NS, N], BF16)
        one_of = sb("one_of", [6 * NS, 2 * NS])
        pick = sb("pick", [6 * NS, 2 * NS, 128], BF16)
        Bs, Ab, Bu = sb("Bs", [128, NC, CW]), sb("Ab", [128, NC, CW]), sb("Bu", [128, NC, CW])
        h, hc, a_now = sb("h", [128, NC, CW]), sb("hc", [128, NC, CW]), sb("a_now", [128, 2])
        set_up, picked, A_step = sem("set_up"), sem("picked"), sem("A_step")
        xdt_mm, xdt_ready, dt_mm, bc_mm, v_ready, neg_ready = sem("xdt_mm"), sem("xdt_ready"), sem("dt_mm"), sem("bc_mm"), sem("v_ready"), sem("neg_ready")
        ex_ready, log_ready, dt_ready, dtu_ready = sem("ex_ready"), sem("log_ready"), sem("dt_ready"), sem("dtu_ready")
        bc_ready, hi_ready, rest_ready, mid_ready, parts_ready = sem("bc_ready"), sem("hi_ready"), sem("rest_ready"), sem("mid_ready"), sem("parts_ready")
        b_mm, c_mm, bs_ready, ab_ready, bu_ready = sem("b_mm"), sem("c_mm"), sem("bs_ready"), sem("ab_ready"), sem("bu_ready")
        h_ready, hc_ready, y_mm, zd_ready, x_done, a_now_ready = sem("h_ready"), sem("hc_ready"), sem("y_mm"), sem("zd_ready"), sem("x_done"), sem("a_now_ready")
        pick_ready, mid_moved = sem("pick_ready"), sem("mid_moved")

        def wait(e, s, v):
            if not (isinstance(v, int) and v <= 0):
                e.wait_ge(s, v)

        def every_state(e, step):
            step(0, 0)
            step(1, 1)
            with e.Fori(1, NS // 2 - 1) as i:
                step(2 * i, 0)
                step(2 * i + 1, 1)
            step(NS - 2, 0)
            step(NS - 1, 1)

        with nc.Block() as block:
            @block.gpsimd
            def _(e):
                e.memset(one[:, :], 1.0).then_inc(set_up, 1)
                e.wait_ge(set_up, 1)
                e.memset(one_of[:, :], 0.0).then_inc(picked, 1)
                for s in range(3):
                    e.wait_ge(picked, s + 1)
                    e.affine_select(out=one_of[:, :], in_=one_of[:, :], compare_op=ALU.not_equal, fill=1.0,
                                    base=-2 * NS * s, pattern=[[-1, 2 * NS]], channel_multiplier=1).then_inc(picked, 1)
                e.wait_ge(picked, 4)
                for c in range(NC):
                    u = c % 2
                    e.wait_ge(mid_ready, c + 1)
                    e.tensor_tensor(parts[4 * NS:6 * NS, chunk(c)], bc_rest[:, u, :], bc_mid[:, u, :], ALU.subtract).then_inc(parts_ready, 1)
                e.wait_ge(dtu_ready, NC)

                def state(n, s):
                    for c in range(NC):
                        g = n * NC + c
                        e.wait_ge(bs_ready, g + 1)
                        wait(e, h_ready, g - NC + 1)
                        e.tensor_tensor(Bu[:, c, :], Bs[:, c, :], dtu[:, chunk(c)], ALU.mult).then_inc(bu_ready, 1)
                every_state(e, state)

            @block.tensor
            def _(e):
                ln.pe(e)

                def project(c):
                    e.wait_ge(ln.z_ready, NC if c == 0 else c + 1)
                    if c >= 2:
                        e.wait_ge(xdt_ready, c - 1)
                        e.wait_ge(bc_ready, c - 1)
                    e.matmul(k.bank[c % 2][0:DTR, :], k.w_xdtT, k.zT[:, chunk(c)], start=True, stop=True).then_inc(xdt_mm, 1)
                    e.matmul(k.bank[4 + c % 2][0:2 * NS, :], k.w_bcT, k.zT[:, chunk(c)], start=True, stop=True).then_inc(bc_mm, 1)

                project(0)
                for c in range(NC):
                    if c + 1 < NC:
                        project(c + 1)
                    e.wait_ge(xdt_ready, c + 1)
                    if c >= 2:
                        e.wait_ge(v_ready, c - 1)
                    e.matmul(k.bank[2 + c % 2][:, :], k.w_dtT, xdt[:, c % 2, :], start=True, stop=True).then_inc(dt_mm, 1)
                e.wait_ge(parts_ready, NC)
                e.wait_ge(mid_moved, NC)
                e.wait_ge(v_ready, NC)
                e.wait_ge(pick_ready, 1)

                def row_of(n):
                    return pick[:, bass.ds(n, 1), :].rearrange("p a m -> p (a m)")

                def spread_b(n, c):
                    wait(e, bs_ready, n * NC + c - 1)
                    n, c = n + c // NC, c % NC
                    e.matmul(k.bank[c % 2][:, :], row_of(n), parts[:, chunk(c)], start=True, stop=True).then_inc(b_mm, 1)

                def spread_c(n, c):
                    wait(e, hc_ready, n * NC + c - 1)
                    n, c = n + c // NC, c % NC
                    e.matmul(k.bank[2 + c % 2][:, :], row_of(n + NS), parts[:, chunk(c)], start=True, stop=True).then_inc(c_mm, 1)

                def state(n, s):
                    end = isinstance(n, int) and n == NS - 1
                    for c in range(NC):
                        if not (end and c + 3 >= NC):
                            spread_b(n, c + 3)
                        if not (end and c + 2 >= NC):
                            spread_c(n, c + 2)
                        e.wait_ge(hc_ready, n * NC + c + 1)
                        e.matmul(k.bank[4 + c][:, :], k.ident[:, :], hc[:, c, :], start=isinstance(n, int) and n == 0,
                                 stop=end).then_inc(y_mm, 1)
                spread_b(0, 0)
                spread_c(0, 0)
                spread_b(0, 1)
                spread_c(0, 1)
                spread_b(0, 2)
                every_state(e, state)

            @block.scalar
            def _(e):
                ln.act(e)
                e.activation(k.A[:, :], k.A[:, :], ACT.Exp).then_inc(A_step, 1)
                e.wait_ge(set_up, 1)

                def rows_in(c):
                    u = c % 2
                    e.wait_ge(xdt_mm, c + 1)
                    if c >= 2:
                        e.wait_ge(dt_mm, c - 1)
                    e.activation(xdt[:, u, :], k.bank[u][0:DTR, :], ACT.Identity, bias=k.vec(V_BXDT)[0:DTR, :]).then_inc(xdt_ready, 1)
                    e.wait_ge(bc_mm, c + 1)
                    if c >= 2:
                        e.wait_ge(rest_ready, c - 1)
                    e.activation(bc[:, u, :], k.bank[4 + u][0:2 * NS, :], ACT.Identity, bias=k.vec(V_BBC)[0:2 * NS, :]).then_inc(bc_ready, 1)
                    e.wait_ge(bc_ready, c + 1)
                    e.activation(parts[0:2 * NS, chunk(c)], bc[:, u, :], ACT.Copy).then_inc(hi_ready, 1)

                def softplus(c):
                    u = c % 2
                    e.wait_ge(rest_ready, c + 1)
                    if c >= 2:
                        e.wait_ge(parts_ready, c - 1)
                        e.wait_ge(mid_moved, c - 1)
                    e.activation(bc_mid[:, u, :], bc_rest[:, u, :], ACT.Copy).then_inc(mid_ready, 1)
                    e.wait_ge(neg_ready, c + 1)
                    e.activation(neg[:, u, :], neg[:, u, :], ACT.Exp).then_inc(ex_ready, 1)
                    e.wait_ge(ex_ready, c + 1)
                    e.activation(neg[:, u, :], neg[:, u, :], ACT.Ln, bias=one[:, 0:1]).then_inc(log_ready, 1)

                rows_in(0)
                for c in range(NC):
                    if c + 1 < NC:
                        rows_in(c + 1)
                    softplus(c)
                e.wait_ge(A_step, 2)
                e.wait_ge(dtu_ready, NC)

                def state(n, s):
                    wait(e, a_now_ready, n + 1)
                    for c in range(NC):
                        g = n * NC + c
                        e.wait_ge(b_mm, g + 1)
                        wait(e, bu_ready, g - NC + 1)
                        e.activation(Bs[:, c, :], k.bank[c % 2][:, :], ACT.Copy).then_inc(bs_ready, 1)
                        wait(e, h_ready, g - NC + 1)
                        e.activation(Ab[:, c, :], dt[:, chunk(c)], ACT.Exp, scale=a_now[:, s:s + 1]).then_inc(ab_ready, 1)
                every_state(e, state)

            @block.vector
            def _(e):
                e.wait_ge(picked, 4)
                e.tensor_copy(pick[:, :, :], along(one_of[:, :], 128)).then_inc(pick_ready, 1)
                ln.dve(e)
                e.wait_ge(A_step, 1)
                e.tensor_scalar(k.A[:, :], k.A[:, :], -1.0, None, ALU.mult).then_inc(A_step, 1)

                def steps_in(c):
                    u = c % 2
                    e.wait_ge(hi_ready, c + 1)
                    if c >= 2:
                        e.wait_ge(parts_ready, c - 1)
                    e.tensor_tensor(bc_rest[:, u, :], bc[:, u, :], parts[0:2 * NS, chunk(c)], ALU.subtract).then_inc(rest_ready, 1)
                    e.wait_ge(dt_mm, c + 1)
                    e.tensor_scalar(v[:, u, :], k.bank[2 + u][:, :], k.vec(V_BDT), None, ALU.add).then_inc(v_ready, 1)
                    e.wait_ge(v_ready, c + 1)
                    e.scalar_tensor_tensor(out=neg[:, u, :], in0=v[:, u, :], scalar=-1.0, in1=v[:, u, :],
                                           op0=ALU.mult, op1=ALU.min).then_inc(neg_ready, 1)

                def steps_out(c):
                    u = c % 2
                    e.wait_ge(mid_ready, c + 1)
                    e.tensor_copy(parts[2 * NS:4 * NS, chunk(c)], bc_mid[:, u, :]).then_inc(mid_moved, 1)
                    e.wait_ge(log_ready, c + 1)
                    e.scalar_tensor_tensor(out=dt[:, chunk(c)], in0=v[:, u, :], scalar=0.0, in1=neg[:, u, :],
                                           op0=ALU.max, op1=ALU.add).then_inc(dt_ready, 1)
                    e.wait_ge(dt_ready, c + 1)
                    e.tensor_tensor(dtu[:, chunk(c)], dt[:, chunk(c)], k.zT[:, chunk(c)], ALU.mult).then_inc(dtu_ready, 1)

                steps_in(0)
                for c in range(NC):
                    if c + 1 < NC:
                        steps_in(c + 1)
                    steps_out(c)

                def column(n, s):
                    wait(e, ab_ready, (n - 1) * NC)
                    e.tensor_copy(a_now[:, s:s + 1], k.A[:, bass.ds(n, 1)]).then_inc(a_now_ready, 1)

                def state(n, s):
                    if not (isinstance(n, int) and n == NS - 1):
                        column(n + 1, 1 - s)
                    for c in range(NC):
                        g, u = n * NC + c, c % 2
                        e.wait_ge(ab_ready, g + 1)
                        e.wait_ge(bu_ready, g + 1)
                        wait(e, hc_ready, g - NC + 1)
                        for b in range(BPC):
                            r = slice(b * T, (b + 1) * T)
                            i = e.tensor_tensor_scan(h[:, c, r], Ab[:, c, r], Bu[:, c, r], 0.0, ALU.mult, ALU.add)
                        i.then_inc(h_ready, 1)
                        e.wait_ge(h_ready, g + 1)
                        e.wait_ge(c_mm, g + 1)
                        wait(e, y_mm, g - NC + 1)
                        e.tensor_tensor(hc[:, c, :], k.bank[2 + u][:, :], h[:, c, :], ALU.mult).then_inc(hc_ready, 1)
                column(0, 0)
                every_state(e, state)
                for c in range(NC):
                    e.scalar_tensor_tensor(out=k.zT[:, chunk(c)], in0=k.zT[:, chunk(c)], scalar=k.vec(V_D),
                                           in1=k.xT[:, chunk(c)], op0=ALU.mult, op1=ALU.add).then_inc(zd_ready, 1)
                for c in range(NC):
                    e.wait_ge(zd_ready, c + 1)
                    e.wait_ge(y_mm, (NS - 1) * NC + c + 1)
                    e.tensor_tensor(k.xT[:, chunk(c)], k.bank[4 + c][:, :], k.zT[:, chunk(c)], ALU.add).then_inc(x_done, 1)


PAIRS = NT // 2
PW = 256
PK = PH * TOPK
FOLDS = 4
OW = 64
RUNS = (((0, 1), (0, 8)), ((1, 2), (0, 4)), ((2, 4), (0, 2)), ((4, 8), (0, 1)))
CAND = sum((x1 - x0) * (y1 - y0) for (x0, x1), (y0, y1) in RUNS)
HI = NE // 128


def product_keys(nc, k):
    ctx, sb, sem = phase(nc, k)
    with ctx:
        ln = Norm(k, sem, "pk")
        stats, mv = sb("stats", [128, NC, 6]), sb("mv", [128, 2])
        bn_scale, bn_bias, bn_log, bn_eps = sb("bn_scale", [128, 1]), sb("bn_bias", [128, 1]), sb("bn_log", [128, 1]), sb("bn_eps", [128, 1])
        low_no, number = sb("low_no", [128, 128, OW], F16), sb("number", [128, CAND, 128], F16)
        xn = sb("xn", [128, PW])
        sims = sb("sims", [128, 2, 2 * PH * NK])
        tops, topi, topf = sb("tops", [128, 2, 2 * PH, 8]), sb("topi", [128, 2, 2 * PH, 8], U32), sb("topf", [128, 2, 2 * PH, 8], F16)
        cand, cand_key = sb("cand", [128, 2 * PH, CAND]), sb("cand_key", [128, CAND, 2 * PH], F16)
        best, pos, posf = sb("best", [128, 2 * PH, 8]), sb("pos", [128, 2 * PH, 8], U32), sb("posf", [128, 2 * PK], F16)
        hit = sb("hit", [128, CAND, 2 * PK], F16)
        expert_i = sb("expert_i", [128, 2 * PK], U32)
        split_i, split = sb("split_i", [128, 2, 2 * PK], U32), sb("split", [128, 2, 2 * PK])
        shifted, ex = sb("shifted", [128, 2 * PH, 8]), sb("ex", [128, 2 * PH, 8])
        total, share = sb("total", [128, 2 * PH]), sb("share", [128, 2 * PH, 8])
        lowT, highT = sb("lowT", [128, 128], F16), sb("highT", [128, 128], F16)
        shareT = sb("shareT", [128, 2, 128], F16)
        at_high = sb("at_high", [128, HI, 128], F16)
        rows = sb("rows", [128, 2, 2, HI, 128], F16)
        onehot = sb("onehot", [128, 2, 128, OW], F16)
        G, WG = sb("G", [128, ET, PW]), sb("WG", [128, ET, PW])
        A0, TB, O0, XB = 0, 2, 3, 7
        bn, bn_rstd, low_made, numbers_made, rows_zero = sem("bn"), sem("bn_rstd"), sem("low_made"), sem("numbers_made"), sem("rows_zero")
        xn_ready, a_mm, a_used, tops_ready, topi_ready = sem("xn_ready"), sem("a_mm"), sem("a_used"), sem("tops_ready"), sem("topi_ready")
        cand_ready, cand_key_ready, topf_ready, best_ready, pos_ready = sem("cand_ready"), sem("cand_key_ready"), sem("topf_ready"), sem("best_ready"), sem("pos_ready")
        posf_ready, hit_ready, picked = sem("posf_ready"), sem("hit_ready"), sem("picked")
        expert_i_ready, split_i_ready, split_ready = sem("expert_i_ready"), sem("split_i_ready"), sem("split_ready")
        shifted_ready, ex_ready, total_ready, share_ready = sem("shifted_ready"), sem("ex_ready"), sem("total_ready"), sem("share_ready")
        turned, turned_out, turned_out_part, low_share, at_ready = sem("turned"), sem("turned_out"), sem("turned_out_part"), sem("low_share"), sem("at_ready")
        rows_ready, rows_dve, oh_ready, outer_mm, wg_ready, out_mm, x_done, settled, folded = sem("rows_ready"), sem("rows_dve"), sem("oh_ready"), sem("outer_mm"), sem("wg_ready"), sem("out_mm"), sem("x_done"), sem("settled"), sem("folded")

        def wait(e, s, v):
            if not (isinstance(v, int) and v <= 0):
                e.wait_ge(s, v)

        def last(p, n=1):
            return isinstance(p, int) and p + n >= PAIRS

        def rows_of(e, s, t):
            half = slice(64 * t, 64 * t + 64)
            return e.tensor_tensor(rows[half, s, t, :, :], at_high[half, :, :], across(shareT[half, s, :], HI), ALU.mult)

        def sim_use(p):
            return 2 * p if isinstance(p, int) and p < 2 else 6 * p - 8

        def gelu_use(p):
            return 6 * p + 6 - (4 if last(p) else 2 if last(p, 2) else 0)

        def loop(e, body):
            body(0)
            with e.Fori(1, PAIRS - 2) as p:
                body(p)
            body(PAIRS - 2)
            body(PAIRS - 1)

        with nc.Block() as block:
            @block.tensor
            def _(e):
                ln.pe(e)

                def sim(p):
                    wait(e, xn_ready, p + 1)
                    for t in range(2):
                        n = sim_use(p) + t
                        wait(e, a_used, n - 1)
                        e.matmul(k.bank[A0 + t][:, :], xn[:, t * 128:(t + 1) * 128], k.M[:, :],
                                 start=True, stop=True).then_inc(a_mm, 1)

                def activations(p):
                    for t in range(4):
                        wait(e, a_used, gelu_use(p) + t - 1)
                        for j in range(2):
                            mm = e.matmul(k.bank[A0 + t % 2][:, j * PW:(j + 1) * PW],
                                          k.key_inT[:, (2 * t + j) * 128:(2 * t + j + 1) * 128],
                                          k.zT[:, bass.ds(p * PW, PW)], start=True, stop=True)
                        mm.then_inc(a_mm, 1)

                def turn(p):
                    wait(e, split_ready, p + 1)
                    wait(e, share_ready, p + 1)
                    wait(e, turned_out, p)
                    wait(e, low_share, p)
                    for i, src in enumerate((split[:, 0, :], split[:, 1, :], share[:, :, :].rearrange("p a b -> p (a b)"))):
                        mm = e.transpose(k.bank[TB][:, i * 128:(i + 1) * 128], src, k.ident[:, :])
                    mm.then_inc(turned, 1)

                def outer(p, a):
                    wait(e, oh_ready, 2 * p + a + 1)
                    wait(e, rows_ready, p + 1)
                    wait(e, rows_dve, p + 1)
                    for q in range(2):
                        bank = 2 * a + q
                        wait(e, wg_ready, 4 * (p - 1) + bank + 1)
                        for i in range(32):
                            n = q * 32 + i
                            for s in range(2):
                                mm = e.matmul(k.bank[O0 + bank][:, i * 2 * HI:(i + 1) * 2 * HI], onehot[:, a, :, n],
                                              rows[:, s, :, :, a * OW + n], start=(s == 0), stop=(s == 1))
                        mm.then_inc(outer_mm, 1)

                def out(p):
                    wait(e, wg_ready, 4 * p + 4)
                    wait(e, x_done, p)
                    for j in range(ET):
                        mm = e.matmul(k.bank[XB][:, 0:PW], k.key_out[:, j, :], WG[:, j, :], start=(j == 0), stop=(j == ET - 1))
                    mm.then_inc(out_mm, 1)

                e.wait_ge(ln.z_ready, NC)
                sim(0)
                sim(1)
                turn(0)

                def body(p):
                    if not last(p, 2):
                        sim(p + 2)
                    activations(p)
                    outer(p, 0)
                    outer(p, 1)
                    if not last(p):
                        turn(p + 1)
                    out(p)
                loop(e, body)

            @block.scalar
            def _(e):
                ln.act(e)
                e.wait_ge(rows_zero, 1)
                e.wait_ge(bn, 2)
                e.activation(bn_log[:, :], mv[:, 1:2], ACT.Ln, bias=bn_eps[:, 0:1]).then_inc(bn_rstd, 1)
                e.wait_ge(bn_rstd, 1)
                e.activation(bn_scale[:, :], bn_log[:, :], ACT.Exp, scale=-0.5).then_inc(bn_rstd, 1)

                def sims_out(p):
                    wait(e, topi_ready, p)
                    for t in range(2):
                        wait(e, a_mm, sim_use(p) + t + 1)
                        e.activation(sims[:, t, :], k.bank[A0 + t][:, :], ACT.Copy).then_inc(a_used, 1)

                def gelus(p):
                    wait(e, wg_ready, 4 * p)
                    for t in range(4):
                        wait(e, a_mm, gelu_use(p) + t + 1)
                        e.activation(G[:, 2 * t:2 * t + 2, :], k.bank[A0 + t % 2].rearrange("p (a n) -> p a n", a=2),
                                     ACT.Gelu).then_inc(a_used, 1)

                def numbers(p):
                    wait(e, topi_ready, p + 1)
                    wait(e, cand_key_ready, p)
                    e.activation(topf[:, 0, :, :], topi[:, 0, :, :], ACT.Copy, scale=float(NK)).then_inc(topf_ready, 1)
                    e.activation(topf[:, 1, :, :], topi[:, 1, :, :], ACT.Copy).then_inc(topf_ready, 1)

                def positions(p):
                    wait(e, pos_ready, p + 1)
                    wait(e, hit_ready, p)
                    e.activation(posf[:, :], pos[:, :, :].rearrange("p a b -> p (a b)"), ACT.Copy).then_inc(posf_ready, 1)

                def exponentials(p):
                    wait(e, shifted_ready, p + 1)
                    wait(e, share_ready, p)
                    e.activation(ex[:, :, :], shifted[:, :, :], ACT.Exp).then_inc(ex_ready, 1)

                def parts_out(p):
                    wait(e, split_i_ready, p + 1)
                    wait(e, turned, p)
                    e.activation(split[:, :, :], split_i[:, :, :], ACT.Copy).then_inc(split_ready, 1)
                    wait(e, turned, p + 1)
                    wait(e, oh_ready, 2 * p)
                    wait(e, rows_ready, p)
                    wait(e, rows_dve, p)
                    e.activation(shareT[:, 0, :], k.bank[TB][:, 256:384], ACT.Copy).then_inc(turned_out_part, 1)
                    e.activation(highT[:, :], k.bank[TB][:, 128:256], ACT.Copy).then_inc(turned_out_part, 1)
                    e.activation(lowT[:, :], k.bank[TB][:, 0:128], ACT.Copy).then_inc(turned_out, 1)

                sims_out(0)
                e.activation(low_no[:, :, :], along(k.iota_f[:, :], OW), ACT.Copy).then_inc(low_made, 1)
                numbers(0)
                sims_out(1)
                positions(0)
                exponentials(0)
                parts_out(0)
                numbers(1)

                def body(p):
                    if not last(p):
                        positions(p + 1)
                    if not last(p, 2):
                        sims_out(p + 2)
                    gelus(p)
                    if not last(p):
                        exponentials(p + 1)
                        parts_out(p + 1)
                        if not last(p, 2):
                            numbers(p + 2)
                loop(e, body)

            @block.gpsimd
            def _(e):
                e.memset(bn_eps[:, :], BN_EPS).then_inc(rows_zero, 1)
                e.wait_ge(rows_zero, 1)
                e.memset(rows[:, :, :, :, :], 0.0).then_inc(rows_zero, 1)
                e.wait_ge(rows_zero, 2)
                e.tensor_copy(number[:, :, :], along(k.iota_f[:, 0:CAND], 128)).then_inc(numbers_made, 1)
                e.wait_ge(numbers_made, 1)

                def runs(x, y, out):
                    at = 0
                    for (x0, x1), (y0, y1) in RUNS:
                        nx, ny = x1 - x0, y1 - y0
                        i = e.tensor_tensor(out(at, nx, ny), x[:, :, x0:x1].unsqueeze(3).broadcast_to([128, 2 * PH, nx, ny]),
                                            y[:, :, y0:y1].unsqueeze(2).broadcast_to([128, 2 * PH, nx, ny]), ALU.add)
                        at += nx * ny
                    return i

                def sums(p):
                    wait(e, tops_ready, p + 1)
                    wait(e, pos_ready, p)
                    runs(tops[:, 0, :, :], tops[:, 1, :, :],
                         lambda at, nx, ny: cand[:, :, at:at + nx * ny].rearrange("p h (a b) -> p h a b", a=nx)).then_inc(cand_ready, 1)

                def keys(p):
                    wait(e, topf_ready, 2 * p + 2)
                    wait(e, picked, p)
                    runs(topf[:, 0, :, :], topf[:, 1, :, :],
                         lambda at, nx, ny: cand_key[:, at:at + nx * ny, :].rearrange("p (a b) h -> p h a b", a=nx)).then_inc(cand_key_ready, 1)

                def pick(p):
                    wait(e, hit_ready, p + 1)
                    wait(e, cand_key_ready, p + 1)
                    e.tensor_tensor(hit[:, :, :].rearrange("p c (h k) -> p (c h) k", k=TOPK), hit[:, :, :].rearrange("p c (h k) -> p (c h) k", k=TOPK),
                                    along(cand_key[:, :, :].rearrange("p c h -> p (c h)"), TOPK), ALU.mult).then_inc(picked, 1)
                    wait(e, picked, p + 1)
                    n, left = 0, CAND
                    while left > 2:
                        half = left // 2
                        e.tensor_tensor(hit[:, 0:half, :], hit[:, 0:half, :], hit[:, left - half:left, :], ALU.add).then_inc(folded, 1)
                        left -= half
                        n += 1
                        wait(e, folded, FOLDS * p + n)

                def share_rows(p):
                    wait(e, cand_key_ready, p + 1 if last(p) else p + 2)
                    wait(e, folded, FOLDS * (p + 1))
                    wait(e, at_ready, p + 1)
                    wait(e, low_share, p + 1)
                    wait(e, outer_mm, 4 * p)
                    for s, t in ((1, 0), (1, 1), (0, 1)):
                        i = rows_of(e, s, t)
                    i.then_inc(rows_ready, 1)

                sums(0)
                keys(0)
                pick(0)
                sums(1)
                keys(1)

                def body(p):
                    share_rows(p)
                    if not last(p):
                        wait(e, rows_ready, p + 1)
                        pick(p + 1)
                    if not last(p, 2):
                        sums(p + 2)
                        keys(p + 2)
                loop(e, body)

            @block.vector
            def _(e):
                for c in range(NC):
                    ln.dve_chunk(e, c)
                    e.wait_ge(ln.z_ready, c + 1)
                    i = e.bn_stats(stats[:, c, :], k.zT[:, chunk(c)])
                i.then_inc(bn, 1)
                e.wait_ge(bn, 1)
                e.bn_aggr(mv[:, :], stats[:, :, :]).then_inc(bn, 1)
                e.wait_ge(bn_rstd, 2)
                e.tensor_scalar(bn_scale[:, :], bn_scale[:, :], k.vec(V_GAMMA), None, ALU.mult).then_inc(bn, 1)
                e.wait_ge(bn, 3)
                e.tensor_scalar(bn_bias[:, :], mv[:, 0:1], bn_scale[:, 0:1], -1.0, ALU.mult, ALU.mult).then_inc(bn, 1)
                e.wait_ge(bn, 4)
                e.tensor_scalar(bn_bias[:, :], bn_bias[:, :], k.vec(V_BETA), None, ALU.add).then_inc(bn, 1)
                e.wait_ge(bn, 5)

                def normalise(p):
                    wait(e, a_mm, sim_use(p - 1) + 2 if not (isinstance(p, int) and p == 0) else 0)
                    e.tensor_scalar(xn[:, :], k.zT[:, bass.ds(p * PW, PW)], bn_scale[:, 0:1], bn_bias[:, 0:1],
                                    ALU.mult, ALU.add).then_inc(xn_ready, 1)

                def top_keys(p):
                    wait(e, a_used, sim_use(p) + 2)
                    wait(e, cand_ready, p)
                    e.sem_inc(settled, 1)
                    for t in range(2):
                        for w in range(2):
                            for h in range(PH):
                                g = (w * PH + h) * NK
                                i = e.max(tops[:, w, t * PH + h, :], sims[:, t, g:g + NK])
                    i.then_inc(tops_ready, 1)

                def top_numbers(p):
                    wait(e, tops_ready, p + 1)
                    wait(e, topf_ready, 2 * p)
                    e.sem_inc(settled, 1)
                    for t in range(2):
                        for w in range(2):
                            for h in range(PH):
                                g = (w * PH + h) * NK
                                i = e.max_index(topi[:, w, t * PH + h, :], tops[:, w, t * PH + h, :], sims[:, t, g:g + NK])
                    i.then_inc(topi_ready, 1)

                def top_sums(p):
                    wait(e, cand_ready, p + 1)
                    e.sem_inc(settled, 1)
                    for g in range(2 * PH):
                        i = e.max(best[:, g, :], cand[:, g, :])
                    i.then_inc(best_ready, 1)
                    wait(e, best_ready, p + 1)
                    wait(e, posf_ready, p)
                    e.sem_inc(settled, 1)
                    for g in range(2 * PH):
                        i = e.max_index(pos[:, g, :], best[:, g, :], cand[:, g, :])
                    i.then_inc(pos_ready, 1)
                    wait(e, ex_ready, p)
                    e.tensor_tensor(shifted[:, :, :], best[:, :, :], best[:, :, 0:1].broadcast_to([128, 2 * PH, 8]),
                                    ALU.subtract).then_inc(shifted_ready, 1)

                def hits(p):
                    wait(e, posf_ready, p + 1)
                    e.tensor_tensor(hit[:, :, :], number[:, :, :], across(posf[:, :], CAND), ALU.is_equal).then_inc(hit_ready, 1)

                def experts(p):
                    wait(e, folded, FOLDS * (p + 1))
                    e.tensor_tensor(expert_i[:, :], hit[:, 0, :], hit[:, 1, :], ALU.add).then_inc(expert_i_ready, 1)
                    wait(e, expert_i_ready, p + 1)
                    wait(e, split_ready, p)
                    e.tensor_scalar(split_i[:, 0, :], expert_i[:, :], 127, None, ALU.bitwise_and)
                    e.tensor_scalar(split_i[:, 1, :], expert_i[:, :], 7, None, ALU.logical_shift_right).then_inc(split_i_ready, 1)
                    wait(e, ex_ready, p + 1)
                    e.tensor_reduce(total[:, :], ex[:, :, :], AX.X, ALU.add).then_inc(total_ready, 1)
                    wait(e, total_ready, 2 * p + 1)
                    e.reciprocal(total[:, :], total[:, :]).then_inc(total_ready, 1)
                    wait(e, total_ready, 2 * p + 2)
                    wait(e, turned, p)
                    e.tensor_tensor(share[:, :, :], ex[:, :, :], along(total[:, :], 8), ALU.mult).then_inc(share_ready, 1)

                def low_part(p):
                    wait(e, turned_out, p + 1)
                    wait(e, rows_ready, p)
                    e.tensor_tensor(shareT[:, 1, :], k.bank[TB][:, 256:384], shareT[:, 0, :], ALU.subtract).then_inc(low_share, 1)

                def at_highs(p):
                    wait(e, turned_out, p + 1)
                    wait(e, rows_ready, p)
                    e.tensor_tensor(at_high[:, :, :], number[:, 0:HI, :], across(highT[:, :], HI), ALU.is_equal).then_inc(at_ready, 1)
                    wait(e, at_ready, p + 1)
                    wait(e, outer_mm, 4 * p)
                    rows_of(e, 0, 0).then_inc(rows_dve, 1)

                def one_hot(p, a):
                    wait(e, outer_mm, 4 * (p - 1) + 2 * a + 2)
                    e.tensor_tensor(onehot[:, a, :, :], low_no[:, :, :], across(lowT[:, a * OW:(a + 1) * OW], 128),
                                    ALU.is_equal).then_inc(oh_ready, 1)

                def weigh(p, a):
                    if a == 0:
                        wait(e, a_used, gelu_use(p) + 4)
                        wait(e, out_mm, p)
                    wait(e, outer_mm, 4 * p + 2 * a + 2)
                    out, g = (x[:, :, :].rearrange("p j (t n) -> p t j n", t=2)[:, :, :, a * OW:(a + 1) * OW] for x in (WG, G))
                    e.tensor_tensor(out, k.psum[:, O0 + 2 * a:O0 + 2 * a + 2, :].rearrange("p b (n t j) -> p t j (b n)", t=2, j=HI),
                                    g, ALU.mult).then_inc(wg_ready, 2)

                def add(p):
                    wait(e, out_mm, p + 1)
                    e.tensor_tensor(k.xT[:, bass.ds(p * PW, PW)], k.bank[XB][:, 0:PW], k.xT[:, bass.ds(p * PW, PW)],
                                    ALU.add).then_inc(x_done, 1)

                normalise(0)
                top_keys(0)
                top_numbers(0)
                normalise(1)
                top_sums(0)
                e.wait_ge(low_made, 1)
                e.wait_ge(numbers_made, 1)
                e.wait_ge(rows_zero, 2)
                hits(0)
                top_keys(1)
                top_numbers(1)
                experts(0)

                def body(p):
                    if not last(p, 2):
                        normalise(p + 2)
                    low_part(p)
                    at_highs(p)
                    if not last(p):
                        top_sums(p + 1)
                    if not (isinstance(p, int) and p == 0):
                        add(p - 1)
                    if not last(p):
                        hits(p + 1)
                    one_hot(p, 0)
                    one_hot(p, 1)
                    weigh(p, 0)
                    if not last(p, 2):
                        top_keys(p + 2)
                    if not last(p):
                        experts(p + 1)
                    weigh(p, 1)
                    if not last(p, 2):
                        top_numbers(p + 2)
                loop(e, body)
                add(PAIRS - 1)


def build(nc, t, out, stages):
    ctx = ExitStack()
    with ctx:
        def sb(name, shape, dt=F32):
            return ctx.enter_context(nc.sbuf_tensor(name, shape, dt))

        k = Kit()
        k.psum = ctx.enter_context(nc.psum_tensor("psum", [128, 8, CW], F32))
        k.bank = [k.psum[:, i, :] for i in range(8)]
        k.xT, k.zT = sb("xT", [128, N]), sb("zT", [128, N])
        k.ident, k.mean, k.centre = sb("ident", [128, 128]), sb("mean", [128, 128]), sb("centre", [128, 128])
        k.iota_i, k.iota_f = sb("iota_i", [128, 128], mybir.dt.int32), sb("iota_f", [128, 128])
        k.eps_ln, k.eps_rms = sb("eps_ln", [128, 1]), sb("eps_rms", [128, 1])
        k.w0T, k.w1T = sb("w0T", [128, 4, 128]), sb("w1T", [128, 4, 128])
        k.vec0 = sb("vec0", [128, 2])
        k.smallT = sb("smallT", [128, 4, 128])
        k.key_inT, k.key_out, k.M = sb("key_inT", [128, NE]), sb("key_out", [128, ET, D]), sb("M", [128, 2 * PH * NK])
        k.w1h, k.w1l = sb("w1h", [128, E, HID], F32R), sb("w1l", [128, E, HID], F32R)
        k.w2h, k.w2l = sb("w2h", [128, E, HT, D], F32R), sb("w2l", [128, E, HT, D], F32R)
        k.gate_w, k.gate_b, k.b2 = sb("gate_w", [128, E]), sb("gate_b", [E, 1]), sb("b2", [W_ROWS, D])
        k.A, k.qscale, k.one_minus_mix = sb("A", [128, NS]), sb("qscale", [128, 1]), sb("one_minus_mix", [128, 1])
        k.sq, k.logv, k.rstd = sb("sq", [128, 2, CW]), sb("logv", [128, 2, CW]), sb("rstd", [128, 2, CW])
        k.vec = lambda v: k.smallT[:, 0, v:v + 1]
        k.b1 = k.smallT[:, 0, 32:32 + E * HT]
        k.w_xdtT, k.w_dtT, k.w_bcT = k.smallT[:, 1, 0:DTR], k.smallT[0:DTR, 2, :], k.smallT[:, 3, 0:2 * NS]
        k.stage = 0
        raw_ctx, raw_sb, raw_sem = phase(nc, k)
        with raw_ctx:
            raw = Raw(raw_sb, raw_sem)
            setup(nc, k, t, raw)
            k.stage = 1
            decay_attention(nc, k, t, raw)
            k.stage = 2
            prepare(nc, k, raw)
        for s in stages:
            k.stage += 1
            s(nc, k)
        k.stage += 1
        store(nc, k, out)


STAGES = [mixture, head_attention, mixture, time_mix_attention, product_keys, state_space, product_keys]


_INS = ['L0_attn_a_x', 'L0_attn_a_Wr', 'L0_attn_a_Wk', 'L0_attn_a_Wv', 'L0_attn_a_Wo', 'L0_attn_a_decay',
        'L0_attn_a_ln_w', 'L0_attn_b_rotation_params', 'L0_attn_b_entangle_params', 'L0_ffn_gate_w',
        'L0_ffn_gate_b', 'L0_ffn_w1', 'L0_ffn_b1', 'L0_ffn_w2', 'L0_ffn_b2', 'L1_attn_a_time_decay',
        'L1_attn_a_time_first', 'L1_attn_a_time_mix', 'L1_attn_a_Wk', 'L1_attn_a_Wv', 'L1_attn_a_Wr',
        'L1_attn_a_Wo', 'L1_attn_b_A_log', 'L1_attn_b_W_xdt', 'L1_attn_b_b_xdt', 'L1_attn_b_W_dt',
        'L1_attn_b_b_dt', 'L1_attn_b_W_B', 'L1_attn_b_b_B', 'L1_attn_b_W_C', 'L1_attn_b_b_C', 'L1_attn_b_D',
        'L1_ffn_gamma', 'L1_ffn_beta', 'L1_ffn_w_q', 'L1_ffn_keys', 'L1_ffn_key_in', 'L1_ffn_key_out']


def kernel(**inputs):
    import numpy as _np
    import concourse.bacc as _bacc
    from concourse import mybir as _mybir
    from concourse.bass_utils import run_bass_kernel_spmd as _run

    nc = _bacc.Bacc("TRN2", target_bir_lowering=False, num_devices=1)
    arrays, args = {}, {}
    for name in _INS:
        a = _np.ascontiguousarray(inputs[name])
        arrays[f"in_{name}_dram"] = a
        args[name] = nc.dram_tensor(f"in_{name}_dram", a.shape, _mybir.dt.from_np(a.dtype), kind="ExternalInput").ap()
    out = nc.dram_tensor("out_0_dram", (B, T, D), _mybir.dt.float32, kind="ExternalOutput").ap()
    build(nc, args, out, STAGES)
    r = _run(nc, [arrays], core_ids=[0])
    return r.results[0]["out_0_dram"]
```
